# Optimizing a Trainium2 kernel written in Bass

```python
import numpy as np
import jax
import jax.numpy as jnp

def _softmax(x, axis=-1):
    return jax.nn.softmax(x, axis=axis)

def _gelu(x):
    return jax.nn.gelu(x, approximate=True)

def _silu(x):
    return jax.nn.silu(x)

def _sigmoid(x):
    return jax.nn.sigmoid(x)

def _layernorm(x, axis=-1, eps=1e-05):
    m = jnp.mean(x, axis=axis, keepdims=True)
    v = jnp.var(x, axis=axis, keepdims=True)
    return (x - m) / jnp.sqrt(v + eps)

def _scatter_add(tgt, idx, src, axis=0):
    return tgt.at[idx].add(src)

def _segment_sum(src, seg, n):
    return jax.ops.segment_sum(src, seg, n)
kernel_name = 'mk_gps_d1_gnn_r16_95bb1b'

def setup_inputs(seed: int=0):
    np.random.seed(seed)
    _w = jnp.asarray

    def _rec_inputs():
        import jax
        import jax.numpy as jnp
        _gk = jax.random.key(seed)
        x = -0.0003713 + 1 * jax.random.normal(jax.random.fold_in(_gk, 1), (3125, 256), jnp.float32)
        src = jax.random.randint(jax.random.fold_in(_gk, 2), (100000,), 0, 3125, jnp.int32)
        dst = jax.random.randint(jax.random.fold_in(_gk, 3), (100000,), 0, 3125, jnp.int32)
        _o = jnp.argsort(dst, stable=True)
        src = src[_o]
        dst = dst[_o]
        edge_attr_16 = 0.000398945 + 1.00003 * jax.random.normal(jax.random.fold_in(_gk, 11), (100000, 16), jnp.float32)
        return (x, src, dst, edge_attr_16)
    x, src, dst, edge_attr_16 = _rec_inputs()

    def _L0_gnn_setup():
        import jax, jax.numpy as jnp
        import numpy as np
        N, E = (3125, 25000)
        HEADS, DIMS, EDGE_DIM = (4, 64, 16)
        FEAT = HEADS * DIMS
        NEG_SLOPE = 0.2

        def _gatv2(x, edge_index, edge_attr, W_l, b_l, W_r, b_r, W_e, att, bias):
            n = x.shape[0]
            src, dst = (edge_index[0], edge_index[1])
            x_l = (x @ W_l.T + b_l).reshape(n, HEADS, DIMS)
            x_r = (x @ W_r.T + b_r).reshape(n, HEADS, DIMS)
            ones = jnp.ones((src.shape[0],), x.dtype)
            deg = jax.ops.segment_sum(ones, dst, num_segments=n)
            loop_attr = jax.ops.segment_sum(edge_attr, dst, num_segments=n)
            loop_attr = loop_attr / jnp.clip(deg, 1.0, None)[:, None]
            loop = jnp.arange(n, dtype=src.dtype)
            src = jnp.concatenate([src, loop])
            dst = jnp.concatenate([dst, loop])
            e_attr = jnp.concatenate([edge_attr, loop_attr], axis=0)
            e_feat = (e_attr @ W_e.T).reshape(-1, HEADS, DIMS)
            s = x_l[src] + x_r[dst] + e_feat
            s = jax.nn.leaky_relu(s, NEG_SLOPE)
            alpha = jnp.einsum('ehc,hc->eh', s, att)
            amax = jax.ops.segment_max(alpha, dst, num_segments=n)
            ex = jnp.exp(alpha - amax[dst])
            denom = jax.ops.segment_sum(ex, dst, num_segments=n)
            alpha = ex / (denom[dst] + 1e-16)
            out = jax.ops.segment_sum(alpha[..., None] * x_l[src], dst, num_segments=n)
            return out.reshape(n, FEAT) + bias
        key = jax.random.key(seed)
        ks = jax.random.split(key, 10)
        s = 0.05
        return {'x': jax.random.normal(ks[0], (N, FEAT), jnp.float32), 'edge_index': jax.random.randint(ks[1], (2, E), 0, N, jnp.int64), 'edge_attr': jax.random.normal(ks[2], (E, EDGE_DIM), jnp.float32), 'W_l': jax.random.normal(ks[3], (FEAT, FEAT), jnp.float32) * s, 'b_l': jnp.zeros((FEAT,), jnp.float32), 'W_r': jax.random.normal(ks[4], (FEAT, FEAT), jnp.float32) * s, 'b_r': jnp.zeros((FEAT,), jnp.float32), 'W_e': jax.random.normal(ks[5], (FEAT, EDGE_DIM), jnp.float32) * s, 'att': jax.random.normal(ks[6], (HEADS, DIMS), jnp.float32) * s, 'bias': jnp.zeros((FEAT,), jnp.float32)}
    _L0_gnn_all = _L0_gnn_setup()
    _L0_gnn_in = {k: v for k, v in _L0_gnn_all.items() if k in ('W_l', 'b_l', 'W_r', 'b_r', 'W_e', 'att', 'bias')}
    del _L0_gnn_all

    def _L0_mix_setup():
        import jax, jax.numpy as jnp
        import numpy as np
        EMB, HEADS, DEPTH, SEQ, BATCH = (256, 8, 4, 512, 4)
        DH = EMB // HEADS
        FF = 4 * EMB
        EPS = 1e-05

        def _layernorm(x, g, b):
            mu = x.mean(-1, keepdims=True)
            var = ((x - mu) ** 2).mean(-1, keepdims=True)
            return (x - mu) * jax.lax.rsqrt(var + EPS) * g + b

        def _linear_attn(x, Wq, Wk, Wv, Wo, bo):
            b, n, dm = x.shape
            split = lambda t: t.reshape(b, n, HEADS, DH).transpose(0, 2, 1, 3)
            scale = DH ** (-0.25)
            q = jax.nn.softmax(split(x @ Wq) * scale, axis=-1)
            k = jax.nn.softmax(split(x @ Wk) * scale, axis=-2)
            v = split(x @ Wv)
            context = jnp.einsum('bhnd,bhne->bhde', k, v)
            out = jnp.einsum('bhnd,bhde->bhne', q, context)
            out = out.transpose(0, 2, 1, 3).reshape(b, n, dm)
            return out @ Wo + bo

        def _forward(x, Wq, Wk, Wv, Wo, bo, ln1_g, ln1_b, W1, b1, W2, b2, ln2_g, ln2_b):
            for i in range(DEPTH):
                h = _layernorm(x, ln1_g[i], ln1_b[i])
                x = x + _linear_attn(h, Wq[i], Wk[i], Wv[i], Wo[i], bo[i])
                h = _layernorm(x, ln2_g[i], ln2_b[i])
                x = x + (jax.nn.gelu(h @ W1[i] + b1[i], approximate=False) @ W2[i] + b2[i])
            return x
        key = jax.random.key(seed)
        ks = jax.random.split(key, 8)
        w = lambda k, shape: jax.random.normal(k, shape, dtype=jnp.float32) * 0.02
        D = DEPTH
        return {'x': jax.random.normal(ks[0], (BATCH, SEQ, EMB), dtype=jnp.float32), 'Wq': w(ks[1], (D, EMB, EMB)), 'Wk': w(ks[2], (D, EMB, EMB)), 'Wv': w(ks[3], (D, EMB, EMB)), 'Wo': w(ks[4], (D, EMB, EMB)), 'bo': jnp.zeros((D, EMB), jnp.float32), 'ln1_g': jnp.ones((D, EMB), jnp.float32), 'ln1_b': jnp.zeros((D, EMB), jnp.float32), 'W1': w(ks[5], (D, EMB, FF)), 'b1': jnp.zeros((D, FF), jnp.float32), 'W2': w(ks[6], (D, FF, EMB)), 'b2': jnp.zeros((D, EMB), jnp.float32), 'ln2_g': jnp.ones((D, EMB), jnp.float32), 'ln2_b': jnp.zeros((D, EMB), jnp.float32)}
    _L0_mix_all = _L0_mix_setup()
    _L0_mix_in = {k: v for k, v in _L0_mix_all.items() if k in ('Wq', 'Wk', 'Wv', 'Wo', 'bo', 'ln1_g', 'ln1_b', 'W1', 'b1', 'W2', 'b2', 'ln2_g', 'ln2_b')}
    del _L0_mix_all

    def _L0_ffn_setup():
        import jax, jax.numpy as jnp
        import numpy as np
        B, S, D, F, E, K = (8, 128, 256, 1024, 8, 2)
        key = jax.random.key(seed)
        ks = jax.random.split(key, 10)
        s = 0.02
        return {'x': jax.random.normal(ks[0], (B, S, D), dtype=jnp.float32), 'Wr': jax.random.normal(ks[1], (D, E), dtype=jnp.float32) * s, 'W1s': jax.random.normal(ks[2], (D, F), dtype=jnp.float32) * s, 'b1s': jnp.zeros((F,), dtype=jnp.float32), 'W2s': jax.random.normal(ks[3], (F, D), dtype=jnp.float32) * s, 'b2s': jnp.zeros((D,), dtype=jnp.float32), 'W1p': jax.random.normal(ks[4], (E, D, F), dtype=jnp.float32) * s, 'b1p': jnp.zeros((E, F), dtype=jnp.float32), 'W2p': jax.random.normal(ks[5], (E, F, D), dtype=jnp.float32) * s, 'b2p': jnp.zeros((E, D), dtype=jnp.float32)}
    _L0_ffn_all = _L0_ffn_setup()
    _L0_ffn_in = {k: v for k, v in _L0_ffn_all.items() if k in ('Wr', 'W1s', 'b1s', 'W2s', 'b2s', 'W1p', 'b1p', 'W2p', 'b2p')}
    del _L0_ffn_all
    return {'x': x, 'src': src, 'dst': dst, 'edge_attr_16': edge_attr_16, 'L0_gnn_W_l': _L0_gnn_in['W_l'], 'L0_gnn_b_l': _L0_gnn_in['b_l'], 'L0_gnn_W_r': _L0_gnn_in['W_r'], 'L0_gnn_b_r': _L0_gnn_in['b_r'], 'L0_gnn_W_e': _L0_gnn_in['W_e'], 'L0_gnn_att': _L0_gnn_in['att'], 'L0_gnn_bias': _L0_gnn_in['bias'], 'L0_mix_Wq': _L0_mix_in['Wq'], 'L0_mix_Wk': _L0_mix_in['Wk'], 'L0_mix_Wv': _L0_mix_in['Wv'], 'L0_mix_Wo': _L0_mix_in['Wo'], 'L0_mix_bo': _L0_mix_in['bo'], 'L0_mix_ln1_g': _L0_mix_in['ln1_g'], 'L0_mix_ln1_b': _L0_mix_in['ln1_b'], 'L0_mix_W1': _L0_mix_in['W1'], 'L0_mix_b1': _L0_mix_in['b1'], 'L0_mix_W2': _L0_mix_in['W2'], 'L0_mix_b2': _L0_mix_in['b2'], 'L0_mix_ln2_g': _L0_mix_in['ln2_g'], 'L0_mix_ln2_b': _L0_mix_in['ln2_b'], 'L0_ffn_Wr': _L0_ffn_in['Wr'], 'L0_ffn_W1s': _L0_ffn_in['W1s'], 'L0_ffn_b1s': _L0_ffn_in['b1s'], 'L0_ffn_W2s': _L0_ffn_in['W2s'], 'L0_ffn_b2s': _L0_ffn_in['b2s'], 'L0_ffn_W1p': _L0_ffn_in['W1p'], 'L0_ffn_b1p': _L0_ffn_in['b1p'], 'L0_ffn_W2p': _L0_ffn_in['W2p'], 'L0_ffn_b2p': _L0_ffn_in['b2p']}

def reference(x, src, dst, edge_attr_16, L0_gnn_W_l, L0_gnn_b_l, L0_gnn_W_r, L0_gnn_b_r, L0_gnn_W_e, L0_gnn_att, L0_gnn_bias, L0_mix_Wq, L0_mix_Wk, L0_mix_Wv, L0_mix_Wo, L0_mix_bo, L0_mix_ln1_g, L0_mix_ln1_b, L0_mix_W1, L0_mix_b1, L0_mix_W2, L0_mix_b2, L0_mix_ln2_g, L0_mix_ln2_b, L0_ffn_Wr, L0_ffn_W1s, L0_ffn_b1s, L0_ffn_W2s, L0_ffn_b2s, L0_ffn_W1p, L0_ffn_b1p, L0_ffn_W2p, L0_ffn_b2p):
    import jax
    import jax.numpy as jnp

    def _L0_gnn_ref(x, edge_index, edge_attr, W_l, b_l, W_r, b_r, W_e, att, bias):
        import jax, jax.numpy as jnp
        import numpy as np
        N, E = (3125, 25000)
        HEADS, DIMS, EDGE_DIM = (4, 64, 16)
        FEAT = HEADS * DIMS
        NEG_SLOPE = 0.2

        def _gatv2(x, edge_index, edge_attr, W_l, b_l, W_r, b_r, W_e, att, bias):
            n = x.shape[0]
            src, dst = (edge_index[0], edge_index[1])
            x_l = (x @ W_l.T + b_l).reshape(n, HEADS, DIMS)
            x_r = (x @ W_r.T + b_r).reshape(n, HEADS, DIMS)
            ones = jnp.ones((src.shape[0],), x.dtype)
            deg = jax.ops.segment_sum(ones, dst, num_segments=n)
            loop_attr = jax.ops.segment_sum(edge_attr, dst, num_segments=n)
            loop_attr = loop_attr / jnp.clip(deg, 1.0, None)[:, None]
            loop = jnp.arange(n, dtype=src.dtype)
            src = jnp.concatenate([src, loop])
            dst = jnp.concatenate([dst, loop])
            e_attr = jnp.concatenate([edge_attr, loop_attr], axis=0)
            e_feat = (e_attr @ W_e.T).reshape(-1, HEADS, DIMS)
            s = x_l[src] + x_r[dst] + e_feat
            s = jax.nn.leaky_relu(s, NEG_SLOPE)
            alpha = jnp.einsum('ehc,hc->eh', s, att)
            amax = jax.ops.segment_max(alpha, dst, num_segments=n)
            ex = jnp.exp(alpha - amax[dst])
            denom = jax.ops.segment_sum(ex, dst, num_segments=n)
            alpha = ex / (denom[dst] + 1e-16)
            out = jax.ops.segment_sum(alpha[..., None] * x_l[src], dst, num_segments=n)
            return out.reshape(n, FEAT) + bias
        h = _gatv2(x, edge_index, edge_attr, W_l, b_l, W_r, b_r, W_e, att, bias)
        h = jax.nn.silu(h)
        return x + h

    def _L0_mix_ref(x, Wq, Wk, Wv, Wo, bo, ln1_g, ln1_b, W1, b1, W2, b2, ln2_g, ln2_b):
        import jax, jax.numpy as jnp
        import numpy as np
        EMB, HEADS, DEPTH, SEQ, BATCH = (256, 8, 4, 512, 4)
        DH = EMB // HEADS
        FF = 4 * EMB
        EPS = 1e-05

        def _layernorm(x, g, b):
            mu = x.mean(-1, keepdims=True)
            var = ((x - mu) ** 2).mean(-1, keepdims=True)
            return (x - mu) * jax.lax.rsqrt(var + EPS) * g + b

        def _linear_attn(x, Wq, Wk, Wv, Wo, bo):
            b, n, dm = x.shape
            split = lambda t: t.reshape(b, n, HEADS, DH).transpose(0, 2, 1, 3)
            scale = DH ** (-0.25)
            q = jax.nn.softmax(split(x @ Wq) * scale, axis=-1)
            k = jax.nn.softmax(split(x @ Wk) * scale, axis=-2)
            v = split(x @ Wv)
            context = jnp.einsum('bhnd,bhne->bhde', k, v)
            out = jnp.einsum('bhnd,bhde->bhne', q, context)
            out = out.transpose(0, 2, 1, 3).reshape(b, n, dm)
            return out @ Wo + bo

        def _forward(x, Wq, Wk, Wv, Wo, bo, ln1_g, ln1_b, W1, b1, W2, b2, ln2_g, ln2_b):
            for i in range(DEPTH):
                h = _layernorm(x, ln1_g[i], ln1_b[i])
                x = x + _linear_attn(h, Wq[i], Wk[i], Wv[i], Wo[i], bo[i])
                h = _layernorm(x, ln2_g[i], ln2_b[i])
                x = x + (jax.nn.gelu(h @ W1[i] + b1[i], approximate=False) @ W2[i] + b2[i])
            return x
        return _forward(x, Wq, Wk, Wv, Wo, bo, ln1_g, ln1_b, W1, b1, W2, b2, ln2_g, ln2_b)

    def _L0_ffn_ref(x, Wr, W1s, b1s, W2s, b2s, W1p, b1p, W2p, b2p):
        import jax, jax.numpy as jnp
        import numpy as np
        B, S, D, F, E, K = (8, 128, 256, 1024, 8, 2)
        gelu = lambda t: jax.nn.gelu(t, approximate=False)
        shared = gelu(x @ W1s + b1s) @ W2s + b2s
        rw = jax.nn.softmax(x @ Wr, axis=-1)
        topw, topi = jax.lax.top_k(rw, K)
        topw = topw / jnp.sum(topw, axis=-1, keepdims=True)
        mask = jnp.sum(jax.nn.one_hot(topi, E, dtype=topw.dtype) * topw[..., None], axis=-2)
        h = gelu(jnp.einsum('bsd,edf->bsef', x, W1p) + b1p)
        priv = jnp.einsum('bsef,efd->bsed', h, W2p) + b2p
        routed = jnp.einsum('bsed,bse->bsd', priv, mask)
        return shared + routed
    edge_index = jnp.stack([src, dst])
    xn = _layernorm(x, axis=-1)
    x = x + _L0_gnn_ref(xn, edge_index, edge_attr_16, L0_gnn_W_l, L0_gnn_b_l, L0_gnn_W_r, L0_gnn_b_r, L0_gnn_W_e, L0_gnn_att, L0_gnn_bias) + _L0_mix_ref(xn[None], L0_mix_Wq, L0_mix_Wk, L0_mix_Wv, L0_mix_Wo, L0_mix_bo, L0_mix_ln1_g, L0_mix_ln1_b, L0_mix_W1, L0_mix_b1, L0_mix_W2, L0_mix_b2, L0_mix_ln2_g, L0_mix_ln2_b)[0]
    x = x + _L0_ffn_ref(_layernorm(x, axis=-1)[None], L0_ffn_Wr, L0_ffn_W1s, L0_ffn_b1s, L0_ffn_W2s, L0_ffn_b2s, L0_ffn_W1p, L0_ffn_b1p, L0_ffn_W2p, L0_ffn_b2p)[0]
    return x

_drawn_inputs = setup_inputs


def setup_inputs(seed=0):
    import zlib

    import numpy as np

    out = dict(_drawn_inputs(seed))
    spreads = {'L0_gnn_b_l': (0.0, 0.431),
     'L0_gnn_b_r': (0.0, 2.0),
     'L0_gnn_bias': (0.0, 0.447),
     'L0_mix_bo': (0.0, 0.1),
     'L0_mix_ln1_g': (1.0, 0.6),
     'L0_mix_ln1_b': (0.0, 0.8),
     'L0_mix_b1': (0.0, 0.315),
     'L0_mix_b2': (0.0, 0.1),
     'L0_mix_ln2_g': (1.0, 0.6),
     'L0_mix_ln2_b': (0.0, 0.8),
     'L0_ffn_b1s': (0.0, 0.74),
     'L0_ffn_b2s': (0.0, 0.429),
     'L0_ffn_b1p': (0.0, 0.8),
     'L0_ffn_b2p': (0.0, 0.332)}
    factors = {'edge_attr_16': 8.0,
     'L0_gnn_W_r': 8.0,
     'L0_gnn_W_e': 8.0,
     'L0_gnn_att': 7.79,
     'L0_mix_Wq': 8.0,
     'L0_mix_Wk': 8.0,
     'L0_mix_Wv': 4.181,
     'L0_mix_Wo': 3.888,
     'L0_ffn_W1p': 3.234}
    for name, (base, spread) in spreads.items():
        noise = np.random.default_rng([zlib.crc32(name.encode()), seed]).standard_normal(out[name].shape)
        drawn = base * np.exp(spread * noise) if base else spread * noise
        out[name] = jnp.asarray(drawn.astype(out[name].dtype))
    for name, factor in factors.items():
        out[name] = (out[name] * factor).astype(out[name].dtype)
    return out
```

```python
from contextlib import ExitStack

import numpy as np

import concourse.bass as bass
from concourse import mybir

F32 = mybir.dt.float32
I32 = mybir.dt.int32
U32 = mybir.dt.uint32
ALU = mybir.AluOpType
ACT = mybir.ActivationFunctionType
AX = mybir.AxisListType

N, D = 3125, 256
P = 125
NT = N // P
GT = 5
NG = NT // GT
GN = GT * P
KC = D // 128
HALVES = ((0, 313), (313, 312))
DEPTH = 4
EXPERTS = 8

E, ED = 100000, 16
TE = 125
NTE = E // TE
WN = 112
NW = -(-N // WN)
GH = 4
IG = 4
STEPS = -(-(NTE + NW - 1) // (2 * IG))
CH = -(-(2 * IG * STEPS) // 128)
ITEMS = 128 * CH
RUN = CH * TE
EA0 = D + 2 * GH
MW = EA0 + ED + 1
SLOPE = 0.2
LOW = -1.0e30
MH, MD = 8, 32
FF = 1024
FC = FF // 128
QK_SCALE = float(MD) ** -0.25
EPS = 1e-5
LOWEST = -3.0e38
CONSTS = 2


class Names:

    def __init__(self, nc):
        self._nc, self._all = nc, {}

    def __getitem__(self, name):
        if name not in self._all:
            self._all[name] = self._nc.alloc_semaphore(name=name)
        return self._all[name]

    def give_back(self):
        self._nc.clear_and_free_semaphores(list(self._all.values()))
        self._nc.all_engine_barrier()


def chunked(w):
    return w.rearrange("(k p) n -> p k n", p=128)


def columns(v):
    v = np.asarray(v)
    return np.ascontiguousarray(np.swapaxes(v.reshape(v.shape[:-1] + (-1, 128)), -1, -2))


def layer_norm(v, s, tag, n, src, dst, st, mv, ve, rstd):
    v.sem_inc(s[tag + "_seen"], 1)
    for j in range(GT):
        v.bn_stats(st[:, j, :], src(j)).then_inc(s[tag + "_stats"], 1)
    v.wait_ge(s[tag + "_stats"], GT * n + GT)
    v.sem_inc(s[tag + "_seen"], 1)
    for j in range(GT):
        v.bn_aggr(mv[:, j, :], st[:, j, :]).then_inc(s[tag + "_aggr"], 1)
    v.wait_ge(s[tag + "_aggr"], GT * n + GT)
    v.tensor_scalar(ve[:, :], mv[:, :, 1], EPS, None, ALU.add).then_inc(s[tag + "_vareps"], 1)
    v.wait_ge(s[tag + "_rstd"], n + 1)
    for j in range(GT):
        v.tensor_scalar(dst(j), src(j), mv[:, j, 0:1], rstd[:, j:j + 1],
                        ALU.subtract, ALU.mult).then_inc(s[tag + "_out"], 1)


def rstd_side(p, s, tag, n, ve, rstd, mhalf):
    p.wait_ge(s[tag + "_vareps"], n + 1)
    p.tensor_tensor(rstd[:, :], ve[:, :], mhalf[:, :], ALU.pow).then_inc(s[tag + "_rstd"], 1)


def row(x, g, j):
    return x[:, g * GT + j, :] if isinstance(g, int) else x[:, bass.ds(g * GT + j, 1), :].rearrange("p a d -> p (a d)")


def picked(a, l):
    if isinstance(l, int):
        return a[l]
    return a[bass.ds(l, 1)].rearrange("a b c -> (a b) c" if len(a.shape) == 3 else "a b -> (a b)")


def mixer(nc, s, XS, ident, w):
    with ExitStack() as c:
        def sb(name, shape, dt=F32):
            return c.enter_context(nc.sbuf_tensor(name, shape, dt))

        def ps(name, shape):
            return c.enter_context(nc.psum_tensor(name, shape, F32))

        KK = sb("m_kk", [P, NT, D])
        VV = sb("m_vv", [P, NT, D])
        HT = sb("m_ht", [128, KC, N])
        H2 = sb("m_h2", [128, KC, GN])
        N2 = sb("m_n2", [P, GT, D])
        HID = sb("m_hid", [128, FC, GN])
        QE = sb("m_qe", [P, GT, D])
        QN = sb("m_qn", [P, GT, D])
        wqkv = sb("m_wqkv", [128, KC, 3 * D])
        wo = sb("m_wo", [128, KC, D])
        w1 = sb("m_w1", [128, KC, FF])
        w2 = sb("m_w2", [128, FC, D])
        ln1 = sb("m_ln1", [128, 2, KC])
        ln2 = sb("m_ln2", [128, 2, KC])
        b1 = sb("m_b1", [128, FC])
        rows = sb("m_rows", [1, 2, D])
        ones = sb("m_ones", [128, 128])
        st = sb("m_st", [P, GT, 6])
        mv = sb("m_mv", [P, GT, 2])
        ve = sb("m_ve", [P, GT])
        rstd = sb("m_rstd", [P, GT])
        mhalf = sb("m_mhalf", [P, GT])
        qmax = sb("m_qmax", [P, GT, MH])
        qsum = sb("m_qsum", [P, GT * MH])
        qrec = sb("m_qrec", [P, GT * MH])
        KM = sb("m_kmax", [P, D])
        KG = sb("m_kgroup", [P, D])
        kcol = sb("m_kcol", [128, KC])
        kdiag = sb("m_kdiag", [128, KC, 128])
        CT = sb("m_ct", [128, KC, 128])
        rk = sb("m_rk", [128, KC])
        MO = sb("m_mo", [128, KC, D])
        pH = ps("m_pH", [128, 4, 512])
        pO0 = ps("m_pO0", [128, 512])
        pT = ps("m_pT", [128, 12, 128])
        pO = (pO0[:, 0:D], pT[:, 10:12, :].rearrange("p a b -> p (a b)"))

        block = c.enter_context(nc.Block())

        PER_T, PER_O = 16, 52
        T1 = lambda l, g: PER_T * l + 2 * g + 1
        TQ = lambda l, g: PER_T * l + 2 * g + 2
        TQ_LAST, TK = 9, 10
        T2 = lambda l, g: PER_T * l + 11 + g
        OUT_FIRST, OUT_LAST = 2, 47
        OUT_ATTN = lambda g: 7 + 10 * g
        OUT_MLP = lambda g: 12 + 10 * g
        ATTN_DMAS, FF_DMAS = 7, 6

        @block.sync
        def _(sp):
            def load_attn(l):
                for i, name in enumerate(("Wq", "Wk", "Wv")):
                    sp.dma_start(wqkv[:, :, i * D:(i + 1) * D], chunked(picked(w[name], l))).then_inc(s["m_attn_w"], 16)
                sp.dma_start(wo[:, :, :], chunked(picked(w["Wo"], l))).then_inc(s["m_attn_w"], 16)
                sp.dma_start(ln1[:, 0, :], picked(w["ln1_g"], l)).then_inc(s["m_attn_w"], 16)
                sp.dma_start(ln1[:, 1, :], picked(w["ln1_b"], l)).then_inc(s["m_attn_w"], 16)
                sp.dma_start(rows[0:1, 0, :], picked(w["bo"], l).unsqueeze(0)).then_inc(s["m_attn_w"], 16)

            def load_ff(l):
                sp.dma_start(w1[:, :, :], chunked(picked(w["W1"], l))).then_inc(s["m_ff_w"], 16)
                sp.dma_start(w2[:, :, :], chunked(picked(w["W2"], l))).then_inc(s["m_ff_w"], 16)
                sp.dma_start(ln2[:, 0, :], picked(w["ln2_g"], l)).then_inc(s["m_ff_w"], 16)
                sp.dma_start(ln2[:, 1, :], picked(w["ln2_b"], l)).then_inc(s["m_ff_w"], 16)
                sp.dma_start(b1[:, :], picked(w["b1"], l)).then_inc(s["m_ff_w"], 16)
                sp.dma_start(rows[0:1, 1, :], picked(w["b2"], l).unsqueeze(0)).then_inc(s["m_ff_w"], 16)

            load_attn(0)
            load_ff(0)
            with sp.Fori(0, DEPTH - 1) as l:
                sp.wait_ge(s["m_o_full"], PER_O * l + OUT_ATTN(NG - 2) + GT)
                load_attn(l + 1)
                sp.wait_ge(s["m_o_full"], PER_O * l + PER_O)
                load_ff(l + 1)

        @block.gpsimd
        def _(p):
            p.memset(mhalf[:, :], -0.5).then_inc(s["m_const"], 1)
            p.memset(ones[:, :], 1.0).then_inc(s["m_const"], 1)
            p.memset(CT[:, :, :], 0.0).then_inc(s["m_const"], 1)
            p.wait_ge(s["m_const"], 3)
            with p.Fori(0, NG + 2 * NG * DEPTH) as n:
                rstd_side(p, s, "m_ln", n, ve, rstd, mhalf)

        @block.tensor
        def _(pe):
            def cols(g, j):
                return slice((g * GT + j) * P, (g * GT + j + 1) * P) if isinstance(g, int) else bass.ds((g * GT + j) * P, P)

            def transposes(n, src, ready, count, outs):
                pe.wait_ge(s[ready], count)
                pe.wait_ge(s["m_t_out"], n + 1)
                pe.wait_ge(s["m_o_out"], outs + 2)
                for k in range(KC):
                    for j in range(GT):
                        ins = pe.transpose(pT[:, GT * k + j, 0:P], src(j)[:, k * 128:(k + 1) * 128], ident[0:P, 0:P])
                ins.then_inc(s["m_t_full"], 1)

            def qkv(l, g):
                for j in range(GT):
                    t = NT * l + g * GT + j
                    b = 2 * (j % 2)
                    pe.wait_ge(s["m_qkv_act"], t + (j == 0))
                    pe.wait_ge(s["m_qkv_dve"], t + (j == 0))
                    for k in range(KC):
                        pe.matmul(pH[0:P, b, 0:256], HT[:, k, cols(g, j)], wqkv[:, k, 0:256], start=(k == 0), stop=(k == KC - 1))
                    for k in range(KC):
                        ins = pe.matmul(pH[0:P, b + 1, 0:512], HT[:, k, cols(g, j)], wqkv[:, k, 256:768],
                                        start=(k == 0), stop=(k == KC - 1))
                    ins.then_inc(s["m_qkv_full"], 1)

            def context(l, g, first, last):
                pe.wait_ge(s["m_kexp"], NG * l + g + 1)
                for j in range(GT):
                    f, e = first and j == 0, last and j == GT - 1
                    k_, v_ = row(KK, g, j), row(VV, g, j)
                    for m in range(KC):
                        half = slice(m * 128, (m + 1) * 128)
                        pe.matmul(pH[:, m, 0:128], v_[:, half], k_[:, half], start=f, stop=e)
                        ins = pe.matmul(pH[:, 2 + m, 0:1], k_[:, half], ones[0:P, 0:1], start=f, stop=e)
                if last:
                    ins.then_inc(s["m_ctx"], 1)

            def out_rows(l, base, parity, bias, lhs, rhs, chunks, t_out):
                for j in range(GT):
                    o = pO[(j + parity) % 2][0:P, :]
                    if (j + parity) % 2:
                        pe.wait_ge(s["m_t_out"], t_out + 1)
                    pe.wait_ge(s["m_o_out"], PER_O * l + base + j + 1)
                    for k in range(chunks):
                        pe.matmul(o, lhs(k, j), rhs[:, k, :], start=(k == 0), stop=False)
                    pe.matmul(o, ones[0:1, 0:P], rows[0:1, bias, :], start=False, stop=True).then_inc(s["m_o_full"], 1)

            def attn_out(l, g, base, parity):
                t_out = PER_T * l + TK + 1 if g == 0 else T2(l, g - 1) + 1
                out_rows(l, base, parity, 0, lambda k, j: HT[:, k, cols(g, j)], MO, KC, t_out)

            def mlp_out(l, g, base, parity):
                pe.wait_ge(s["m_gelu"], FC * (NG * l + g) + FC + 2)
                out_rows(l, base, parity, 1, lambda k, j: HID[:, k, j * P:(j + 1) * P], w2, FC,
                         T2(l, min(g + 1, NG - 1)) + 1)

            def hidden(l, g):
                pe.wait_ge(s["m_t_out"], T2(l, g) + 2)
                for f in range(FC):
                    b = 2 * (f % 2)
                    pe.wait_ge(s["m_gelu"], FC * (NG * l + g) + f + 1)
                    for h, (at, n) in enumerate(HALVES):
                        for k in range(KC):
                            ins = pe.matmul(pH[:, b + h, 0:n], w1[:, k, f * 128:(f + 1) * 128], H2[:, k, at:at + n],
                                            start=(k == 0), stop=(k == KC - 1))
                    ins.then_inc(s["m_hid"], 1)

            pe.wait_ge(s["m_const"], 3)
            with pe.Fori(0, DEPTH) as l:
                pe.wait_ge(s["m_attn_w"], 16 * ATTN_DMAS * l + 16 * ATTN_DMAS)
                transposes(PER_T * l, lambda j: row(KK, 0, j), "m_ln_out", 50 * l + 25, PER_O * l)
                pe.wait_ge(s["m_t_out"], PER_T * l + 2)
                for g in range(NG - 1):
                    qkv(l, g)
                    transposes(T1(l, g), lambda j: row(KK, g + 1, j), "m_ln_out", 50 * l + 25, PER_O * l)
                    transposes(TQ(l, g), lambda j: QN[:, j, :], "m_qn", NG * l + g + 1, PER_O * l)
                qkv(l, NG - 1)
                transposes(PER_T * l + TQ_LAST, lambda j: QN[:, j, :], "m_qn", NG * l + NG, PER_O * l)

                pe.wait_ge(s["m_kmax"], (NG + 1) * l + NG + 1)
                pe.wait_ge(s["m_t_out"], PER_T * l + TK + 1)
                for k in range(KC):
                    ins = pe.transpose(pT[:, k, 0:P], KM[:, k * 128:(k + 1) * 128], ident[0:P, 0:P])
                ins.then_inc(s["m_t_full"], 1)
                pe.wait_ge(s["m_kdiag"], KC * l + KC)
                for k in range(KC):
                    ins = pe.matmul(pT[0:P, 4 + k, :], ones[:, 0:P], kdiag[:, k, :], start=True, stop=True)
                ins.then_inc(s["m_kmax_rows"], 1)

                pe.wait_ge(s["m_qkv_act"], NT * l + NT + 1)
                pe.wait_ge(s["m_qkv_dve"], NT * l + NT + 1)
                context(l, 0, True, False)
                for g in range(1, NG - 1):
                    context(l, g, False, False)
                context(l, NG - 1, False, True)
                pe.wait_ge(s["m_ct"], 8 * l + 8)
                pe.wait_ge(s["m_t_out"], PER_T * l + TK + 2)
                for m in range(KC):
                    pe.wait_ge(s["m_o_out"], PER_O * l + m + 1)
                    pe.matmul(pO[m], CT[:, m, :], wo[:, m, :], start=True, stop=True).then_inc(s["m_o_full"], 1)
                pe.wait_ge(s["m_o_out"], PER_O * l + 4)
                pe.wait_ge(s["m_ksub"], NG * l + NG)

                attn_out(l, 0, OUT_FIRST, 0)
                transposes(T2(l, 0), lambda j: N2[:, j, :], "m_ln_out", 50 * l + 30, PER_O * l + OUT_FIRST + GT)
                pe.wait_ge(s["m_ff_w"], 16 * FF_DMAS * l + 16 * FF_DMAS)
                for g in range(NG - 1):
                    attn_out(l, g + 1, OUT_ATTN(g), 1)
                    hidden(l, g)
                    transposes(T2(l, g + 1), lambda j: N2[:, j, :], "m_ln_out", 50 * l + 10 * g + 35, PER_O * l + OUT_ATTN(g) + GT)
                    mlp_out(l, g, OUT_MLP(g), 0)
                hidden(l, NG - 1)
                mlp_out(l, NG - 1, OUT_LAST, 1)

        @block.scalar
        def _(a):
            with a.Fori(0, DEPTH) as l:
                with a.Fori(0, NG) as g:
                    for j in range(GT):
                        b = 2 * (j % 2)
                        a.wait_ge(s["m_qkv_full"], NT * l + g * GT + j + 1)
                        a.activation(row(KK, g, j), pH[0:P, b + 1, 0:256], ACT.Copy)
                        a.activation(row(VV, g, j), pH[0:P, b + 1, 256:512], ACT.Copy).then_inc(s["m_qkv_act"], 1)
                    a.wait_ge(s["m_qkv_dve"], NT * l + g * GT + GT + 1)
                    a.activation(QE[:, :, :], QE[:, :, :], ACT.Exp, scale=QK_SCALE).then_inc(s["m_qexp"], 1)
                with a.Fori(0, NG) as g:
                    a.wait_ge(s["m_ksub"], NG * l + g + 1)
                    kg = KK[:, bass.ds(g * GT, GT), :]
                    a.activation(kg, kg, ACT.Exp, scale=QK_SCALE).then_inc(s["m_kexp"], 1)
                a.wait_ge(s["m_ff_w"], 16 * FF_DMAS * l + 16 * FF_DMAS)
                with a.Fori(0, NG) as g:
                    a.wait_ge(s["m_o_full"], PER_O * l + 10 * g + 7)
                    for f in range(FC):
                        b = 2 * (f % 2)
                        a.wait_ge(s["m_hid"], FC * (NG * l + g) + f + 1)
                        for h, (at, n) in enumerate(HALVES):
                            ins = a.activation(HID[:, f, at:at + n], pH[:, b + h, 0:n], ACT.Gelu, bias=b1[:, f:f + 1])
                        ins.then_inc(s["m_gelu"], 1)

        @block.vector
        def _(v):
            def norm(n, src, dst):
                layer_norm(v, s, "m_ln", n, src, dst, st, mv, ve, rstd)

            def out_transposed(n, dst, ln=None):
                v.wait_ge(s["m_t_full"], n + 1)
                for k in range(KC):
                    o = dst(k).rearrange("p (j q) -> p j q", j=GT)
                    i = pT[:, GT * k:GT * k + GT, 0:P]
                    if ln is None:
                        ins = v.tensor_copy(o, i)
                    else:
                        ins = v.tensor_scalar(o, i, ln[:, 0, k:k + 1], ln[:, 1, k:k + 1], ALU.mult, ALU.add)
                ins.then_inc(s["m_t_out"], 1)

            def group_cols(g):
                return lambda k: HT[:, k, g * GN:(g + 1) * GN] if isinstance(g, int) else HT[:, k, bass.ds(g * GN, GN)]

            def q_tiles(l, g):
                for j in range(GT):
                    t = NT * l + g * GT + j
                    b = 2 * (j % 2)
                    v.wait_ge(s["m_qkv_full"], t + 1)
                    q = pH[0:P, b, 0:256].rearrange("p (h d) -> p h d", h=MH)
                    v.tensor_reduce(qmax[:, j, :], q, AX.X, ALU.max).then_inc(s["m_qmax"], 1)
                    v.wait_ge(s["m_qmax"], t + 1)
                    v.tensor_tensor(QE[:, j, :].rearrange("p (h d) -> p h d", h=MH), q,
                                    qmax[:, j, :].unsqueeze(2).broadcast_to([P, MH, MD]), ALU.subtract).then_inc(s["m_qkv_dve"], 1)

            def k_max(l, g):
                v.wait_ge(s["m_qkv_act"], NT * l + g * GT + GT + 1)
                kg = KK[:, g * GT:(g + 1) * GT, :] if isinstance(g, int) else KK[:, bass.ds(g * GT, GT), :]
                v.tensor_reduce(KG[:, :], kg.rearrange("p j d -> p d j"), AX.X, ALU.max).then_inc(s["m_kgroup"], 1)
                v.wait_ge(s["m_kgroup"], NG * l + g + 1)
                v.wait_ge(s["m_kmax"], (NG + 1) * l + g + 1)
                v.tensor_tensor(KM[:, :], KM[:, :], KG[:, :], ALU.max).then_inc(s["m_kmax"], 1)

            def q_finish(l, g):
                v.wait_ge(s["m_qexp"], NG * l + g + 1)
                e = QE[:, :, :].rearrange("p j (h d) -> p (j h) d", h=MH)
                v.tensor_reduce(qsum[:, :], e, AX.X, ALU.add).then_inc(s["m_qsum"], 1)
                v.wait_ge(s["m_qsum"], NG * l + g + 1)
                v.reciprocal(qrec[:, :], qsum[:, :]).then_inc(s["m_qrec"], 1)
                v.wait_ge(s["m_qrec"], NG * l + g + 1)
                v.tensor_tensor(QN[:, :, :].rearrange("p j (h d) -> p (j h) d", h=MH), e,
                                qrec[:, :].unsqueeze(2).broadcast_to([P, GT * MH, MD]), ALU.mult).then_inc(s["m_qn"], 1)

            def add_rows(l, g, base, parity):
                for j in range(GT):
                    v.wait_ge(s["m_o_full"], PER_O * l + base + j + 1)
                    x = row(XS, g, j)
                    v.tensor_tensor(x, x, pO[(j + parity) % 2][0:P, :], ALU.add).then_inc(s["m_o_out"], 1)

            def norm_after(l, g, n, base, dst):
                v.wait_ge(s["m_o_out"], PER_O * l + base + GT + 2)
                norm(n, lambda j: row(XS, g, j), dst)

            for name, k in (("m_t_out", 1), ("m_o_out", 2), ("m_gelu", 2), ("m_qkv_act", 1), ("m_qkv_dve", 1)):
                v.sem_inc(s[name], k)
            with v.Fori(0, NG) as g:
                norm(g, lambda j: row(XS, g, j), lambda j: row(KK, g, j))
            with v.Fori(0, DEPTH) as l:
                v.wait_ge(s["m_attn_w"], 16 * ATTN_DMAS * l + 16 * ATTN_DMAS)
                v.memset(KM[:, :], LOWEST).then_inc(s["m_kmax"], 1)
                out_transposed(PER_T * l, group_cols(0), ln1)
                with v.Fori(0, NG - 1) as g:
                    q_tiles(l, g)
                    out_transposed(T1(l, g), group_cols(g + 1), ln1)
                    k_max(l, g)
                    q_finish(l, g)
                    out_transposed(TQ(l, g), group_cols(g))
                q_tiles(l, NG - 1)
                k_max(l, NG - 1)
                q_finish(l, NG - 1)
                out_transposed(PER_T * l + TQ_LAST, group_cols(NG - 1))

                v.wait_ge(s["m_t_full"], PER_T * l + TK + 1)
                v.tensor_reduce(kcol[:, :], pT[:, 0:KC, 0:P], AX.X, ALU.max).then_inc(s["m_t_out"], 1)
                v.wait_ge(s["m_t_out"], PER_T * l + TK + 2)
                for k in range(KC):
                    v.tensor_scalar(kdiag[:, k, :], ident[:, :], kcol[:, k:k + 1], None, ALU.mult).then_inc(s["m_kdiag"], 1)
                v.wait_ge(s["m_kmax_rows"], l + 1)
                v.wait_ge(s["m_qkv_act"], NT * l + NT + 1)
                v.sem_inc(s["m_k_seen"], 1)
                kmax_rows = pT[0:P, 4:6, :].rearrange("p a b -> p (a b)").unsqueeze(1).broadcast_to([P, GT, D])
                with v.Fori(0, NG) as g:
                    kg = KK[:, bass.ds(g * GT, GT), :]
                    v.tensor_tensor(kg, kg, kmax_rows, ALU.subtract).then_inc(s["m_ksub"], 1)

                v.wait_ge(s["m_ctx"], l + 1)
                v.reciprocal(rk[:, :], pH[:, 2:4, 0]).then_inc(s["m_rk"], 1)
                for m in range(KC):
                    for b in range(4):
                        r = slice(32 * b, 32 * b + 32)
                        v.tensor_copy(CT[r, m, 32 * b:32 * b + 32], pH[r, m, 32 * b:32 * b + 32]).then_inc(s["m_ct"], 1)
                v.wait_ge(s["m_rk"], l + 1)
                for m in range(KC):
                    v.wait_ge(s["m_o_full"], PER_O * l + m + 1)
                    v.tensor_scalar(MO[:, m, :], pO[m], rk[:, m:m + 1], None, ALU.mult).then_inc(s["m_o_out"], 1)

                v.wait_ge(s["m_ff_w"], 16 * FF_DMAS * l + 16 * FF_DMAS)
                to_n2, to_h2 = (lambda j: N2[:, j, :]), (lambda k: H2[:, k, :])
                add_rows(l, 0, OUT_FIRST, 0)
                norm_after(l, 0, 10 * l + 5, OUT_FIRST, to_n2)
                out_transposed(T2(l, 0), to_h2, ln2)
                with v.Fori(0, NG - 1) as g:
                    add_rows(l, g + 1, OUT_ATTN(g), 1)
                    norm_after(l, g + 1, 10 * l + 2 * g + 6, OUT_ATTN(g), to_n2)
                    out_transposed(T2(l, g + 1), to_h2, ln2)
                    add_rows(l, g, OUT_MLP(g), 0)
                    norm_after(l, g, 10 * l + 2 * g + 7, OUT_MLP(g), lambda j: row(KK, g, j))
                add_rows(l, NG - 1, OUT_LAST, 1)
                norm_after(l, NG - 1, 10 * l + 14, OUT_LAST, lambda j: row(KK, NG - 1, j))


def graph_attention(nc, s, XS, ident, x, xn_d, g, sums_d, scratch):
    key_d, dl_d, eat_d, ea_d, xl_d, al_d, pc_d, wl_d = (scratch[n] for n in ("key", "dl", "eat", "ea", "xl", "al", "pc", "wl"))
    with ExitStack() as keep:
        def kept(name, shape, dt=F32):
            return keep.enter_context(nc.sbuf_tensor(name, shape, dt))

        XL = kept("g_xl", [WN, NW, D])
        XRW = kept("g_xr", [128, NW, D])
        SRCX = kept("g_srcx", [TE, ITEMS], I32)
        DLX = kept("g_dlx", [TE, ITEMS])
        WI = kept("g_wi", [1, ITEMS], I32)
        attb = kept("g_attb", [128, D])

        with ExitStack() as c:
            XT = c.enter_context(nc.sbuf_tensor("p_xt", [128, KC, NW * WN], F32))
            wlr = c.enter_context(nc.sbuf_tensor("p_wlr", [128, KC, 2 * D], F32))
            brow = c.enter_context(nc.sbuf_tensor("p_brow", [1, 2 * D], F32))
            ones = c.enter_context(nc.sbuf_tensor("p_ones", [1, WN], F32))
            att = c.enter_context(nc.sbuf_tensor("p_att", [128, D], F32))
            st = c.enter_context(nc.sbuf_tensor("p_st", [P, GT, 6], F32))
            mv = c.enter_context(nc.sbuf_tensor("p_mv", [P, GT, 2], F32))
            ve = c.enter_context(nc.sbuf_tensor("p_ve", [P, GT], F32))
            rstd = c.enter_context(nc.sbuf_tensor("p_rstd", [P, GT], F32))
            mhalf = c.enter_context(nc.sbuf_tensor("p_mhalf", [P, GT], F32))
            pT = c.enter_context(nc.psum_tensor("p_pT", [128, 12, 128], F32))
            pP = c.enter_context(nc.psum_tensor("p_pP", [128, 4, 512], F32))
            block = c.enter_context(nc.Block())

            @block.sync
            def _(sp):
                sp.dma_start(XS[:, :, :], x.rearrange("(t p) d -> p t d", p=P)).then_inc(s["p_x"], 16)
                sp.dma_start(wlr[:, :, 0:D], chunked(g["W_lT"])).then_inc(s["p_w"], 16)
                sp.dma_start(wlr[:, :, D:], chunked(g["W_rT"])).then_inc(s["p_w"], 16)
                sp.dma_start(brow[0:1, 0:D], g["b_l"].unsqueeze(0)).then_inc(s["p_w"], 16)
                sp.dma_start(brow[0:1, D:], g["b_r"].unsqueeze(0)).then_inc(s["p_w"], 16)
                sp.dma_start(att[:, :], g["att"].rearrange("h d -> (h d)").unsqueeze(0).broadcast_to([128, D])).then_inc(s["p_att"], 16)
                sp.dma_start(XRW[WN:128, :, :], g["W_eT"].unsqueeze(1).broadcast_to([ED, NW, D])).then_inc(s["p_we"], 16)
                sp.wait_ge(s["p_ln_out"], NT)
                sp.dma_start(xn_d.rearrange("(t p) d -> p t d", p=P), XS[:, :, :]).then_inc(s["p_stored"], 16)
                sp.wait_ge(s["p_xl"], NW)
                sp.dma_start(xl_d.rearrange("(w p) d -> p w d", p=WN), XL[:, :, :]).then_inc(s["p_stored"], 16)
                sp.wait_ge(s["p_we"], 16)
                sp.wait_ge(s["p_stored"], 32)

            @block.gpsimd
            def _(p):
                p.memset(mhalf[:, :], -0.5).then_inc(s["p_const"], 1)
                p.memset(ones[:, :], 1.0).then_inc(s["p_const"], 1)
                p.memset(XT[:, :, N:], 0.0).then_inc(s["p_const"], 1)
                p.wait_ge(s["p_const"], 3)
                for n in range(NG):
                    rstd_side(p, s, "p_ln", n, ve, rstd, mhalf)

            @block.tensor
            def _(pe):
                for q in range(NG):
                    pe.wait_ge(s["p_ln_out"], GT * (q + 1))
                    if q:
                        pe.wait_ge(s["p_t_out"], q)
                    for k in range(KC):
                        for j in range(GT):
                            ins = pe.transpose(pT[:, GT * k + j, 0:P], XS[:, GT * q + j, k * 128:(k + 1) * 128], ident[0:P, 0:P])
                    ins.then_inc(s["p_t_full"], 1)
                pe.wait_ge(s["p_t_out"], NG)
                pe.wait_ge(s["p_w"], 64)
                pe.wait_ge(s["p_const"], 3)
                for w in range(NW):
                    if w >= 4:
                        pe.wait_ge(s["p_xl"], w - 3)
                        pe.wait_ge(s["p_xr"], w - 3)
                    for k in range(KC):
                        pe.matmul(pP[0:WN, w % 4, :], XT[:, k, w * WN:(w + 1) * WN], wlr[:, k, :], start=(k == 0), stop=False)
                    pe.matmul(pP[0:WN, w % 4, :], ones[0:1, :], brow[0:1, :], start=False, stop=True).then_inc(s["p_lr"], 1)

            @block.vector
            def _(v):
                v.wait_ge(s["p_x"], 16)
                for q in range(NG):
                    layer_norm(v, s, "p_ln", q, lambda j: XS[:, q * GT + j, :], lambda j: XS[:, q * GT + j, :], st, mv, ve, rstd)
                    v.wait_ge(s["p_t_full"], q + 1)
                    for k in range(KC):
                        ins = v.tensor_copy(XT[:, k, q * GN:(q + 1) * GN].rearrange("p (j n) -> p j n", j=GT), pT[:, GT * k:GT * k + GT, 0:P])
                    ins.then_inc(s["p_t_out"], 1)
                v.wait_ge(s["p_att"], 16)
                v.tensor_scalar(attb[:, :], att[:, :], SLOPE, None, ALU.mult).then_inc(s["p_attb"], 1)
                for w in range(NW):
                    v.wait_ge(s["p_lr"], w + 1)
                    v.tensor_copy(XL[:, w, :], pP[0:WN, w % 4, 0:D]).then_inc(s["p_xl"], 1)
                    v.tensor_copy(XRW[0:WN, w, :], pP[0:WN, w % 4, D:]).then_inc(s["p_xr"], 1)

        with ExitStack() as c:
            def sb(name, shape, dt=F32):
                return c.enter_context(nc.sbuf_tensor(name, shape, dt))

            ends_i = sb("i_ends_i", [NW, 2, NTE], I32)
            ends = sb("i_ends", [NW, 2, NTE])
            below = sb("i_below", [NW, 2, NTE])
            wbase = sb("i_wbase", [NW, 2])
            counts = sb("i_counts", [NW, 2])
            nitems = sb("i_nitems", [NW, 1])
            wide = sb("i_wide", [NW, 2, 128])
            one28 = sb("i_one28", [NW, 128])
            upto = sb("i_upto", [NW, NW])
            inum = sb("i_inum", [128, CH])
            lane = sb("i_lane", [128, NW])
            tab = sb("i_tab", [128, 3, NW])
            shift = sb("i_shift", [128, NW])
            cmp = sb("i_cmp", [128, CH, NW])
            wv = sb("i_wv", [128, CH])
            tile_f = sb("i_tile_f", [128, CH])
            tile_i = sb("i_tile_i", [128, CH], I32)
            base = sb("i_base", [128, CH])
            wc_i = sb("i_wc_i", [128, CH], I32)
            src_i = sb("i_src_i", [128, CH, TE], I32)
            dst_i = sb("i_dst_i", [128, CH, TE], I32)
            src_f = sb("i_src_f", [128, CH, TE])
            dst_f = sb("i_dst_f", [128, CH, TE])
            dl = sb("i_dl", [128, CH, TE])
            ok = sb("i_ok", [128, 2, CH, TE])
            eaT = sb("i_eaT", [128, 2, ED * TE])
            ea = sb("i_ea", [128, 2, ED * TE])
            edge = sb("i_edge", [1, 2])
            pN = c.enter_context(nc.psum_tensor("i_pN", [128, 512], F32))
            pX = c.enter_context(nc.psum_tensor("i_pX", [128, 2, 512], F32))
            block = c.enter_context(nc.Block())

            @block.sync
            def _(sp):
                sp.dma_start(ends_i[:, 0, :], g["dstT"][0:1, :].broadcast_to([NW, NTE])).then_inc(s["i_ends"], 16)
                sp.dma_start(ends_i[:, 1, :], g["dstT"][TE - 1:TE, :].broadcast_to([NW, NTE])).then_inc(s["i_ends"], 16)
                for k in range(CH):
                    sp.wait_ge(s[f"i_ea{k % 2}"], 32 * (k // 2 + 1))
                    sp.dma_start(eat_d[k * 128:(k + 1) * 128, :], eaT[:, k % 2, :]).then_inc(s[f"i_ea_out{k % 2}"], 16)
                    sp.dma_start(ea_d[k * 128:(k + 1) * 128, :], ea[:, k % 2, :]).then_inc(s[f"i_ea_out{k % 2}"], 16)
                sp.wait_ge(s["i_dl"], 1)
                sp.dma_start(dl_d.rearrange("(c p) e -> p c e", p=128), dl[:, :, :]).then_inc(s["i_stored"], 16)
                sp.wait_ge(s["i_key"], 1)
                sp.dma_start(key_d[1:1 + ITEMS * TE].rearrange("(c p e) -> p c e", p=128, e=TE), ok[:, 0, :, :]).then_inc(s["i_stored"], 16)
                sp.wait_ge(s["i_const"], 5)
                sp.dma_start(key_d[0:1].unsqueeze(0), edge[0:1, 0:1]).then_inc(s["i_stored"], 16)
                sp.dma_start(key_d[ITEMS * TE + 1:ITEMS * TE + 2].unsqueeze(0), edge[0:1, 1:2]).then_inc(s["i_stored"], 16)
                sp.wait_ge(s["i_wc"], 1)
                with nc.allow_non_contiguous_dma(reason="896 words"):
                    sp.dma_start(wl_d.rearrange("(c p) -> p c", p=128), wc_i[:, :]).then_inc(s["i_wl"], 16)
                sp.wait_ge(s["i_wl"], 16)
                sp.dma_start(WI[0:1, :], wl_d.unsqueeze(0)).then_inc(s["i_stored"], 16)
                sp.wait_ge(s["i_stored"], 16 * 5)
                sp.wait_ge(s["i_ea_out0"], 32 * 4)
                sp.wait_ge(s["i_ea_out1"], 32 * 3)

            @block.gpsimd
            def _(p):
                p.iota(wbase[:, :], pattern=[[WN, 2]], base=0, channel_multiplier=WN, allow_small_or_imprecise_dtypes=True).then_inc(s["i_const"], 1)
                p.iota(inum[:, :], pattern=[[128, CH]], base=0, channel_multiplier=1, allow_small_or_imprecise_dtypes=True).then_inc(s["i_const"], 1)
                p.iota(lane[:, :], pattern=[[1, NW]], base=0, channel_multiplier=0, allow_small_or_imprecise_dtypes=True).then_inc(s["i_const"], 1)
                p.memset(edge[:, :], -1.0).then_inc(s["i_const"], 1)
                p.memset(one28[:, :], 1.0).then_inc(s["i_const"], 1)
                p.wait_ge(s["i_const"], 5)
                p.affine_select(out=upto[:, :], in_=one28[:, 0:NW], compare_op=ALU.is_ge, fill=0.0, base=0,
                                pattern=[[1, NW]], channel_multiplier=-1).then_inc(s["i_upto"], 1)
                p.wait_ge(s["i_tile"], 1)
                for k in range(CH):
                    at = bass.IndirectOffsetOnAxis(ap=tile_i[:, k:k + 1], axis=0)
                    p.indirect_dma_start(out=dst_i[:, k, :], out_offset=None, in_=g["dst"], in_offset=at).then_inc(s["i_dst"], 16)
                    p.indirect_dma_start(out=src_i[:, k, :], out_offset=None, in_=g["src"], in_offset=at).then_inc(s["i_src"], 16)
                for k in range(CH):
                    at = bass.IndirectOffsetOnAxis(ap=tile_i[:, k:k + 1], axis=0)
                    if k >= 2:
                        p.wait_ge(s[f"i_ea_out{k % 2}"], 32 * (k // 2))
                    p.indirect_dma_start(out=eaT[:, k % 2, :], out_offset=None, in_=g["eaT"], in_offset=at).then_inc(s[f"i_ea{k % 2}"], 16)
                    p.indirect_dma_start(out=ea[:, k % 2, :], out_offset=None, in_=g["ea"], in_offset=at).then_inc(s[f"i_ea{k % 2}"], 16)

            @block.tensor
            def _(pe):
                pe.wait_ge(s["i_wide"], 2)
                pe.wait_ge(s["i_upto"], 1)
                pe.matmul(pN[:, 0:NW], wide[:, 0, :], upto[:, :], start=True, stop=True)
                pe.matmul(pN[:, NW:2 * NW], wide[:, 0, :], ident[0:NW, 0:NW], start=True, stop=True)
                pe.matmul(pN[:, 2 * NW:3 * NW], wide[:, 1, :], ident[0:NW, 0:NW], start=True, stop=True).then_inc(s["i_tab"], 1)
                for n, (ready, t) in enumerate([("i_src_f", src_f)] * CH + [("i_dl", dl)] * CH):
                    pe.wait_ge(s[ready], 1)
                    if n >= 2:
                        pe.wait_ge(s["i_x_out"], n - 1)
                    pe.transpose(pX[0:TE, n % 2, 0:128], t[:, n % CH, :], ident[:, :]).then_inc(s["i_x"], 1)

            @block.vector
            def _(v):
                chain = s["i_chain"]
                done = [0]

                def then(ins):
                    done[0] += 1
                    ins.then_inc(chain, 1)
                    v.wait_ge(chain, done[0])

                v.wait_ge(s["i_ends"], 32)
                v.wait_ge(s["i_const"], 5)
                then(v.tensor_copy(ends[:, :, :], ends_i[:, :, :]))
                v.tensor_scalar(below[:, 0, :], ends[:, 1, :], wbase[:, 0:1], None, ALU.is_lt)
                then(v.tensor_scalar(below[:, 1, :], ends[:, 0, :], wbase[:, 1:2], None, ALU.is_lt))
                then(v.tensor_reduce(counts[:, :], below[:, :, :], AX.X, ALU.add))
                then(v.tensor_tensor(nitems[:, :], counts[:, 1:2], counts[:, 0:1], ALU.subtract))
                v.tensor_scalar(wide[:, 0, :], one28[:, :], nitems[:, 0:1], None, ALU.mult).then_inc(s["i_wide"], 1)
                v.tensor_scalar(wide[:, 1, :], one28[:, :], counts[:, 0:1], None, ALU.mult).then_inc(s["i_wide"], 1)
                v.wait_ge(s["i_tab"], 1)
                then(v.tensor_copy(tab[:, :, :], pN[:, 0:3 * NW].rearrange("p (a w) -> p a w", a=3)))
                then(v.tensor_tensor(shift[:, :], tab[:, 2, :], tab[:, 0, :], ALU.subtract))
                then(v.tensor_tensor(shift[:, :], shift[:, :], tab[:, 1, :], ALU.add))
                over_w = lambda a: a.unsqueeze(1).broadcast_to([128, CH, NW])
                over_c = lambda a: a.unsqueeze(2).broadcast_to([128, CH, NW])
                then(v.tensor_tensor(cmp[:, :, :], over_w(tab[:, 0, :]), over_c(inum[:, :]), ALU.is_le))
                then(v.tensor_reduce(wv[:, :], cmp[:, :, :], AX.X, ALU.add))
                then(v.tensor_tensor(cmp[:, :, :], over_w(lane[:, :]), over_c(wv[:, :]), ALU.is_equal))
                then(v.tensor_tensor(cmp[:, :, :], cmp[:, :, :], over_w(shift[:, :]), ALU.mult))
                then(v.tensor_reduce(tile_f[:, :], cmp[:, :, :], AX.X, ALU.add))
                then(v.tensor_tensor(tile_f[:, :], tile_f[:, :], inum[:, :], ALU.add))
                then(v.tensor_scalar(tile_f[:, :], tile_f[:, :], float(NTE - 1), None, ALU.min))
                v.tensor_copy(tile_i[:, :], tile_f[:, :]).then_inc(s["i_tile"], 1)
                v.tensor_scalar(base[:, :], wv[:, :], float(WN), None, ALU.mult)
                v.tensor_scalar(wc_i[:, :], wv[:, :], float(NW - 1), None, ALU.min).then_inc(s["i_wc"], 1)
                v.wait_ge(s["i_src"], 16 * CH)
                v.wait_ge(s["i_dst"], 16 * CH)
                v.tensor_copy(src_f[:, :, :], src_i[:, :, :]).then_inc(s["i_src_f"], 1)
                then(v.tensor_copy(dst_f[:, :, :], dst_i[:, :, :]))
                then(v.tensor_tensor(dl[:, :, :], dst_f[:, :, :], base[:, :].unsqueeze(2).broadcast_to([128, CH, TE]), ALU.subtract))
                v.sem_inc(s["i_dl"], 1)
                v.tensor_scalar(ok[:, 0, :, :], dl[:, :, :], 0.0, None, ALU.is_ge)
                then(v.tensor_scalar(ok[:, 1, :, :], dl[:, :, :], float(WN), None, ALU.is_lt))
                then(v.tensor_tensor(ok[:, 0, :, :], ok[:, 0, :, :], ok[:, 1, :, :], ALU.mult))
                then(v.tensor_scalar(dst_f[:, :, :], dst_f[:, :, :], 1.0, None, ALU.add))
                v.tensor_tensor(ok[:, 0, :, :], ok[:, 0, :, :], dst_f[:, :, :], ALU.mult).then_inc(s["i_key"], 1)
                for n in range(2 * CH):
                    v.wait_ge(s["i_x"], n + 1)
                    to = SRCX if n < CH else DLX
                    k = n % CH
                    v.tensor_copy(to[:, k * 128:(k + 1) * 128], pX[0:TE, n % 2, 0:128]).then_inc(s["i_x_out"], 1)

        with ExitStack() as mid:
            PCX = mid.enter_context(nc.sbuf_tensor("g_pcx", [TE, ITEMS, 2 * GH], F32))

            with ExitStack() as c:
                def sb(name, shape, dt=F32):
                    return c.enter_context(nc.sbuf_tensor(name, shape, dt))

                LT = sb("a_lt", [128, 2, IG, TE])
                DB = sb("a_db", [WN, 2, IG, TE])
                G = sb("a_g", [TE, 2, IG, D])
                R = sb("a_r", [TE, 2, IG, D])
                IX = sb("a_ix", [TE, 2, IG], I32)
                AX_ = sb("a_alpha", [TE, ITEMS, GH])
                AT = sb("a_alphaT", [128, CH, GH, TE])
                node = sb("a_node", [128, 1])
                pS = c.enter_context(nc.psum_tensor("a_pS", [128, 2, IG * D], F32))
                pA = c.enter_context(nc.psum_tensor("a_pA", [128, 2, 512], F32))
                block = c.enter_context(nc.Block())

                @block.sync
                def _(sp):
                    with sp.Fori(0, STEPS) as i:
                        for h in range(2):
                            q = 2 * i + h
                            sp.wait_ge(s["a_scored"], q + 1)
                            at = bass.ds(q * IG, IG)
                            sp.dma_start(DB[:, h, :, :], dl_d[at, :].rearrange("i e -> (i e)").unsqueeze(0).broadcast_to([WN, IG * TE])
                                         .rearrange("p (i e) -> p i e", i=IG)).then_inc(s[f"a_db{h}"], 16)
                            sp.dma_start(LT[WN:128, h, :, :], eat_d[at, :].rearrange("i (c e) -> c i e", c=ED)).then_inc(s[f"a_eat{h}"], 16)
                    sp.wait_ge(s["a_at"], CH * GH)
                    sp.dma_start(al_d.rearrange("(c p) h e -> p c h e", p=128), AT[:, :, :, :]).then_inc(s["a_stored"], 16)
                    sp.wait_ge(s["a_stored"], 16)

                @block.gpsimd
                def _(p):
                    p.iota(node[:, :], pattern=[[0, 1]], base=0, channel_multiplier=1, allow_small_or_imprecise_dtypes=True).then_inc(s["a_const"], 1)
                    p.memset(AX_[:, STEPS * 2 * IG:, :], 0.0).then_inc(s["a_const"], 1)
                    with p.Fori(0, STEPS) as i:
                        for h in range(2):
                            q = 2 * i + h
                            p.wait_ge(s["a_scored"], q + 1)
                            p.sem_inc(s["a_seen"], 1)
                            p.tensor_copy(IX[:, h, :], SRCX[:, bass.ds(q * IG, IG)]).then_inc(s["a_ix"], 1)
                            p.wait_ge(s["a_ix"], q + 1)
                            p.sem_inc(s["a_seen"], 1)
                            for j in range(IG):
                                p.indirect_dma_start(out=G[:, h, j, :], out_offset=None, in_=xl_d,
                                                     in_offset=bass.IndirectOffsetOnAxis(ap=IX[:, h, j:j + 1], axis=0)).then_inc(s[f"a_g{h}"], 16)

                @block.tensor
                def _(pe):
                    with pe.Fori(0, STEPS) as i:
                        for h in range(2):
                            q = 2 * i + h
                            ws = [pe.value_load(WI[0:1, bass.ds(q * IG + j, 1)], min_val=0, max_val=NW - 1) for j in range(IG)]
                            pe.wait_ge(s["a_summed"], q + 1)
                            pe.wait_ge(s["a_onehot"], q + 1)
                            pe.wait_ge(s[f"a_eat{h}"], 16 * i + 16)
                            pe.wait_ge(s[f"a_g{h}"], 64 * i + 64)
                            for j in range(IG):
                                o = pS[0:TE, h, j * D:(j + 1) * D]
                                pe.matmul(o, LT[:, h, j, :], XRW[:, bass.ds(ws[j], 1), :].rearrange("p a d -> p (a d)"), start=True, stop=False)
                                ins = pe.matmul(o, ident[0:TE, 0:TE], G[:, h, j, :], start=False, stop=True)
                            ins.then_inc(s["a_scored"], 1)
                    pe.wait_ge(s["a_alpha"], 2 * STEPS + 2)
                    pe.wait_ge(s["a_const"], 2)
                    for k in range(CH):
                        for hd in range(GH):
                            n = k * GH + hd
                            if n >= 2:
                                pe.wait_ge(s["a_at"], n - 1)
                            pe.transpose(pA[:, n % 2, 0:TE], AX_[:, k * 128:(k + 1) * 128, hd], ident[0:TE, 0:TE]).then_inc(s["a_ta"], 1)

                @block.scalar
                def _(a):
                    with a.Fori(0, STEPS) as i:
                        for h in range(2):
                            q = 2 * i + h
                            a.wait_ge(s["a_scored"], q + 3)
                            a.wait_ge(s["a_alpha"], q + 1)
                            a.activation(R[:, h, :, :].rearrange("p i d -> p (i d)"), pS[0:TE, h, :], ACT.Relu).then_inc(s["a_relu"], 1)

                @block.vector
                def _(v):
                    for name, k in (("a_scored", 2), ("a_summed", 2), ("a_alpha", 2)):
                        v.sem_inc(s[name], k)
                    v.wait_ge(s["a_const"], 2)

                    def onehot(q, i, h):
                        v.wait_ge(s[f"a_db{h}"], 16 * i + 16)
                        v.tensor_scalar(LT[0:WN, h, :, :], DB[:, h, :, :], node[0:WN, 0:1], None, ALU.is_equal).then_inc(s["a_onehot"], 1)

                    def score(q, h):
                        r = R[:, h, :, :].rearrange("p i d -> p (i d)")
                        v.wait_ge(s["a_relu"], q + 1)
                        v.scalar_tensor_tensor(out=r, in0=r, scalar=1.0 / SLOPE - 1.0, in1=pS[0:TE, h, :], op0=ALU.mult, op1=ALU.add).then_inc(s["a_summed"], 1)
                        v.wait_ge(s["a_summed"], q + 3)
                        v.tensor_tensor(R[:, h, :, :], R[:, h, :, :], attb[0:TE, :].unsqueeze(1).broadcast_to([TE, IG, D]), ALU.mult).then_inc(s["a_times"], 1)
                        v.wait_ge(s["a_times"], q + 1)
                        v.sem_inc(s["a_seen_v"], 1)
                        v.tensor_reduce(AX_[:, bass.ds(q * IG, IG), :].rearrange("p i h -> p (i h)"),
                                        R[:, h, :, :].rearrange("p i (h d) -> p (i h) d", h=GH), AX.X, ALU.add).then_inc(s["a_alpha"], 1)

                    onehot(0, 0, 0)
                    with v.Fori(0, STEPS - 1) as i:
                        onehot(2 * i + 1, i, 1)
                        score(2 * i, 0)
                        onehot(2 * i + 2, i + 1, 0)
                        score(2 * i + 1, 1)
                    onehot(2 * STEPS - 1, STEPS - 1, 1)
                    score(2 * STEPS - 2, 0)
                    score(2 * STEPS - 1, 1)
                    for n in range(CH * GH):
                        v.wait_ge(s["a_ta"], n + 1)
                        v.tensor_copy(AT[:, n // GH, n % GH, :], pA[:, n % 2, 0:TE]).then_inc(s["a_at"], 1)

            with ExitStack() as c:
                def sb(name, shape, dt=F32):
                    return c.enter_context(nc.sbuf_tensor(name, shape, dt))

                A = sb("s_a", [128, GH, RUN])
                F = sb("s_f", [128, GH, RUN])
                B = sb("s_b", [128, GH, RUN])
                key = sb("s_key", [128, 3, RUN])
                edge = sb("s_edge", [128, 2, RUN])
                last = sb("s_last", [128, RUN])
                outside = sb("s_outside", [128, RUN])
                sums = sb("s_sums", [128, 4, GH])
                rows = sb("s_rows", [GH, 4, 128])
                state = sb("s_state", [GH, 2, 128])
                carry = sb("s_carry", [GH, 2, 128])
                init = sb("s_init", [128, 2, GH])
                PT = sb("s_pt", [128, 2, 2 * GH, TE])
                pR = c.enter_context(nc.psum_tensor("s_pR", [128, 4, 512], F32))
                pX = c.enter_context(nc.psum_tensor("s_pX", [128, 2, 512], F32))
                block = c.enter_context(nc.Block())

                @block.sync
                def _(sp):
                    for hd in range(GH):
                        sp.dma_start(A[:, hd, :].rearrange("p (k e) -> p k e", e=TE),
                                     al_d.rearrange("(p k) h e -> h p k e", p=128)[hd]).then_inc(s["s_in"], 16)
                    for n in range(3):
                        sp.dma_start(key[:, n, :], key_d[n:n + ITEMS * TE].rearrange("(p r) -> p r", p=128)).then_inc(s["s_in"], 16)
                    sp.wait_ge(s["s_p"], 1)
                    sp.wait_ge(s["s_cl"], 1)
                    view = pc_d.rearrange("(p k) c e -> c p k e", p=128)
                    for hd in range(GH):
                        sp.dma_start(view[hd], A[:, hd, :].rearrange("p (k e) -> p k e", e=TE)).then_inc(s["s_pc"], 16)
                        sp.dma_start(view[GH + hd], F[:, hd, :].rearrange("p (k e) -> p k e", e=TE)).then_inc(s["s_pc"], 16)
                    sp.wait_ge(s["s_pc"], 16 * 2 * GH)
                    for k in range(CH):
                        if k >= 2:
                            sp.wait_ge(s["s_x"], 2 * GH * (k - 1))
                        sp.dma_start(PT[:, k % 2, :, :], pc_d[k * 128:(k + 1) * 128, :, :]).then_inc(s[f"s_pt{k % 2}"], 16)

                @block.scalar
                def _(a):
                    a.wait_ge(s["s_diff"], 1)
                    a.activation(A[:, :, :], A[:, :, :], ACT.Exp).then_inc(s["s_p"], 1)

                @block.tensor
                def _(pe):
                    pe.wait_ge(s["s_sums"], 1)
                    for n in range(4):
                        ins = pe.transpose(pR[0:GH, n, 0:128], sums[:, n, :], ident[:, :])
                    ins.then_inc(s["s_rows"], 1)
                    pe.wait_ge(s["s_carry"], 1)
                    for n in range(2):
                        ins = pe.transpose(pR[:, n, 128:128 + GH], carry[:, n, :], ident[0:GH, 0:GH])
                    ins.then_inc(s["s_init"], 1)
                    for k in range(CH):
                        pe.wait_ge(s[f"s_pt{k % 2}"], 16 * (k // 2 + 1))
                        for q in range(2 * GH):
                            n = 2 * GH * k + q
                            if n >= 2:
                                pe.wait_ge(s["s_pcx"], n - 1)
                            pe.transpose(pX[0:TE, n % 2, 0:128], PT[:, k % 2, q, :], ident[:, :]).then_inc(s["s_x"], 1)

                @block.vector
                def _(v):
                    done = [0]

                    def then(ins):
                        done[0] += 1
                        ins.then_inc(s["s_chain"], 1)
                        v.wait_ge(s["s_chain"], done[0])

                    v.wait_ge(s["s_in"], 16 * (GH + 3))
                    v.tensor_tensor(edge[:, 0, :], key[:, 1, :], key[:, 0, :], ALU.not_equal)
                    v.tensor_tensor(last[:, :], key[:, 1, :], key[:, 2, :], ALU.not_equal)
                    then(v.tensor_scalar(outside[:, :], key[:, 1, :], 0.0, LOW, ALU.is_equal, ALU.mult))
                    v.tensor_scalar(edge[:, 0, :], edge[:, 0, :], LOW, None, ALU.mult)
                    v.tensor_scalar(edge[:, 1, :], last[:, :], LOW, None, ALU.mult)
                    then(v.tensor_tensor(A[:, :, :], A[:, :, :], outside[:, :].unsqueeze(1).broadcast_to([128, GH, RUN]), ALU.add))

                    def scans(initial):
                        for hd in range(GH):
                            v.tensor_tensor_scan(F[:, hd, :], edge[:, 0, :], A[:, hd, :], initial(0, hd), ALU.add, ALU.max)
                            ins = v.tensor_tensor_scan(B[:, hd, ::-1], edge[:, 1, ::-1], A[:, hd, ::-1], initial(1, hd), ALU.add, ALU.max)
                        then(ins)

                    scans(lambda n, hd: LOW)
                    v.tensor_copy(sums[:, 0, :], F[:, :, RUN - 1])
                    v.tensor_copy(sums[:, 1, :], B[:, :, 0])
                    v.tensor_reduce(sums[:, 2, 0:1], edge[:, 0, :], AX.X, ALU.min)
                    then(v.tensor_reduce(sums[:, 3, 0:1], edge[:, 1, :], AX.X, ALU.min))
                    for n in (2, 3):
                        ins = v.tensor_copy(sums[:, n, 1:GH], sums[:, n, 0:1].broadcast_to([128, GH - 1]))
                    ins.then_inc(s["s_sums"], 1)
                    v.wait_ge(s["s_rows"], 1)
                    then(v.tensor_copy(rows[:, :, :], pR[0:GH, :, 0:128]))
                    v.tensor_tensor_scan(state[:, 0, :], rows[:, 2, :], rows[:, 0, :], LOW, ALU.add, ALU.max)
                    v.tensor_tensor_scan(state[:, 1, ::-1], rows[:, 3, ::-1], rows[:, 1, ::-1], LOW, ALU.add, ALU.max)
                    then(v.memset(carry[:, :, :], LOW))
                    v.tensor_copy(carry[:, 0, 1:128], state[:, 0, 0:127])
                    v.tensor_copy(carry[:, 1, 0:127], state[:, 1, 1:128]).then_inc(s["s_carry"], 1)
                    v.wait_ge(s["s_init"], 1)
                    then(v.tensor_copy(init[:, :, :], pR[:, 0:2, 128:128 + GH]))
                    scans(lambda n, hd: init[:, n, hd:hd + 1])
                    then(v.tensor_tensor(F[:, :, :], F[:, :, :], B[:, :, :], ALU.max))
                    v.tensor_tensor(A[:, :, :], A[:, :, :], F[:, :, :], ALU.subtract).then_inc(s["s_diff"], 1)
                    v.wait_ge(s["s_diff"], 1)
                    v.tensor_tensor(F[:, :, :], F[:, :, :], last[:, :].unsqueeze(1).broadcast_to([128, GH, RUN]), ALU.mult).then_inc(s["s_cl"], 1)
                    for n in range(2 * GH * CH):
                        k, q = n // (2 * GH), n % (2 * GH)
                        v.wait_ge(s["s_x"], n + 1)
                        v.tensor_copy(PCX[:, k * 128:(k + 1) * 128, q], pX[0:TE, n % 2, 0:128]).then_inc(s["s_pcx"], 1)

            with ExitStack() as c:
                def sb(name, shape, dt=F32):
                    return c.enter_context(nc.sbuf_tensor(name, shape, dt))

                ACC = sb("b_acc", [WN, NW, MW])

                with ExitStack() as d:
                    G = d.enter_context(nc.sbuf_tensor("b_g", [TE, 2, IG, D], F32))
                    M = d.enter_context(nc.sbuf_tensor("b_m", [TE, 2, IG, MW], F32))
                    OH = d.enter_context(nc.sbuf_tensor("b_oh", [TE, 2, IG, WN], F32))
                    IX = d.enter_context(nc.sbuf_tensor("b_ix", [TE, 2, IG], I32))
                    node = d.enter_context(nc.sbuf_tensor("b_node", [TE, WN], F32))
                    pM = d.enter_context(nc.psum_tensor("b_pM", [128, 2, IG, 512], F32))
                    block = d.enter_context(nc.Block())

                    @block.sync
                    def _(sp):
                        sp.wait_ge(s["b_const"], 3)
                        with sp.Fori(0, STEPS) as i:
                            for h in range(2):
                                q = 2 * i + h
                                sp.wait_ge(s["b_summed"], q + 1)
                                sp.dma_start(M[:, h, :, EA0:EA0 + ED],
                                             ea_d[bass.ds(q * IG, IG), :].rearrange("i (e c) -> e i c", c=ED)).then_inc(s[f"b_ea{h}"], 16)

                    @block.gpsimd
                    def _(p):
                        p.iota(node[:, :], pattern=[[1, WN]], base=0, channel_multiplier=0, allow_small_or_imprecise_dtypes=True).then_inc(s["b_const"], 1)
                        p.memset(M[:, :, :, :], 1.0).then_inc(s["b_const"], 1)
                        p.memset(ACC[:, :, :], 0.0).then_inc(s["b_const"], 1)
                        with p.Fori(0, STEPS) as i:
                            for h in range(2):
                                q = 2 * i + h
                                p.wait_ge(s["b_weighted"], q + 1)
                                p.sem_inc(s["b_seen"], 1)
                                p.tensor_copy(IX[:, h, :], SRCX[:, bass.ds(q * IG, IG)]).then_inc(s["b_ix"], 1)
                                p.wait_ge(s["b_ix"], q + 1)
                                p.sem_inc(s["b_seen"], 1)
                                for j in range(IG):
                                    p.indirect_dma_start(out=G[:, h, j, :], out_offset=None, in_=xl_d,
                                                         in_offset=bass.IndirectOffsetOnAxis(ap=IX[:, h, j:j + 1], axis=0)).then_inc(s[f"b_g{h}"], 16)

                    @block.tensor
                    def _(pe):
                        with pe.Fori(0, STEPS) as i:
                            for h in range(2):
                                q = 2 * i + h
                                pe.wait_ge(s["b_weighted"], q + 3)
                                pe.wait_ge(s["b_acc"], IG * q + 1)
                                pe.wait_ge(s[f"b_ea{h}"], 16 * i + 16)
                                for j in range(IG):
                                    ins = pe.matmul(pM[0:WN, h, j, 0:MW], OH[:, h, j, :], M[:, h, j, :], start=True, stop=True)
                                ins.then_inc(s["b_summed"], 1)

                    @block.vector
                    def _(v):
                        for name, k in (("b_weighted", 2), ("b_summed", 2), ("b_acc", 2 * IG)):
                            v.sem_inc(s[name], k)
                        v.wait_ge(s["b_const"], 3)

                        def weigh(q, i, h):
                            v.wait_ge(s["b_summed"], q + 1)
                            v.sem_inc(s["b_seen_v"], 1)
                            at = bass.ds(q * IG, IG) if not isinstance(q, int) else slice(q * IG, q * IG + IG)
                            v.tensor_tensor(OH[:, h, :, :], node[:, :].unsqueeze(1).broadcast_to([TE, IG, WN]),
                                            DLX[:, at].unsqueeze(2).broadcast_to([TE, IG, WN]), ALU.is_equal)
                            v.tensor_copy(M[:, h, :, D:D + 2 * GH], PCX[:, at, :])
                            v.wait_ge(s[f"b_g{h}"], 64 * i + 64)
                            for j in range(IG):
                                one = bass.ds(q * IG + j, 1) if not isinstance(q, int) else slice(q * IG + j, q * IG + j + 1)
                                ins = v.tensor_tensor(M[:, h, j, 0:D].rearrange("p (h d) -> p h d", h=GH), G[:, h, j, :].rearrange("p (h d) -> p h d", h=GH),
                                                      PCX[:, one, 0:GH].rearrange("p a h -> p (a h)").unsqueeze(2).broadcast_to([TE, GH, D // GH]), ALU.mult)
                            ins.then_inc(s["b_weighted"], 1)

                        def add(q, h):
                            for j in range(IG):
                                w = v.value_load(WI[0:1, (bass.ds(q * IG + j, 1) if not isinstance(q, int) else slice(q * IG + j, q * IG + j + 1))], min_val=0, max_val=NW - 1)
                                a = ACC[:, bass.ds(w, 1), :].rearrange("p a m -> p (a m)")
                                v.wait_ge(s["b_summed"], q + 3)
                                v.wait_ge(s["b_acc"], IG * q + j + 2 * IG)
                                v.tensor_tensor(a, a, pM[0:WN, h, j, 0:MW], ALU.add).then_inc(s["b_acc"], 1)

                        weigh(0, 0, 0)
                        with v.Fori(0, STEPS - 1) as i:
                            weigh(2 * i + 1, i, 1)
                            add(2 * i, 0)
                            weigh(2 * i + 2, i + 1, 0)
                            add(2 * i + 1, 1)
                        weigh(2 * STEPS - 1, STEPS - 1, 1)
                        add(2 * STEPS - 2, 0)
                        add(2 * STEPS - 1, 1)

                deg1 = sb("e_deg1", [WN, NW])
                la = sb("e_la", [WN, NW, ED])
                laT = sb("e_laT", [ED, 2, WN])
                weT = sb("e_weT", [ED, D])
                S = sb("e_s", [WN, NW, D])
                T = XRW[0:WN, :, :]
                own = sb("e_own", [WN, NW, GH])
                none = sb("e_none", [WN, NW])
                cmax = sb("e_cmax", [WN, NW, GH])
                m = sb("e_m", [WN, NW, GH])
                e12 = sb("e_e12", [WN, 2, NW, GH])
                den = sb("e_den", [WN, NW, GH])
                bias = sb("e_bias", [WN, D])
                pL = c.enter_context(nc.psum_tensor("e_pL", [128, 2, 512], F32))
                pE = c.enter_context(nc.psum_tensor("e_pE", [128, 2, 512], F32))
                block = c.enter_context(nc.Block())

                @block.sync
                def _(sp):
                    sp.dma_start(weT[:, :], g["W_eT"]).then_inc(s["e_w"], 16)
                    sp.dma_start(bias[:, :], g["bias"].unsqueeze(0).broadcast_to([WN, D])).then_inc(s["e_w"], 16)
                    sp.wait_ge(s["e_silu"], 1)
                    sp.dma_start(sums_d.rearrange("(w p) d -> p w d", p=WN), S[:, :, :]).then_inc(s["e_stored"], 16)
                    sp.wait_ge(s["e_stored"], 16)

                @block.tensor
                def _(pe):
                    pe.wait_ge(s["e_la"], 1)
                    pe.wait_ge(s["e_w"], 32)
                    for w in range(NW):
                        if w >= 2:
                            pe.wait_ge(s["e_laT"], w - 1)
                        pe.transpose(pL[0:ED, w % 2, 0:WN], la[:, w, :], ident[0:WN, 0:WN]).then_inc(s["e_lt"], 1)
                        pe.wait_ge(s["e_laT"], w + 1)
                        if w >= 2:
                            pe.wait_ge(s["e_sum"], w - 1)
                        pe.matmul(pE[0:WN, w % 2, 0:D], laT[:, w % 2, :], weT[:, :], start=True, stop=True).then_inc(s["e_feat"], 1)

                @block.scalar
                def _(a):
                    a.wait_ge(s["e_less"], 1)
                    a.activation(e12[:, :, :, :], e12[:, :, :, :], ACT.Exp).then_inc(s["e_exp"], 1)
                    a.wait_ge(s["e_out"], 1)
                    a.activation(S[:, :, :], S[:, :, :], ACT.Silu).then_inc(s["e_silu"], 1)

                @block.vector
                def _(v):
                    done = [0]

                    def then(ins):
                        done[0] += 1
                        ins.then_inc(s["e_chain"], 1)
                        v.wait_ge(s["e_chain"], done[0])

                    heads = lambda a: a.rearrange("p w (h d) -> p (w h) d", h=GH)
                    spread = lambda a, n: a.rearrange("p w h -> p (w h)").unsqueeze(2).broadcast_to([WN, NW * GH, n])
                    deg = ACC[:, :, EA0 + ED]
                    v.tensor_scalar(none[:, :], deg, 0.0, LOW, ALU.is_equal, ALU.mult)
                    then(v.tensor_scalar(deg1[:, :], deg, 1.0, None, ALU.max))
                    then(v.reciprocal(deg1[:, :], deg1[:, :]))
                    v.tensor_tensor(la[:, :, :], ACC[:, :, EA0:EA0 + ED], deg1[:, :].unsqueeze(2).broadcast_to([WN, NW, ED]), ALU.mult).then_inc(s["e_la"], 1)
                    v.tensor_tensor(cmax[:, :, :], ACC[:, :, D + GH:D + 2 * GH], none[:, :].unsqueeze(2).broadcast_to([WN, NW, GH]), ALU.add)
                    for w in range(NW):
                        v.wait_ge(s["e_lt"], w + 1)
                        v.tensor_copy(laT[:, w % 2, :], pL[0:ED, w % 2, 0:WN]).then_inc(s["e_laT"], 1)
                        v.wait_ge(s["e_feat"], w + 1)
                        v.tensor_tensor(S[:, w, :], pE[0:WN, w % 2, 0:D], XL[:, w, :], ALU.add).then_inc(s["e_sum"], 1)
                    v.wait_ge(s["e_sum"], NW)
                    then(v.tensor_tensor(S[:, :, :], S[:, :, :], XRW[0:WN, :, :], ALU.add))
                    then(v.scalar_tensor_tensor(out=S[:, :, :], in0=S[:, :, :], scalar=SLOPE, in1=S[:, :, :], op0=ALU.mult, op1=ALU.max))
                    then(v.tensor_scalar(S[:, :, :], S[:, :, :], 1.0 / SLOPE, None, ALU.mult))
                    then(v.tensor_tensor(S[:, :, :], S[:, :, :], attb[0:WN, :].unsqueeze(1).broadcast_to([WN, NW, D]), ALU.mult))
                    then(v.tensor_reduce(own[:, :, :].rearrange("p w h -> p (w h)"), heads(S[:, :, :]), AX.X, ALU.add))
                    then(v.tensor_tensor(m[:, :, :], cmax[:, :, :], own[:, :, :], ALU.max))
                    v.tensor_tensor(e12[:, 0, :, :], cmax[:, :, :], m[:, :, :], ALU.subtract)
                    v.tensor_tensor(e12[:, 1, :, :], own[:, :, :], m[:, :, :], ALU.subtract).then_inc(s["e_less"], 1)
                    v.wait_ge(s["e_exp"], 1)
                    then(v.tensor_tensor(den[:, :, :], ACC[:, :, D:D + GH], e12[:, 0, :, :], ALU.mult))
                    then(v.tensor_tensor(den[:, :, :], den[:, :, :], e12[:, 1, :, :], ALU.add))
                    then(v.tensor_scalar(den[:, :, :], den[:, :, :], 1e-16, None, ALU.add))
                    then(v.reciprocal(den[:, :, :], den[:, :, :]))
                    v.tensor_tensor(e12[:, 0, :, :], e12[:, 0, :, :], den[:, :, :], ALU.mult)
                    then(v.tensor_tensor(e12[:, 1, :, :], e12[:, 1, :, :], den[:, :, :], ALU.mult))
                    for w in range(NW):
                        hd = lambda a: a.rearrange("p (h d) -> p h d", h=GH)
                        by = lambda n: e12[:, n, w, :].unsqueeze(2).broadcast_to([WN, GH, D // GH])
                        v.tensor_tensor(hd(S[:, w, :]), hd(ACC[:, w, 0:D]), by(0), ALU.mult)
                        ins = v.tensor_tensor(hd(T[:, w, :]), hd(XL[:, w, :]), by(1), ALU.mult)
                    then(ins)
                    then(v.tensor_tensor(S[:, :, :], S[:, :, :], T[:, :, :], ALU.add))
                    v.wait_ge(s["e_w"], 32)
                    v.tensor_tensor(S[:, :, :], S[:, :, :], bias[:, :].unsqueeze(1).broadcast_to([WN, NW, D]), ALU.add).then_inc(s["e_out"], 1)


def experts(nc, s, XS, ident, w, out):
    with ExitStack() as c:
        def sb(name, shape, dt=F32):
            return c.enter_context(nc.sbuf_tensor(name, shape, dt))

        def ps(name, shape):
            return c.enter_context(nc.psum_tensor(name, shape, F32))

        HT = sb("f_ht", [128, KC, N])
        NR = sb("f_nr", [P, GT, D])
        HID = sb("f_hid", [128, 2, FC, GN])
        w1 = sb("f_w1", [128, 2, KC, FF])
        w2 = sb("f_w2", [128, 2, FC, D])
        b1 = sb("f_b1", [128, 2, FC])
        b2 = sb("f_b2", [1, 2, D])
        wr = sb("f_wr", [128, KC, EXPERTS])
        ones = sb("f_ones", [1, P])
        st = sb("f_st", [P, GT, 6])
        mv = sb("f_mv", [P, GT, 2])
        ve = sb("f_ve", [P, GT])
        rstd = sb("f_rstd", [P, GT])
        mhalf = sb("f_mhalf", [P, GT])
        lane = sb("f_lane", [P, EXPERTS])
        rw = sb("f_rw", [P, NT, EXPERTS])
        rmax = sb("f_rmax", [P, NT])
        rsum = sb("f_rsum", [P, NT])
        rrec = sb("f_rrec", [P, NT])
        top = sb("f_top", [P, NT, 8])
        topi = sb("f_topi", [P, NT, 8], U32)
        topf = sb("f_topf", [P, NT, 8])
        pick = sb("f_pick", [P, 2, NT, EXPERTS])
        gate = sb("f_gate", [P, NT, 1 + EXPERTS])
        pH = ps("f_pH", [128, 4, 512])
        pO = ps("f_pO", [128, 2, 512])

        block = c.enter_context(nc.Block())
        GROUPS = NG * (1 + EXPERTS)

        def steps(eng, one):
            for g in range(NG):
                one(g, 0, 0, g, g % 2)
            with eng.Fori(0, EXPERTS // 2) as i:
                for q in range(2 * NG):
                    one(2 * NG * i + NG + q, 2 * i + 1 + q // NG, (1 + q // NG) % 2, q % NG, (NG + q) % 2)

        @block.sync
        def _(sp):
            def load(e, slot, W1, B1, W2, B2, wait):
                if wait:
                    sp.wait_ge(s["f_rows"], GT * NG * (e - 1))
                sp.dma_start(w1[:, slot, :, :], chunked(W1)).then_inc(s[f"f_w{slot}"], 16)
                sp.dma_start(w2[:, slot, :, :], chunked(W2)).then_inc(s[f"f_w{slot}"], 16)
                sp.dma_start(b1[:, slot, :], B1).then_inc(s[f"f_w{slot}"], 16)
                sp.dma_start(b2[0:1, slot, :], B2.unsqueeze(0)).then_inc(s[f"f_w{slot}"], 16)

            def load_private(e, slot, at, wait):
                load(e, slot, *(picked(w[x], at) for x in ("W1p", "b1p", "W2p", "b2p")), wait)

            sp.dma_start(wr[:, :, :], chunked(w["Wr"])).then_inc(s["f_small"], 16)
            load(0, 0, w["W1s"], w["b1s"], w["W2s"], w["b2s"], False)
            load_private(1, 1, 0, False)
            load_private(2, 0, 1, True)
            with sp.Fori(1, EXPERTS // 2) as i:
                load_private(2 * i + 1, 1, 2 * i, True)
                load_private(2 * i + 2, 0, 2 * i + 1, True)
            rows = out.rearrange("(t p) d -> p t d", p=P)
            for g in range(NG):
                sp.wait_ge(s["f_added"], GT * (GROUPS - NG + g + 1) + 2)
                sp.dma_start(rows[:, g * GT:(g + 1) * GT, :], XS[:, g * GT:(g + 1) * GT, :]).then_inc(s["f_stored"], 16)
            sp.wait_ge(s["f_stored"], 16 * NG)

        @block.gpsimd
        def _(p):
            p.memset(mhalf[:, :], -0.5).then_inc(s["f_const"], 1)
            p.memset(ones[:, :], 1.0).then_inc(s["f_const"], 1)
            p.memset(gate[:, :, 0:1], 1.0).then_inc(s["f_const"], 1)
            p.iota(lane[:, :], pattern=[[1, EXPERTS]], base=0, channel_multiplier=0,
                   allow_small_or_imprecise_dtypes=True).then_inc(s["f_const"], 1)
            p.wait_ge(s["f_const"], 4)
            with p.Fori(0, NG) as n:
                rstd_side(p, s, "f_ln", n, ve, rstd, mhalf)

        @block.tensor
        def _(pe):
            pT = pH[:, 0:3, :].rearrange("p b (j q) -> p (b j) q", q=128)
            for g in range(NG):
                pe.wait_ge(s["f_ln_out"], GT * (g + 1))
                if g:
                    pe.wait_ge(s["f_t_out"], g)
                for k in range(KC):
                    for j in range(GT):
                        ins = pe.transpose(pT[:, GT * k + j, 0:P], NR[:, j, k * 128:(k + 1) * 128], ident[0:P, 0:P])
                ins.then_inc(s["f_t_full"], 1)
            pe.wait_ge(s["f_t_out"], NG)
            pe.wait_ge(s["f_small"], 16)
            pe.wait_ge(s["f_const"], 4)
            for t in range(NT):
                for k in range(KC):
                    ins = pe.matmul(pH[0:P, 3, t * EXPERTS:(t + 1) * EXPERTS], HT[:, k, t * P:(t + 1) * P], wr[:, k, :],
                                    start=(k == 0), stop=(k == KC - 1))
            ins.then_inc(s["f_logits"], 1)
            pe.wait_ge(s["f_lmax"], 1)
            pe.wait_ge(s["f_lsub"], 1)

            def hidden(G, e, slot, g, hid):
                if g == 0:
                    pe.wait_ge(s[f"f_w{slot}"], 32 * (e - slot) + 64)
                for f in range(FC):
                    b = 2 * (f % 2)
                    pe.wait_ge(s["f_gelu"], FC * G + f + 1)
                    for h, (at, n) in enumerate(HALVES):
                        for k in range(KC):
                            ins = pe.matmul(pH[:, b + h, 0:n], w1[:, slot, k, f * 128:(f + 1) * 128],
                                            HT[:, k, g * GN + at:g * GN + at + n], start=(k == 0), stop=(k == KC - 1))
                    ins.then_inc(s["f_hid"], 1)

            def rows(G, e, slot, g, hid):
                pe.wait_ge(s["f_gelu"], FC * G + FC + 2)
                for j in range(GT):
                    o = pO[0:P, (hid + j) % 2, 0:D]
                    pe.wait_ge(s["f_added"], GT * G + j + 1)
                    for f in range(FC):
                        pe.matmul(o, HID[:, hid, f, j * P:(j + 1) * P], w2[:, slot, f, :], start=(f == 0), stop=False)
                    pe.matmul(o, ones[0:1, 0:P], b2[0:1, slot, :], start=False, stop=True).then_inc(s["f_rows"], 1)

            hidden(0, 0, 0, 0, 0)
            for g in range(NG - 1):
                hidden(g + 1, 0, 0, g + 1, (g + 1) % 2)
                rows(g, 0, 0, g, g % 2)
            with pe.Fori(0, EXPERTS // 2) as i:
                for q in range(2 * NG):
                    hidden(2 * NG * i + NG + q, 2 * i + 1 + q // NG, (1 + q // NG) % 2, q % NG, (NG + q) % 2)
                    r = q - 1 + NG
                    rows(2 * NG * i + r, 2 * i + r // NG, (r // NG) % 2, r % NG, r % 2)
            rows(GROUPS - 1, EXPERTS, 0, NG - 1, (GROUPS - 1) % 2)

        @block.scalar
        def _(a):
            a.wait_ge(s["f_lsub"], 1)
            a.activation(rw[:, :, :], rw[:, :, :], ACT.Exp).then_inc(s["f_rexp"], 1)

            def gelus(G, e, slot, g, hid):
                if g == 0:
                    a.wait_ge(s[f"f_w{slot}"], 32 * (e - slot) + 64)
                for f in range(FC):
                    b = 2 * (f % 2)
                    a.wait_ge(s["f_hid"], FC * G + f + 1)
                    if f == 0 and not (isinstance(G, int) and G < 2):
                        a.wait_ge(s["f_rows"], GT * G - GT)
                    for h, (at, n) in enumerate(HALVES):
                        ins = a.activation(HID[:, hid, f, at:at + n], pH[:, b + h, 0:n], ACT.Gelu, bias=b1[:, slot, f:f + 1])
                    ins.then_inc(s["f_gelu"], 1)

            steps(a, gelus)

        @block.vector
        def _(v):
            v.sem_inc(s["f_gelu"], 2)
            v.sem_inc(s["f_added"], 2)
            for g in range(NG):
                if g:
                    v.wait_ge(s["f_t_full"], g)
                layer_norm(v, s, "f_ln", g, lambda j: XS[:, g * GT + j, :], lambda j: NR[:, j, :], st, mv, ve, rstd)
                v.wait_ge(s["f_t_full"], g + 1)
                for k in range(KC):
                    pT = pH[:, 0:3, :].rearrange("p b (j q) -> p (b j) q", q=128)
                    ins = v.tensor_copy(HT[:, k, g * GN:(g + 1) * GN].rearrange("p (j q) -> p j q", j=GT),
                                        pT[:, GT * k:GT * k + GT, 0:P])
                ins.then_inc(s["f_t_out"], 1)

            def spread(x):
                return x.unsqueeze(2).broadcast_to([P, NT, EXPERTS])

            v.wait_ge(s["f_logits"], 1)
            logits = pH[0:P, 3, 0:NT * EXPERTS].rearrange("p (t e) -> p t e", t=NT)
            v.tensor_reduce(rmax[:, :], logits, AX.X, ALU.max).then_inc(s["f_lmax"], 1)
            v.wait_ge(s["f_lmax"], 1)
            v.tensor_tensor(rw[:, :, :], logits, spread(rmax[:, :]), ALU.subtract).then_inc(s["f_lsub"], 1)
            v.wait_ge(s["f_rexp"], 1)
            v.tensor_reduce(rsum[:, :], rw[:, :, :], AX.X, ALU.add).then_inc(s["f_rsum"], 1)
            v.wait_ge(s["f_rsum"], 1)
            v.reciprocal(rrec[:, :], rsum[:, :]).then_inc(s["f_rrec"], 1)
            v.wait_ge(s["f_rrec"], 1)
            v.tensor_tensor(rw[:, :, :], rw[:, :, :], spread(rrec[:, :]), ALU.mult).then_inc(s["f_softmax"], 1)
            v.wait_ge(s["f_softmax"], 1)
            for t in range(NT):
                v.max(top[:, t, :], rw[:, t, :]).then_inc(s["f_top"], 1)
            v.wait_ge(s["f_top"], NT)
            for t in range(NT):
                v.max_index(topi[:, t, :], top[:, t, :], rw[:, t, :]).then_inc(s["f_topi"], 1)
            v.wait_ge(s["f_topi"], NT)
            v.tensor_copy(topf[:, :, :], topi[:, :, :]).then_inc(s["f_topf"], 1)
            v.tensor_tensor(rsum[:, :], top[:, :, 0], top[:, :, 1], ALU.add).then_inc(s["f_rsum"], 1)
            v.wait_ge(s["f_topf"], 1)
            v.wait_ge(s["f_rsum"], 2)
            v.reciprocal(rrec[:, :], rsum[:, :]).then_inc(s["f_rrec"], 1)
            v.wait_ge(s["f_const"], 4)
            lanes = lane[:, :].unsqueeze(1).broadcast_to([P, NT, EXPERTS])
            for n in range(2):
                v.tensor_tensor(pick[:, n, :, :], lanes, spread(topf[:, :, n]), ALU.is_equal).then_inc(s["f_pick"], 1)
            v.wait_ge(s["f_pick"], 2)
            for n in range(2):
                v.tensor_tensor(pick[:, n, :, :], pick[:, n, :, :], spread(top[:, :, n]), ALU.mult).then_inc(s["f_pick"], 1)
            v.wait_ge(s["f_pick"], 4)
            v.tensor_tensor(pick[:, 0, :, :], pick[:, 0, :, :], pick[:, 1, :, :], ALU.add).then_inc(s["f_pick"], 1)
            v.wait_ge(s["f_pick"], 5)
            v.wait_ge(s["f_rrec"], 2)
            v.tensor_tensor(gate[:, :, 1:], pick[:, 0, :, :], spread(rrec[:, :]), ALU.mult).then_inc(s["f_gate"], 1)
            v.wait_ge(s["f_gate"], 1)

            def add(G, e, slot, g, hid):
                for j in range(GT):
                    t = g * GT + j
                    by = gate[:, t, e:e + 1] if isinstance(e, int) else gate[:, t, bass.ds(e, 1)]
                    v.wait_ge(s["f_rows"], GT * G + j + 1)
                    v.scalar_tensor_tensor(out=XS[:, t, :], in0=pO[0:P, (hid + j) % 2, 0:D], scalar=by, in1=XS[:, t, :],
                                           op0=ALU.mult, op1=ALU.add).then_inc(s["f_added"], 1)

            steps(v, add)


def add_branches(nc, s, XS, x, xn_d, sums_d):
    with ExitStack() as c:
        parts = [c.enter_context(nc.sbuf_tensor(f"c_{n}", [P, NT, D], F32)) for n in ("x", "xn", "g")]
        block = c.enter_context(nc.Block())

        @block.sync
        def _(sp):
            for n, a in enumerate((x, xn_d, sums_d[0:N, :])):
                sp.dma_start(parts[n][:, :, :], a.rearrange("(t p) d -> p t d", p=P)).then_inc(s[f"c_part{n}"], 16)

        @block.vector
        def _(v):
            for n in range(3):
                v.wait_ge(s[f"c_part{n}"], 16)
                if n:
                    v.wait_ge(s["c_added"], n)
                v.tensor_tensor(XS[:, :, :], XS[:, :, :], parts[n][:, :, :], ALU.add).then_inc(s["c_added"], 1)


def gps_layer(nc, a, out):
    with ExitStack() as c:
        XS = c.enter_context(nc.sbuf_tensor("XS", [P, NT, D], F32))
        ident = c.enter_context(nc.sbuf_tensor("ident", [128, 128], F32))
        dram = lambda n, shape, dt=F32: nc.dram_tensor(n, shape, dt).ap()
        xn_d = dram("xn_d", (N, D))
        sums_d = dram("sums_d", (NW * WN, D))
        scratch = {"key": dram("key_d", (ITEMS * TE + 2,)), "dl": dram("dl_d", (ITEMS, TE)),
                   "eat": dram("eat_d", (ITEMS, ED * TE)), "ea": dram("ea_d", (ITEMS, ED * TE)),
                   "xl": dram("xl_d", (NW * WN, D)), "al": dram("al_d", (ITEMS, GH, TE)),
                   "pc": dram("pc_d", (ITEMS, 2 * GH, TE)), "wl": dram("wl_d", (ITEMS,), I32)}
        s = Names(nc)
        with nc.Block() as block:
            @block.gpsimd
            def _(p):
                p.memset(ident[:, :], 0.0).then_inc(s["const"], 1)
                p.wait_ge(s["const"], 1)
                p.affine_select(out=ident[:, :], in_=ident[:, :], compare_op=ALU.not_equal, fill=1.0, base=0,
                                pattern=[[-1, 128]], channel_multiplier=1).then_inc(s["const"], 1)
                p.wait_ge(s["const"], 2)
        part = lambda prefix: {n[len(prefix):]: v for n, v in a.items() if n.startswith(prefix)}
        s.give_back()
        for stage in (lambda s: graph_attention(nc, s, XS, ident, a["x"], xn_d, part("gnn_"), sums_d, scratch),
                      lambda s: mixer(nc, s, XS, ident, part("mix_")),
                      lambda s: add_branches(nc, s, XS, a["x"], xn_d, sums_d),
                      lambda s: experts(nc, s, XS, ident, part("ffn_"), out)):
            s = Names(nc)
            stage(s)
            s.give_back()


def laid_out(inputs):
    a = {n: np.asarray(v) for n, v in inputs.items()}
    ea = a["edge_attr_16"].reshape(NTE, TE, ED)
    src, dst = (a[n].reshape(NTE, TE) for n in ("src", "dst"))
    d = {"x": a["x"], "gnn_src": src, "gnn_dst": dst, "gnn_dstT": dst.T, "gnn_ea": ea.reshape(NTE, -1),
         "gnn_eaT": ea.transpose(0, 2, 1).reshape(NTE, -1)}
    for n in ("W_l", "W_r", "W_e"):
        d[f"gnn_{n}T"] = a[f"L0_gnn_{n}"].T
    for n in ("b_l", "b_r", "att", "bias"):
        d[f"gnn_{n}"] = a[f"L0_gnn_{n}"]
    for n in ("Wq", "Wk", "Wv", "Wo", "bo", "W1", "W2", "b2"):
        d[f"mix_{n}"] = a[f"L0_mix_{n}"]
    for n in ("ln1_g", "ln1_b", "b1", "ln2_g", "ln2_b"):
        d[f"mix_{n}"] = columns(a[f"L0_mix_{n}"])
    for n in ("Wr", "W1s", "W2s", "b2s", "W1p", "W2p", "b2p"):
        d[f"ffn_{n}"] = a[f"L0_ffn_{n}"]
    for n in ("b1s", "b1p"):
        d[f"ffn_{n}"] = columns(a[f"L0_ffn_{n}"])
    return {n: np.ascontiguousarray(v) for n, v in d.items()}


def kernel(**inputs):
    import concourse.bacc as bacc
    from concourse.bass_utils import run_bass_kernel_spmd

    nc = bacc.Bacc("TRN2", target_bir_lowering=False, num_devices=1)
    arrays, args = {}, {}
    for name, v in laid_out(inputs).items():
        arrays[f"in_{name}"] = v
        args[name] = nc.dram_tensor(f"in_{name}", v.shape, mybir.dt.from_np(v.dtype), kind="ExternalInput").ap()
    out = nc.dram_tensor("out", (N, D), F32, kind="ExternalOutput").ap()
    gps_layer(nc, args, out)
    return run_bass_kernel_spmd(nc, [arrays], core_ids=[0]).results[0]["out"]
```

```python
from contextlib import ExitStack

import numpy as np

import concourse.bass as bass
from concourse import mybir

F32 = mybir.dt.float32
I32 = mybir.dt.int32
U32 = mybir.dt.uint32
ALU = mybir.AluOpType
ACT = mybir.ActivationFunctionType
AX = mybir.AxisListType

N, D = 3125, 256
P = 125
NT = N // P
GT = 5
NG = NT // GT
GN = GT * P
KC = D // 128
HALVES = ((0, 313), (313, 312))
DEPTH = 4
EXPERTS = 8

E, ED = 100000, 16
TE = 125
NTE = E // TE
WN = 112
NW = -(-N // WN)
GH = 4
IG = 4
STEPS = 2 * -(-(NTE + NW - 1) // (4 * IG))
GB = 4
BYV = 3
CH = -(-(2 * IG * STEPS) // 128)
ITEMS = 128 * CH
RUN = CH * TE
EA0 = D + 2 * GH
MW = EA0 + ED + 1
SLOPE = 0.2
LOW = -1.0e30
MH, MD = 8, 32
FF = 1024
FC = FF // 128
QK_SCALE = float(MD) ** -0.25
EPS = 1e-5
LOWEST = -3.0e38
CONSTS = 2


class Names:

    def __init__(self, nc):
        self._nc, self._all = nc, {}

    def __getitem__(self, name):
        if name not in self._all:
            self._all[name] = self._nc.alloc_semaphore(name=name)
        return self._all[name]

    def give_back(self):
        self._nc.clear_and_free_semaphores(list(self._all.values()))
        self._nc.all_engine_barrier()


def chunked(w):
    return w.rearrange("(k p) n -> p k n", p=128)


def columns(v):
    v = np.asarray(v)
    return np.ascontiguousarray(np.swapaxes(v.reshape(v.shape[:-1] + (-1, 128)), -1, -2))


def layer_norm(v, s, tag, n, src, dst, st, mv, ve, rstd):
    v.sem_inc(s[tag + "_seen"], 1)
    for j in range(GT):
        v.bn_stats(st[:, j, :], src(j)).then_inc(s[tag + "_stats"], 1)
    v.wait_ge(s[tag + "_stats"], GT * n + GT)
    v.sem_inc(s[tag + "_seen"], 1)
    for j in range(GT):
        v.bn_aggr(mv[:, j, :], st[:, j, :]).then_inc(s[tag + "_aggr"], 1)
    v.wait_ge(s[tag + "_aggr"], GT * n + GT)
    v.tensor_scalar(ve[:, :], mv[:, :, 1], EPS, None, ALU.add).then_inc(s[tag + "_vareps"], 1)
    v.wait_ge(s[tag + "_rstd"], n + 1)
    for j in range(GT):
        v.tensor_scalar(dst(j), src(j), mv[:, j, 0:1], rstd[:, j:j + 1],
                        ALU.subtract, ALU.mult).then_inc(s[tag + "_out"], 1)


def rstd_side(p, s, tag, n, ve, rstd, mhalf):
    p.wait_ge(s[tag + "_vareps"], n + 1)
    p.tensor_tensor(rstd[:, :], ve[:, :], mhalf[:, :], ALU.pow).then_inc(s[tag + "_rstd"], 1)


def row(x, g, j):
    return x[:, g * GT + j, :] if isinstance(g, int) else x[:, bass.ds(g * GT + j, 1), :].rearrange("p a d -> p (a d)")


def picked(a, l):
    if isinstance(l, int):
        return a[l]
    return a[bass.ds(l, 1)].rearrange("a b c -> (a b) c" if len(a.shape) == 3 else "a b -> (a b)")


def mixer(nc, s, XS, ident, w):
    with ExitStack() as c:
        def sb(name, shape, dt=F32):
            return c.enter_context(nc.sbuf_tensor(name, shape, dt))

        def ps(name, shape):
            return c.enter_context(nc.psum_tensor(name, shape, F32))

        KK = sb("m_kk", [P, NT, D])
        VV = sb("m_vv", [P, NT, D])
        HT = sb("m_ht", [128, KC, N])
        H2 = sb("m_h2", [128, KC, GN])
        N2 = sb("m_n2", [P, GT, D])
        HID = sb("m_hid", [128, FC, GN])
        QE = sb("m_qe", [P, GT, D])
        QN = sb("m_qn", [P, GT, D])
        wqkv = sb("m_wqkv", [128, KC, 3 * D])
        wo = sb("m_wo", [128, KC, D])
        w1 = sb("m_w1", [128, KC, FF])
        w2 = sb("m_w2", [128, FC, D])
        ln1 = sb("m_ln1", [128, 2, KC])
        ln2 = sb("m_ln2", [128, 2, KC])
        b1 = sb("m_b1", [128, FC])
        rows = sb("m_rows", [1, 2, D])
        ones = sb("m_ones", [128, 128])
        st = sb("m_st", [P, GT, 6])
        mv = sb("m_mv", [P, GT, 2])
        ve = sb("m_ve", [P, GT])
        rstd = sb("m_rstd", [P, GT])
        mhalf = sb("m_mhalf", [P, GT])
        qmax = sb("m_qmax", [P, GT, MH])
        qsum = sb("m_qsum", [P, GT * MH])
        qrec = sb("m_qrec", [P, GT * MH])
        KM = sb("m_kmax", [P, D])
        KG = sb("m_kgroup", [P, D])
        kcol = sb("m_kcol", [128, KC])
        kdiag = sb("m_kdiag", [128, KC, 128])
        CT = sb("m_ct", [128, KC, 128])
        rk = sb("m_rk", [128, KC])
        MO = sb("m_mo", [128, KC, D])
        pH = ps("m_pH", [128, 4, 512])
        pO0 = ps("m_pO0", [128, 512])
        pT = ps("m_pT", [128, 12, 128])
        pO = (pO0[:, 0:D], pT[:, 10:12, :].rearrange("p a b -> p (a b)"))

        block = c.enter_context(nc.Block())

        PER_T, PER_O = 16, 52
        T1 = lambda l, g: PER_T * l + 2 * g + 1
        TQ = lambda l, g: PER_T * l + 2 * g + 2
        TQ_LAST, TK = 9, 10
        T2 = lambda l, g: PER_T * l + 11 + g
        OUT_FIRST, OUT_LAST = 2, 47
        OUT_ATTN = lambda g: 7 + 10 * g
        OUT_MLP = lambda g: 12 + 10 * g
        ATTN_DMAS, FF_DMAS = 7, 6

        @block.sync
        def _(sp):
            def load_attn(l):
                for i, name in enumerate(("Wq", "Wk", "Wv")):
                    sp.dma_start(wqkv[:, :, i * D:(i + 1) * D], chunked(picked(w[name], l))).then_inc(s["m_attn_w"], 16)
                sp.dma_start(wo[:, :, :], chunked(picked(w["Wo"], l))).then_inc(s["m_attn_w"], 16)
                sp.dma_start(ln1[:, 0, :], picked(w["ln1_g"], l)).then_inc(s["m_attn_w"], 16)
                sp.dma_start(ln1[:, 1, :], picked(w["ln1_b"], l)).then_inc(s["m_attn_w"], 16)
                sp.dma_start(rows[0:1, 0, :], picked(w["bo"], l).unsqueeze(0)).then_inc(s["m_attn_w"], 16)

            def load_ff(l):
                sp.dma_start(w1[:, :, :], chunked(picked(w["W1"], l))).then_inc(s["m_ff_w"], 16)
                sp.dma_start(w2[:, :, :], chunked(picked(w["W2"], l))).then_inc(s["m_ff_w"], 16)
                sp.dma_start(ln2[:, 0, :], picked(w["ln2_g"], l)).then_inc(s["m_ff_w"], 16)
                sp.dma_start(ln2[:, 1, :], picked(w["ln2_b"], l)).then_inc(s["m_ff_w"], 16)
                sp.dma_start(b1[:, :], picked(w["b1"], l)).then_inc(s["m_ff_w"], 16)
                sp.dma_start(rows[0:1, 1, :], picked(w["b2"], l).unsqueeze(0)).then_inc(s["m_ff_w"], 16)

            load_attn(0)
            load_ff(0)
            with sp.Fori(0, DEPTH - 1) as l:
                sp.wait_ge(s["m_o_full"], PER_O * l + OUT_ATTN(NG - 2) + GT)
                load_attn(l + 1)
                sp.wait_ge(s["m_o_full"], PER_O * l + PER_O)
                load_ff(l + 1)

        @block.gpsimd
        def _(p):
            p.memset(mhalf[:, :], -0.5).then_inc(s["m_const"], 1)
            p.memset(ones[:, :], 1.0).then_inc(s["m_const"], 1)
            p.memset(CT[:, :, :], 0.0).then_inc(s["m_const"], 1)
            p.wait_ge(s["m_const"], 3)
            with p.Fori(0, NG + 2 * NG * DEPTH) as n:
                rstd_side(p, s, "m_ln", n, ve, rstd, mhalf)

        @block.tensor
        def _(pe):
            def cols(g, j):
                return slice((g * GT + j) * P, (g * GT + j + 1) * P) if isinstance(g, int) else bass.ds((g * GT + j) * P, P)

            def transposes(n, src, ready, count, outs):
                pe.wait_ge(s[ready], count)
                pe.wait_ge(s["m_t_out"], n + 1)
                pe.wait_ge(s["m_o_out"], outs + 2)
                for k in range(KC):
                    for j in range(GT):
                        ins = pe.transpose(pT[:, GT * k + j, 0:P], src(j)[:, k * 128:(k + 1) * 128], ident[0:P, 0:P])
                ins.then_inc(s["m_t_full"], 1)

            def qkv(l, g):
                for j in range(GT):
                    t = NT * l + g * GT + j
                    b = 2 * (j % 2)
                    pe.wait_ge(s["m_qkv_act"], t + (j == 0))
                    pe.wait_ge(s["m_qkv_dve"], t + (j == 0))
                    for k in range(KC):
                        pe.matmul(pH[0:P, b, 0:256], HT[:, k, cols(g, j)], wqkv[:, k, 0:256], start=(k == 0), stop=(k == KC - 1))
                    for k in range(KC):
                        ins = pe.matmul(pH[0:P, b + 1, 0:512], HT[:, k, cols(g, j)], wqkv[:, k, 256:768],
                                        start=(k == 0), stop=(k == KC - 1))
                    ins.then_inc(s["m_qkv_full"], 1)

            def context(l, g, first, last):
                pe.wait_ge(s["m_kexp"], NG * l + g + 1)
                for j in range(GT):
                    f, e = first and j == 0, last and j == GT - 1
                    k_, v_ = row(KK, g, j), row(VV, g, j)
                    for m in range(KC):
                        half = slice(m * 128, (m + 1) * 128)
                        pe.matmul(pH[:, m, 0:128], v_[:, half], k_[:, half], start=f, stop=e)
                        ins = pe.matmul(pH[:, 2 + m, 0:1], k_[:, half], ones[0:P, 0:1], start=f, stop=e)
                if last:
                    ins.then_inc(s["m_ctx"], 1)

            def out_rows(l, base, parity, bias, lhs, rhs, chunks, t_out):
                for j in range(GT):
                    o = pO[(j + parity) % 2][0:P, :]
                    if (j + parity) % 2:
                        pe.wait_ge(s["m_t_out"], t_out + 1)
                    pe.wait_ge(s["m_o_out"], PER_O * l + base + j + 1)
                    for k in range(chunks):
                        pe.matmul(o, lhs(k, j), rhs[:, k, :], start=(k == 0), stop=False)
                    pe.matmul(o, ones[0:1, 0:P], rows[0:1, bias, :], start=False, stop=True).then_inc(s["m_o_full"], 1)

            def attn_out(l, g, base, parity):
                t_out = PER_T * l + TK + 1 if g == 0 else T2(l, g - 1) + 1
                out_rows(l, base, parity, 0, lambda k, j: HT[:, k, cols(g, j)], MO, KC, t_out)

            def mlp_out(l, g, base, parity):
                pe.wait_ge(s["m_gelu"], FC * (NG * l + g) + FC + 2)
                out_rows(l, base, parity, 1, lambda k, j: HID[:, k, j * P:(j + 1) * P], w2, FC,
                         T2(l, min(g + 1, NG - 1)) + 1)

            def hidden(l, g):
                pe.wait_ge(s["m_t_out"], T2(l, g) + 2)
                for f in range(FC):
                    b = 2 * (f % 2)
                    pe.wait_ge(s["m_gelu"], FC * (NG * l + g) + f + 1)
                    for h, (at, n) in enumerate(HALVES):
                        for k in range(KC):
                            ins = pe.matmul(pH[:, b + h, 0:n], w1[:, k, f * 128:(f + 1) * 128], H2[:, k, at:at + n],
                                            start=(k == 0), stop=(k == KC - 1))
                    ins.then_inc(s["m_hid"], 1)

            pe.wait_ge(s["m_const"], 3)
            with pe.Fori(0, DEPTH) as l:
                pe.wait_ge(s["m_attn_w"], 16 * ATTN_DMAS * l + 16 * ATTN_DMAS)
                transposes(PER_T * l, lambda j: row(KK, 0, j), "m_ln_out", 50 * l + 25, PER_O * l)
                pe.wait_ge(s["m_t_out"], PER_T * l + 2)
                for g in range(NG - 1):
                    qkv(l, g)
                    transposes(T1(l, g), lambda j: row(KK, g + 1, j), "m_ln_out", 50 * l + 25, PER_O * l)
                    transposes(TQ(l, g), lambda j: QN[:, j, :], "m_qn", NG * l + g + 1, PER_O * l)
                qkv(l, NG - 1)
                transposes(PER_T * l + TQ_LAST, lambda j: QN[:, j, :], "m_qn", NG * l + NG, PER_O * l)

                pe.wait_ge(s["m_kmax"], (NG + 1) * l + NG + 1)
                pe.wait_ge(s["m_t_out"], PER_T * l + TK + 1)
                for k in range(KC):
                    ins = pe.transpose(pT[:, k, 0:P], KM[:, k * 128:(k + 1) * 128], ident[0:P, 0:P])
                ins.then_inc(s["m_t_full"], 1)
                pe.wait_ge(s["m_kdiag"], KC * l + KC)
                for k in range(KC):
                    ins = pe.matmul(pT[0:P, 4 + k, :], ones[:, 0:P], kdiag[:, k, :], start=True, stop=True)
                ins.then_inc(s["m_kmax_rows"], 1)

                pe.wait_ge(s["m_qkv_act"], NT * l + NT + 1)
                pe.wait_ge(s["m_qkv_dve"], NT * l + NT + 1)
                context(l, 0, True, False)
                for g in range(1, NG - 1):
                    context(l, g, False, False)
                context(l, NG - 1, False, True)
                pe.wait_ge(s["m_ct"], 8 * l + 8)
                pe.wait_ge(s["m_t_out"], PER_T * l + TK + 2)
                for m in range(KC):
                    pe.wait_ge(s["m_o_out"], PER_O * l + m + 1)
                    pe.matmul(pO[m], CT[:, m, :], wo[:, m, :], start=True, stop=True).then_inc(s["m_o_full"], 1)
                pe.wait_ge(s["m_o_out"], PER_O * l + 4)
                pe.wait_ge(s["m_ksub"], NG * l + NG)

                attn_out(l, 0, OUT_FIRST, 0)
                transposes(T2(l, 0), lambda j: N2[:, j, :], "m_ln_out", 50 * l + 30, PER_O * l + OUT_FIRST + GT)
                pe.wait_ge(s["m_ff_w"], 16 * FF_DMAS * l + 16 * FF_DMAS)
                for g in range(NG - 1):
                    attn_out(l, g + 1, OUT_ATTN(g), 1)
                    hidden(l, g)
                    transposes(T2(l, g + 1), lambda j: N2[:, j, :], "m_ln_out", 50 * l + 10 * g + 35, PER_O * l + OUT_ATTN(g) + GT)
                    mlp_out(l, g, OUT_MLP(g), 0)
                hidden(l, NG - 1)
                mlp_out(l, NG - 1, OUT_LAST, 1)

        @block.scalar
        def _(a):
            with a.Fori(0, DEPTH) as l:
                with a.Fori(0, NG) as g:
                    for j in range(GT):
                        b = 2 * (j % 2)
                        a.wait_ge(s["m_qkv_full"], NT * l + g * GT + j + 1)
                        a.activation(row(KK, g, j), pH[0:P, b + 1, 0:256], ACT.Copy)
                        a.activation(row(VV, g, j), pH[0:P, b + 1, 256:512], ACT.Copy).then_inc(s["m_qkv_act"], 1)
                    a.wait_ge(s["m_qkv_dve"], NT * l + g * GT + GT + 1)
                    a.activation(QE[:, :, :], QE[:, :, :], ACT.Exp, scale=QK_SCALE).then_inc(s["m_qexp"], 1)
                with a.Fori(0, NG) as g:
                    a.wait_ge(s["m_ksub"], NG * l + g + 1)
                    kg = KK[:, bass.ds(g * GT, GT), :]
                    a.activation(kg, kg, ACT.Exp, scale=QK_SCALE).then_inc(s["m_kexp"], 1)
                a.wait_ge(s["m_ff_w"], 16 * FF_DMAS * l + 16 * FF_DMAS)
                with a.Fori(0, NG) as g:
                    a.wait_ge(s["m_o_full"], PER_O * l + 10 * g + 7)
                    for f in range(FC):
                        b = 2 * (f % 2)
                        a.wait_ge(s["m_hid"], FC * (NG * l + g) + f + 1)
                        for h, (at, n) in enumerate(HALVES):
                            ins = a.activation(HID[:, f, at:at + n], pH[:, b + h, 0:n], ACT.Gelu, bias=b1[:, f:f + 1])
                        ins.then_inc(s["m_gelu"], 1)

        @block.vector
        def _(v):
            def norm(n, src, dst):
                layer_norm(v, s, "m_ln", n, src, dst, st, mv, ve, rstd)

            def out_transposed(n, dst, ln=None):
                v.wait_ge(s["m_t_full"], n + 1)
                for k in range(KC):
                    o = dst(k).rearrange("p (j q) -> p j q", j=GT)
                    i = pT[:, GT * k:GT * k + GT, 0:P]
                    if ln is None:
                        ins = v.tensor_copy(o, i)
                    else:
                        ins = v.tensor_scalar(o, i, ln[:, 0, k:k + 1], ln[:, 1, k:k + 1], ALU.mult, ALU.add)
                ins.then_inc(s["m_t_out"], 1)

            def group_cols(g):
                return lambda k: HT[:, k, g * GN:(g + 1) * GN] if isinstance(g, int) else HT[:, k, bass.ds(g * GN, GN)]

            def q_tiles(l, g):
                for j in range(GT):
                    t = NT * l + g * GT + j
                    b = 2 * (j % 2)
                    v.wait_ge(s["m_qkv_full"], t + 1)
                    q = pH[0:P, b, 0:256].rearrange("p (h d) -> p h d", h=MH)
                    v.tensor_reduce(qmax[:, j, :], q, AX.X, ALU.max).then_inc(s["m_qmax"], 1)
                    v.wait_ge(s["m_qmax"], t + 1)
                    v.tensor_tensor(QE[:, j, :].rearrange("p (h d) -> p h d", h=MH), q,
                                    qmax[:, j, :].unsqueeze(2).broadcast_to([P, MH, MD]), ALU.subtract).then_inc(s["m_qkv_dve"], 1)

            def k_max(l, g):
                v.wait_ge(s["m_qkv_act"], NT * l + g * GT + GT + 1)
                kg = KK[:, g * GT:(g + 1) * GT, :] if isinstance(g, int) else KK[:, bass.ds(g * GT, GT), :]
                v.tensor_reduce(KG[:, :], kg.rearrange("p j d -> p d j"), AX.X, ALU.max).then_inc(s["m_kgroup"], 1)
                v.wait_ge(s["m_kgroup"], NG * l + g + 1)
                v.wait_ge(s["m_kmax"], (NG + 1) * l + g + 1)
                v.tensor_tensor(KM[:, :], KM[:, :], KG[:, :], ALU.max).then_inc(s["m_kmax"], 1)

            def q_finish(l, g):
                v.wait_ge(s["m_qexp"], NG * l + g + 1)
                e = QE[:, :, :].rearrange("p j (h d) -> p (j h) d", h=MH)
                v.tensor_reduce(qsum[:, :], e, AX.X, ALU.add).then_inc(s["m_qsum"], 1)
                v.wait_ge(s["m_qsum"], NG * l + g + 1)
                v.reciprocal(qrec[:, :], qsum[:, :]).then_inc(s["m_qrec"], 1)
                v.wait_ge(s["m_qrec"], NG * l + g + 1)
                v.tensor_tensor(QN[:, :, :].rearrange("p j (h d) -> p (j h) d", h=MH), e,
                                qrec[:, :].unsqueeze(2).broadcast_to([P, GT * MH, MD]), ALU.mult).then_inc(s["m_qn"], 1)

            def add_rows(l, g, base, parity):
                for j in range(GT):
                    v.wait_ge(s["m_o_full"], PER_O * l + base + j + 1)
                    x = row(XS, g, j)
                    v.tensor_tensor(x, x, pO[(j + parity) % 2][0:P, :], ALU.add).then_inc(s["m_o_out"], 1)

            def norm_after(l, g, n, base, dst):
                v.wait_ge(s["m_o_out"], PER_O * l + base + GT + 2)
                norm(n, lambda j: row(XS, g, j), dst)

            for name, k in (("m_t_out", 1), ("m_o_out", 2), ("m_gelu", 2), ("m_qkv_act", 1), ("m_qkv_dve", 1)):
                v.sem_inc(s[name], k)
            with v.Fori(0, NG) as g:
                norm(g, lambda j: row(XS, g, j), lambda j: row(KK, g, j))
            with v.Fori(0, DEPTH) as l:
                v.wait_ge(s["m_attn_w"], 16 * ATTN_DMAS * l + 16 * ATTN_DMAS)
                v.memset(KM[:, :], LOWEST).then_inc(s["m_kmax"], 1)
                out_transposed(PER_T * l, group_cols(0), ln1)
                with v.Fori(0, NG - 1) as g:
                    q_tiles(l, g)
                    out_transposed(T1(l, g), group_cols(g + 1), ln1)
                    k_max(l, g)
                    q_finish(l, g)
                    out_transposed(TQ(l, g), group_cols(g))
                q_tiles(l, NG - 1)
                k_max(l, NG - 1)
                q_finish(l, NG - 1)
                out_transposed(PER_T * l + TQ_LAST, group_cols(NG - 1))

                v.wait_ge(s["m_t_full"], PER_T * l + TK + 1)
                v.tensor_reduce(kcol[:, :], pT[:, 0:KC, 0:P], AX.X, ALU.max).then_inc(s["m_t_out"], 1)
                v.wait_ge(s["m_t_out"], PER_T * l + TK + 2)
                for k in range(KC):
                    v.tensor_scalar(kdiag[:, k, :], ident[:, :], kcol[:, k:k + 1], None, ALU.mult).then_inc(s["m_kdiag"], 1)
                v.wait_ge(s["m_kmax_rows"], l + 1)
                v.wait_ge(s["m_qkv_act"], NT * l + NT + 1)
                v.sem_inc(s["m_k_seen"], 1)
                kmax_rows = pT[0:P, 4:6, :].rearrange("p a b -> p (a b)").unsqueeze(1).broadcast_to([P, GT, D])
                with v.Fori(0, NG) as g:
                    kg = KK[:, bass.ds(g * GT, GT), :]
                    v.tensor_tensor(kg, kg, kmax_rows, ALU.subtract).then_inc(s["m_ksub"], 1)

                v.wait_ge(s["m_ctx"], l + 1)
                v.reciprocal(rk[:, :], pH[:, 2:4, 0]).then_inc(s["m_rk"], 1)
                for m in range(KC):
                    for b in range(4):
                        r = slice(32 * b, 32 * b + 32)
                        v.tensor_copy(CT[r, m, 32 * b:32 * b + 32], pH[r, m, 32 * b:32 * b + 32]).then_inc(s["m_ct"], 1)
                v.wait_ge(s["m_rk"], l + 1)
                for m in range(KC):
                    v.wait_ge(s["m_o_full"], PER_O * l + m + 1)
                    v.tensor_scalar(MO[:, m, :], pO[m], rk[:, m:m + 1], None, ALU.mult).then_inc(s["m_o_out"], 1)

                v.wait_ge(s["m_ff_w"], 16 * FF_DMAS * l + 16 * FF_DMAS)
                to_n2, to_h2 = (lambda j: N2[:, j, :]), (lambda k: H2[:, k, :])
                add_rows(l, 0, OUT_FIRST, 0)
                norm_after(l, 0, 10 * l + 5, OUT_FIRST, to_n2)
                out_transposed(T2(l, 0), to_h2, ln2)
                with v.Fori(0, NG - 1) as g:
                    add_rows(l, g + 1, OUT_ATTN(g), 1)
                    norm_after(l, g + 1, 10 * l + 2 * g + 6, OUT_ATTN(g), to_n2)
                    out_transposed(T2(l, g + 1), to_h2, ln2)
                    add_rows(l, g, OUT_MLP(g), 0)
                    norm_after(l, g, 10 * l + 2 * g + 7, OUT_MLP(g), lambda j: row(KK, g, j))
                add_rows(l, NG - 1, OUT_LAST, 1)
                norm_after(l, NG - 1, 10 * l + 14, OUT_LAST, lambda j: row(KK, NG - 1, j))


def graph_attention(nc, s, XS, ident, x, xn_d, g, sums_d, scratch):
    key_d, dl_d, eat_d, ea_d, xl_d, al_d, pc_d, wl_d = (scratch[n] for n in ("key", "dl", "eat", "ea", "xl", "al", "pc", "wl"))
    with ExitStack() as keep:
        def kept(name, shape, dt=F32):
            return keep.enter_context(nc.sbuf_tensor(name, shape, dt))

        XL = kept("g_xl", [WN, NW, D])
        XRW = kept("g_xr", [128, NW, D])
        SRCX = kept("g_srcx", [TE, ITEMS], I32)
        DLX = kept("g_dlx", [TE, ITEMS])
        WI = kept("g_wi", [1, ITEMS], I32)
        WP = kept("g_wp", [1, ITEMS // IG], I32)
        attb = kept("g_attb", [128, D])

        with ExitStack() as c:
            XT = c.enter_context(nc.sbuf_tensor("p_xt", [128, KC, NW * WN], F32))
            wlr = c.enter_context(nc.sbuf_tensor("p_wlr", [128, KC, 2 * D], F32))
            brow = c.enter_context(nc.sbuf_tensor("p_brow", [1, 2 * D], F32))
            ones = c.enter_context(nc.sbuf_tensor("p_ones", [1, WN], F32))
            st = c.enter_context(nc.sbuf_tensor("p_st", [P, GT, 6], F32))
            mv = c.enter_context(nc.sbuf_tensor("p_mv", [P, GT, 2], F32))
            ve = c.enter_context(nc.sbuf_tensor("p_ve", [P, GT], F32))
            rstd = c.enter_context(nc.sbuf_tensor("p_rstd", [P, GT], F32))
            mhalf = c.enter_context(nc.sbuf_tensor("p_mhalf", [P, GT], F32))
            pT = c.enter_context(nc.psum_tensor("p_pT", [128, 12, 128], F32))
            pP = c.enter_context(nc.psum_tensor("p_pP", [128, 4, 512], F32))
            block = c.enter_context(nc.Block())

            @block.sync
            def _(sp):
                sp.dma_start(XS[:, :, :], x.rearrange("(t p) d -> p t d", p=P)).then_inc(s["p_x"], 16)
                sp.dma_start(wlr[:, :, 0:D], chunked(g["W_lT"])).then_inc(s["p_w"], 16)
                sp.dma_start(wlr[:, :, D:], chunked(g["W_rT"])).then_inc(s["p_w"], 16)
                sp.dma_start(brow[0:1, 0:D], g["b_l"].unsqueeze(0)).then_inc(s["p_w"], 16)
                sp.dma_start(brow[0:1, D:], g["b_r"].unsqueeze(0)).then_inc(s["p_w"], 16)
                sp.dma_start(attb[:, :], g["att"].rearrange("h d -> (h d)").unsqueeze(0).broadcast_to([128, D])).then_inc(s["p_att"], 16)
                sp.dma_start(XRW[WN:128, :, :], g["W_eT"].unsqueeze(1).broadcast_to([ED, NW, D])).then_inc(s["p_we"], 16)
                sp.wait_ge(s["p_ln_out"], NT)
                sp.dma_start(xn_d.rearrange("(t p) d -> p t d", p=P), XS[:, :, :]).then_inc(s["p_stored"], 16)
                sp.wait_ge(s["p_xl"], NW)
                sp.dma_start(xl_d.rearrange("(w p) d -> p w d", p=WN), XL[:, :, :]).then_inc(s["p_stored"], 16)
                sp.wait_ge(s["p_we"], 16)
                sp.wait_ge(s["p_att"], 16)
                sp.wait_ge(s["p_stored"], 32)

            @block.gpsimd
            def _(p):
                p.memset(mhalf[:, :], -0.5).then_inc(s["p_const"], 1)
                p.memset(ones[:, :], 1.0).then_inc(s["p_const"], 1)
                p.memset(XT[:, :, N:], 0.0).then_inc(s["p_const"], 1)
                p.wait_ge(s["p_const"], 3)
                for n in range(NG):
                    rstd_side(p, s, "p_ln", n, ve, rstd, mhalf)

            @block.tensor
            def _(pe):
                for q in range(NG):
                    pe.wait_ge(s["p_ln_out"], GT * (q + 1))
                    if q:
                        pe.wait_ge(s["p_t_out"], q)
                    for k in range(KC):
                        for j in range(GT):
                            ins = pe.transpose(pT[:, GT * k + j, 0:P], XS[:, GT * q + j, k * 128:(k + 1) * 128], ident[0:P, 0:P])
                    ins.then_inc(s["p_t_full"], 1)
                pe.wait_ge(s["p_t_out"], NG)
                pe.wait_ge(s["p_w"], 64)
                pe.wait_ge(s["p_const"], 3)
                for w in range(NW):
                    if w >= 4:
                        pe.wait_ge(s["p_xl"], w - 3)
                        pe.wait_ge(s["p_xr"], w - 3)
                    for k in range(KC):
                        pe.matmul(pP[0:WN, w % 4, :], XT[:, k, w * WN:(w + 1) * WN], wlr[:, k, :], start=(k == 0), stop=False)
                    pe.matmul(pP[0:WN, w % 4, :], ones[0:1, :], brow[0:1, :], start=False, stop=True).then_inc(s["p_lr"], 1)

            @block.vector
            def _(v):
                v.wait_ge(s["p_x"], 16)
                for q in range(NG):
                    layer_norm(v, s, "p_ln", q, lambda j: XS[:, q * GT + j, :], lambda j: XS[:, q * GT + j, :], st, mv, ve, rstd)
                    v.wait_ge(s["p_t_full"], q + 1)
                    for k in range(KC):
                        ins = v.tensor_copy(XT[:, k, q * GN:(q + 1) * GN].rearrange("p (j n) -> p j n", j=GT), pT[:, GT * k:GT * k + GT, 0:P])
                    ins.then_inc(s["p_t_out"], 1)
                for w in range(NW):
                    v.wait_ge(s["p_lr"], w + 1)
                    v.tensor_copy(XL[:, w, :], pP[0:WN, w % 4, 0:D]).then_inc(s["p_xl"], 1)
                    v.tensor_copy(XRW[0:WN, w, :], pP[0:WN, w % 4, D:]).then_inc(s["p_xr"], 1)

        with ExitStack() as c:
            def sb(name, shape, dt=F32):
                return c.enter_context(nc.sbuf_tensor(name, shape, dt))

            ends_i = sb("i_ends_i", [NW, 2, NTE], I32)
            ends = sb("i_ends", [NW, 2, NTE])
            below = sb("i_below", [NW, 2, NTE])
            wbase = sb("i_wbase", [NW, 2])
            counts = sb("i_counts", [NW, 2])
            nitems = sb("i_nitems", [NW, 1])
            wide = sb("i_wide", [NW, 2, 128])
            one28 = sb("i_one28", [NW, 128])
            upto = sb("i_upto", [NW, NW])
            inum = sb("i_inum", [128, CH])
            lane = sb("i_lane", [128, NW])
            tab = sb("i_tab", [128, 3, NW])
            shift = sb("i_shift", [128, NW])
            cmp = sb("i_cmp", [128, CH, NW])
            wv = sb("i_wv", [128, CH])
            tile_f = sb("i_tile_f", [128, CH])
            tile_i = sb("i_tile_i", [128, CH], I32)
            base = sb("i_base", [128, CH])
            wc_i = sb("i_wc_i", [128, CH], I32)
            src_i = sb("i_src_i", [128, CH, TE], I32)
            dst_i = sb("i_dst_i", [128, CH, TE], I32)
            src_f = sb("i_src_f", [128, CH, TE])
            dst_f = sb("i_dst_f", [128, CH, TE])
            dl = sb("i_dl", [128, CH, TE])
            ok = sb("i_ok", [128, 2, CH, TE])
            eaT = sb("i_eaT", [128, 2, ED * TE])
            ea = sb("i_ea", [128, 2, ED * TE])
            edge = sb("i_edge", [1, 2])
            pN = c.enter_context(nc.psum_tensor("i_pN", [128, 512], F32))
            pX = c.enter_context(nc.psum_tensor("i_pX", [128, 2, 512], F32))
            block = c.enter_context(nc.Block())

            @block.sync
            def _(sp):
                sp.dma_start(ends_i[:, 0, :], g["dstT"][0:1, :].broadcast_to([NW, NTE])).then_inc(s["i_ends"], 16)
                sp.dma_start(ends_i[:, 1, :], g["dstT"][TE - 1:TE, :].broadcast_to([NW, NTE])).then_inc(s["i_ends"], 16)
                for k in range(CH):
                    sp.wait_ge(s[f"i_ea{k % 2}"], 32 * (k // 2 + 1))
                    sp.dma_start(eat_d[k * 128:(k + 1) * 128, :], eaT[:, k % 2, :]).then_inc(s[f"i_ea_out{k % 2}"], 16)
                    sp.dma_start(ea_d[k * 128:(k + 1) * 128, :], ea[:, k % 2, :]).then_inc(s[f"i_ea_out{k % 2}"], 16)
                sp.wait_ge(s["i_dl"], 1)
                sp.dma_start(dl_d.rearrange("(c p) e -> p c e", p=128), dl[:, :, :]).then_inc(s["i_stored"], 16)
                sp.wait_ge(s["i_key"], 1)
                sp.dma_start(key_d[1:1 + ITEMS * TE].rearrange("(c p e) -> p c e", p=128, e=TE), ok[:, 0, :, :]).then_inc(s["i_stored"], 16)
                sp.wait_ge(s["i_const"], 5)
                sp.dma_start(key_d[0:1].unsqueeze(0), edge[0:1, 0:1]).then_inc(s["i_stored"], 16)
                sp.dma_start(key_d[ITEMS * TE + 1:ITEMS * TE + 2].unsqueeze(0), edge[0:1, 1:2]).then_inc(s["i_stored"], 16)
                sp.wait_ge(s["i_wc"], 1)
                with nc.allow_non_contiguous_dma(reason="896 words"):
                    sp.dma_start(wl_d.rearrange("(c p) -> p c", p=128), wc_i[:, :]).then_inc(s["i_wl"], 16)
                sp.wait_ge(s["i_wl"], 16)
                sp.dma_start(WI[0:1, :], wl_d.unsqueeze(0)).then_inc(s["i_stored"], 16)
                sp.wait_ge(s["i_stored"], 16 * 5)
                sp.wait_ge(s["i_ea_out0"], 32 * 4)
                sp.wait_ge(s["i_ea_out1"], 32 * 3)

            @block.gpsimd
            def _(p):
                p.iota(wbase[:, :], pattern=[[WN, 2]], base=0, channel_multiplier=WN, allow_small_or_imprecise_dtypes=True).then_inc(s["i_const"], 1)
                p.iota(inum[:, :], pattern=[[128, CH]], base=0, channel_multiplier=1, allow_small_or_imprecise_dtypes=True).then_inc(s["i_const"], 1)
                p.iota(lane[:, :], pattern=[[1, NW]], base=0, channel_multiplier=0, allow_small_or_imprecise_dtypes=True).then_inc(s["i_const"], 1)
                p.memset(edge[:, :], -1.0).then_inc(s["i_const"], 1)
                p.memset(one28[:, :], 1.0).then_inc(s["i_const"], 1)
                p.wait_ge(s["i_const"], 5)
                p.affine_select(out=upto[:, :], in_=one28[:, 0:NW], compare_op=ALU.is_ge, fill=0.0, base=0,
                                pattern=[[1, NW]], channel_multiplier=-1).then_inc(s["i_upto"], 1)
                p.wait_ge(s["i_tile"], 1)
                for k in range(CH):
                    at = bass.IndirectOffsetOnAxis(ap=tile_i[:, k:k + 1], axis=0)
                    p.indirect_dma_start(out=dst_i[:, k, :], out_offset=None, in_=g["dst"], in_offset=at).then_inc(s["i_dst"], 16)
                    p.indirect_dma_start(out=src_i[:, k, :], out_offset=None, in_=g["src"], in_offset=at).then_inc(s["i_src"], 16)
                for k in range(CH):
                    at = bass.IndirectOffsetOnAxis(ap=tile_i[:, k:k + 1], axis=0)
                    if k >= 2:
                        p.wait_ge(s[f"i_ea_out{k % 2}"], 32 * (k // 2))
                    p.indirect_dma_start(out=eaT[:, k % 2, :], out_offset=None, in_=g["eaT"], in_offset=at).then_inc(s[f"i_ea{k % 2}"], 16)
                    p.indirect_dma_start(out=ea[:, k % 2, :], out_offset=None, in_=g["ea"], in_offset=at).then_inc(s[f"i_ea{k % 2}"], 16)

            @block.tensor
            def _(pe):
                pe.wait_ge(s["i_wide"], 2)
                pe.wait_ge(s["i_upto"], 1)
                pe.matmul(pN[:, 0:NW], wide[:, 0, :], upto[:, :], start=True, stop=True)
                pe.matmul(pN[:, NW:2 * NW], wide[:, 0, :], ident[0:NW, 0:NW], start=True, stop=True)
                pe.matmul(pN[:, 2 * NW:3 * NW], wide[:, 1, :], ident[0:NW, 0:NW], start=True, stop=True).then_inc(s["i_tab"], 1)
                for n, (ready, t) in enumerate([("i_src_f", src_f)] * CH + [("i_dl", dl)] * CH):
                    pe.wait_ge(s[ready], 1)
                    if n >= 2:
                        pe.wait_ge(s["i_x_out"], n - 1)
                    pe.transpose(pX[0:TE, n % 2, 0:128], t[:, n % CH, :], ident[:, :]).then_inc(s["i_x"], 1)

            @block.vector
            def _(v):
                chain = s["i_chain"]
                done = [0]

                def then(ins):
                    done[0] += 1
                    ins.then_inc(chain, 1)
                    v.wait_ge(chain, done[0])

                v.wait_ge(s["i_ends"], 32)
                v.wait_ge(s["i_const"], 5)
                then(v.tensor_copy(ends[:, :, :], ends_i[:, :, :]))
                v.tensor_scalar(below[:, 0, :], ends[:, 1, :], wbase[:, 0:1], None, ALU.is_lt)
                then(v.tensor_scalar(below[:, 1, :], ends[:, 0, :], wbase[:, 1:2], None, ALU.is_lt))
                then(v.tensor_reduce(counts[:, :], below[:, :, :], AX.X, ALU.add))
                then(v.tensor_tensor(nitems[:, :], counts[:, 1:2], counts[:, 0:1], ALU.subtract))
                v.tensor_scalar(wide[:, 0, :], one28[:, :], nitems[:, 0:1], None, ALU.mult).then_inc(s["i_wide"], 1)
                v.tensor_scalar(wide[:, 1, :], one28[:, :], counts[:, 0:1], None, ALU.mult).then_inc(s["i_wide"], 1)
                v.wait_ge(s["i_tab"], 1)
                then(v.tensor_copy(tab[:, :, :], pN[:, 0:3 * NW].rearrange("p (a w) -> p a w", a=3)))
                then(v.tensor_tensor(shift[:, :], tab[:, 2, :], tab[:, 0, :], ALU.subtract))
                then(v.tensor_tensor(shift[:, :], shift[:, :], tab[:, 1, :], ALU.add))
                over_w = lambda a: a.unsqueeze(1).broadcast_to([128, CH, NW])
                over_c = lambda a: a.unsqueeze(2).broadcast_to([128, CH, NW])
                then(v.tensor_tensor(cmp[:, :, :], over_w(tab[:, 0, :]), over_c(inum[:, :]), ALU.is_le))
                then(v.tensor_reduce(wv[:, :], cmp[:, :, :], AX.X, ALU.add))
                then(v.tensor_tensor(cmp[:, :, :], over_w(lane[:, :]), over_c(wv[:, :]), ALU.is_equal))
                then(v.tensor_tensor(cmp[:, :, :], cmp[:, :, :], over_w(shift[:, :]), ALU.mult))
                then(v.tensor_reduce(tile_f[:, :], cmp[:, :, :], AX.X, ALU.add))
                then(v.tensor_tensor(tile_f[:, :], tile_f[:, :], inum[:, :], ALU.add))
                then(v.tensor_scalar(tile_f[:, :], tile_f[:, :], float(NTE - 1), None, ALU.min))
                v.tensor_copy(tile_i[:, :], tile_f[:, :]).then_inc(s["i_tile"], 1)
                v.tensor_scalar(base[:, :], wv[:, :], float(WN), None, ALU.mult)
                v.tensor_scalar(wc_i[:, :], wv[:, :], float(NW - 1), None, ALU.min).then_inc(s["i_wc"], 1)
                v.wait_ge(s["i_src"], 16 * CH)
                v.wait_ge(s["i_dst"], 16 * CH)
                v.tensor_copy(src_f[:, :, :], src_i[:, :, :]).then_inc(s["i_src_f"], 1)
                then(v.tensor_copy(dst_f[:, :, :], dst_i[:, :, :]))
                then(v.tensor_tensor(dl[:, :, :], dst_f[:, :, :], base[:, :].unsqueeze(2).broadcast_to([128, CH, TE]), ALU.subtract))
                v.sem_inc(s["i_dl"], 1)
                v.tensor_scalar(ok[:, 0, :, :], dl[:, :, :], 0.0, None, ALU.is_ge)
                then(v.tensor_scalar(ok[:, 1, :, :], dl[:, :, :], float(WN), None, ALU.is_lt))
                then(v.tensor_tensor(ok[:, 0, :, :], ok[:, 0, :, :], ok[:, 1, :, :], ALU.mult))
                then(v.tensor_scalar(dst_f[:, :, :], dst_f[:, :, :], 1.0, None, ALU.add))
                v.tensor_tensor(ok[:, 0, :, :], ok[:, 0, :, :], dst_f[:, :, :], ALU.mult).then_inc(s["i_key"], 1)
                for n in range(2 * CH):
                    v.wait_ge(s["i_x"], n + 1)
                    to = SRCX if n < CH else DLX
                    k = n % CH
                    v.tensor_copy(to[:, k * 128:(k + 1) * 128], pX[0:TE, n % 2, 0:128]).then_inc(s["i_x_out"], 1)

        with ExitStack() as mid:
            PCX = mid.enter_context(nc.sbuf_tensor("g_pcx", [TE, ITEMS, 2 * GH], F32))

            with ExitStack() as c:
                def sb(name, shape, dt=F32):
                    return c.enter_context(nc.sbuf_tensor(name, shape, dt))

                LT = sb("a_lt", [128, GB, IG, TE])
                DB = sb("a_db", [WN, GB, IG, TE])
                G = sb("a_g", [TE, GB, IG, D])
                R = sb("a_r", [TE, 2, IG, D])
                IX = sb("a_ix", [TE, GB, IG], I32)
                AX_ = sb("a_alpha", [TE, ITEMS, GH])
                AT = sb("a_alphaT", [128, CH, GH, TE])
                node = sb("a_node", [128, 1])
                pS = c.enter_context(nc.psum_tensor("a_pS", [128, GB, IG * D], F32))
                block = c.enter_context(nc.Block())

                @block.sync
                def _(sp):
                    with sp.Fori(0, STEPS // 2) as i:
                        for h in range(GB):
                            q = GB * i + h
                            sp.wait_ge(s["a_scored"], q + 1)
                            at = bass.ds(q * IG, IG)
                            sp.dma_start(DB[:, h, :, :], dl_d[at, :].rearrange("i e -> (i e)").unsqueeze(0).broadcast_to([WN, IG * TE])
                                         .rearrange("p (i e) -> p i e", i=IG)).then_inc(s[f"a_db{h}"], 16)
                            sp.dma_start(LT[WN:128, h, :, :], eat_d[at, :].rearrange("i (c e) -> c i e", c=ED)).then_inc(s[f"a_eat{h}"], 16)
                    sp.wait_ge(s["a_at"], CH * GH)
                    sp.dma_start(al_d.rearrange("(c p) h e -> p c h e", p=128), AT[:, :, :, :]).then_inc(s["a_stored"], 16)
                    sp.wait_ge(s["a_stored"], 16)

                @block.gpsimd
                def _(p):
                    p.iota(node[:, :], pattern=[[0, 1]], base=0, channel_multiplier=1, allow_small_or_imprecise_dtypes=True).then_inc(s["a_const"], 1)
                    p.memset(AX_[:, STEPS * 2 * IG:, :], 0.0).then_inc(s["a_const"], 1)
                    with p.Fori(0, STEPS // 2) as i:
                        for h in range(GB):
                            q = GB * i + h
                            p.wait_ge(s["a_scored"], q + 1)
                            p.sem_inc(s["a_seen"], 1)
                            p.tensor_copy(IX[:, h, :], SRCX[:, bass.ds(q * IG, IG)]).then_inc(s["a_ix"], 1)
                            p.wait_ge(s["a_ix"], q + 1)
                            p.sem_inc(s["a_seen"], 1)
                            for j in range(IG):
                                p.indirect_dma_start(out=G[:, h, j, :], out_offset=None, in_=xl_d,
                                                     in_offset=bass.IndirectOffsetOnAxis(ap=IX[:, h, j:j + 1], axis=0)).then_inc(s[f"a_g{h}"], 16)

                @block.tensor
                def _(pe):
                    with pe.Fori(0, STEPS // 2) as i:
                        for h in range(GB):
                            q = GB * i + h
                            ws = [pe.value_load(WI[0:1, bass.ds(q * IG + j, 1)], min_val=0, max_val=NW - 1) for j in range(IG)]
                            pe.wait_ge(s["a_summed"], q + 1)
                            pe.wait_ge(s["a_onehot"], q + 1)
                            pe.wait_ge(s[f"a_eat{h}"], 16 * i + 16)
                            pe.wait_ge(s[f"a_g{h}"], 64 * i + 64)
                            for j in range(IG):
                                o = pS[0:TE, h, j * D:(j + 1) * D]
                                pe.matmul(o, LT[:, h, j, :], XRW[:, bass.ds(ws[j], 1), :].rearrange("p a d -> p (a d)"), start=True, stop=False)
                                ins = pe.matmul(o, ident[0:TE, 0:TE], G[:, h, j, :], start=False, stop=True)
                            ins.then_inc(s["a_scored"], 1)
                    pe.wait_ge(s["a_alpha"], 2 * STEPS + 2)
                    pe.wait_ge(s["a_const"], 2)
                    for k in range(CH):
                        for hd in range(GH):
                            n = k * GH + hd
                            if n >= 2:
                                pe.wait_ge(s["a_at"], n - 1)
                            pe.transpose(pS[:, n % 2, 0:TE], AX_[:, k * 128:(k + 1) * 128, hd], ident[0:TE, 0:TE]).then_inc(s["a_ta"], 1)

                @block.scalar
                def _(a):
                    with a.Fori(0, STEPS // 2) as i:
                        for h in range(GB):
                            q = GB * i + h
                            a.wait_ge(s["a_scored"], q + GB + 1)
                            a.wait_ge(s["a_alpha"], q + 1)
                            a.activation(R[:, h % 2, :, :].rearrange("p i d -> p (i d)"), pS[0:TE, h, :], ACT.Copy, scale=SLOPE).then_inc(s["a_fifth"], 1)

                @block.vector
                def _(v):
                    for name, k in (("a_scored", GB), ("a_summed", GB), ("a_alpha", 2)):
                        v.sem_inc(s[name], k)
                    v.wait_ge(s["a_const"], 2)

                    def onehot(q, i, h):
                        v.wait_ge(s[f"a_db{h}"], 16 * i + 16)
                        v.tensor_scalar(LT[0:WN, h, :, :], DB[:, h, :, :], node[0:WN, 0:1], None, ALU.is_equal).then_inc(s["a_onehot"], 1)

                    def score(q, h):
                        r = R[:, h % 2, :, :]
                        flat = r.rearrange("p i d -> p (i d)")
                        v.wait_ge(s["a_fifth"], q + 1)
                        v.tensor_tensor(flat, flat, pS[0:TE, h, :], ALU.max).then_inc(s["a_summed"], 1)
                        v.wait_ge(s["a_summed"], q + GB + 1)
                        v.tensor_tensor(r, r, attb[0:TE, :].unsqueeze(1).broadcast_to([TE, IG, D]), ALU.mult).then_inc(s["a_times"], 1)
                        v.wait_ge(s["a_times"], q + 1)
                        v.sem_inc(s["a_seen_v"], 1)
                        v.tensor_reduce(AX_[:, bass.ds(q * IG, IG), :].rearrange("p i h -> p (i h)"),
                                        r.rearrange("p i (h d) -> p (i h) d", h=GH), AX.X, ALU.add).then_inc(s["a_alpha"], 1)

                    onehot(0, 0, 0)
                    onehot(1, 0, 1)
                    with v.Fori(0, STEPS // 2 - 1) as i:
                        for h in range(GB):
                            onehot(GB * i + h + 2, i + (h + 2) // GB, (h + 2) % GB)
                            score(GB * i + h, h)
                    for h in range(GB):
                        if h < 2:
                            onehot(2 * STEPS - GB + h + 2, STEPS // 2 - 1, h + 2)
                        score(2 * STEPS - GB + h, h)
                    for n in range(CH * GH):
                        v.wait_ge(s["a_ta"], n + 1)
                        v.tensor_copy(AT[:, n // GH, n % GH, :], pS[:, n % 2, 0:TE]).then_inc(s["a_at"], 1)

            with ExitStack() as c:
                def sb(name, shape, dt=F32):
                    return c.enter_context(nc.sbuf_tensor(name, shape, dt))

                A = sb("s_a", [128, GH, RUN])
                F = sb("s_f", [128, GH, RUN])
                B = sb("s_b", [128, GH, RUN])
                key = sb("s_key", [128, 3, RUN])
                edge = sb("s_edge", [128, 2, RUN])
                last = sb("s_last", [128, RUN])
                outside = sb("s_outside", [128, RUN])
                sums = sb("s_sums", [128, 4, GH])
                rows = sb("s_rows", [GH, 4, 128])
                state = sb("s_state", [GH, 2, 128])
                carry = sb("s_carry", [GH, 2, 128])
                init = sb("s_init", [128, 2, GH])
                PT = sb("s_pt", [128, 2, 2 * GH, TE])
                wf = sb("s_wf", [1, ITEMS // IG, IG])
                digit = sb("s_digit", [1, IG])
                wsum = sb("s_wsum", [1, ITEMS // IG])
                pR = c.enter_context(nc.psum_tensor("s_pR", [128, 4, 512], F32))
                pX = c.enter_context(nc.psum_tensor("s_pX", [128, 2, 512], F32))
                block = c.enter_context(nc.Block())

                @block.sync
                def _(sp):
                    for hd in range(GH):
                        sp.dma_start(A[:, hd, :].rearrange("p (k e) -> p k e", e=TE),
                                     al_d.rearrange("(p k) h e -> h p k e", p=128)[hd]).then_inc(s["s_in"], 16)
                    for n in range(3):
                        sp.dma_start(key[:, n, :], key_d[n:n + ITEMS * TE].rearrange("(p r) -> p r", p=128)).then_inc(s["s_in"], 16)
                    sp.wait_ge(s["s_p"], 1)
                    sp.wait_ge(s["s_cl"], 1)
                    view = pc_d.rearrange("(p k) c e -> c p k e", p=128)
                    for hd in range(GH):
                        sp.dma_start(view[hd], A[:, hd, :].rearrange("p (k e) -> p k e", e=TE)).then_inc(s["s_pc"], 16)
                        sp.dma_start(view[GH + hd], F[:, hd, :].rearrange("p (k e) -> p k e", e=TE)).then_inc(s["s_pc"], 16)
                    sp.wait_ge(s["s_pc"], 16 * 2 * GH)
                    for k in range(CH):
                        if k >= 2:
                            sp.wait_ge(s["s_x"], 2 * GH * (k - 1))
                        sp.dma_start(PT[:, k % 2, :, :], pc_d[k * 128:(k + 1) * 128, :, :]).then_inc(s[f"s_pt{k % 2}"], 16)

                @block.scalar
                def _(a):
                    a.wait_ge(s["s_diff"], 1)
                    a.activation(A[:, :, :], A[:, :, :], ACT.Exp).then_inc(s["s_p"], 1)

                @block.tensor
                def _(pe):
                    pe.wait_ge(s["s_sums"], 1)
                    for n in range(4):
                        ins = pe.transpose(pR[0:GH, n, 0:128], sums[:, n, :], ident[:, :])
                    ins.then_inc(s["s_rows"], 1)
                    pe.wait_ge(s["s_carry"], 1)
                    for n in range(2):
                        ins = pe.transpose(pR[:, n, 128:128 + GH], carry[:, n, :], ident[0:GH, 0:GH])
                    ins.then_inc(s["s_init"], 1)
                    for k in range(CH):
                        pe.wait_ge(s[f"s_pt{k % 2}"], 16 * (k // 2 + 1))
                        for q in range(2 * GH):
                            n = 2 * GH * k + q
                            if n >= 2:
                                pe.wait_ge(s["s_pcx"], n - 1)
                            pe.transpose(pX[0:TE, n % 2, 0:128], PT[:, k % 2, q, :], ident[:, :]).then_inc(s["s_x"], 1)

                @block.vector
                def _(v):
                    done = [0]

                    def then(ins):
                        done[0] += 1
                        ins.then_inc(s["s_chain"], 1)
                        v.wait_ge(s["s_chain"], done[0])

                    for j in range(IG):
                        v.memset(digit[:, j:j + 1], float(1 << (5 * j)))
                    then(v.tensor_copy(wf[:, :, :], WI[:, :].rearrange("p (n i) -> p n i", i=IG)))
                    then(v.tensor_tensor(wf[:, :, :], wf[:, :, :], digit[:, :].unsqueeze(1).broadcast_to([1, ITEMS // IG, IG]), ALU.mult))
                    then(v.tensor_reduce(wsum[:, :], wf[:, :, :], AX.X, ALU.add))
                    then(v.tensor_copy(WP[:, :], wsum[:, :]))
                    v.wait_ge(s["s_in"], 16 * (GH + 3))
                    v.tensor_tensor(edge[:, 0, :], key[:, 1, :], key[:, 0, :], ALU.not_equal)
                    v.tensor_tensor(last[:, :], key[:, 1, :], key[:, 2, :], ALU.not_equal)
                    then(v.tensor_scalar(outside[:, :], key[:, 1, :], 0.0, LOW, ALU.is_equal, ALU.mult))
                    v.tensor_scalar(edge[:, 0, :], edge[:, 0, :], LOW, None, ALU.mult)
                    v.tensor_scalar(edge[:, 1, :], last[:, :], LOW, None, ALU.mult)
                    then(v.tensor_tensor(A[:, :, :], A[:, :, :], outside[:, :].unsqueeze(1).broadcast_to([128, GH, RUN]), ALU.add))

                    def scans(initial):
                        for hd in range(GH):
                            v.tensor_tensor_scan(F[:, hd, :], edge[:, 0, :], A[:, hd, :], initial(0, hd), ALU.add, ALU.max)
                            ins = v.tensor_tensor_scan(B[:, hd, ::-1], edge[:, 1, ::-1], A[:, hd, ::-1], initial(1, hd), ALU.add, ALU.max)
                        then(ins)

                    scans(lambda n, hd: LOW)
                    v.tensor_copy(sums[:, 0, :], F[:, :, RUN - 1])
                    v.tensor_copy(sums[:, 1, :], B[:, :, 0])
                    v.tensor_reduce(sums[:, 2, 0:1], edge[:, 0, :], AX.X, ALU.min)
                    then(v.tensor_reduce(sums[:, 3, 0:1], edge[:, 1, :], AX.X, ALU.min))
                    for n in (2, 3):
                        ins = v.tensor_copy(sums[:, n, 1:GH], sums[:, n, 0:1].broadcast_to([128, GH - 1]))
                    ins.then_inc(s["s_sums"], 1)
                    v.wait_ge(s["s_rows"], 1)
                    then(v.tensor_copy(rows[:, :, :], pR[0:GH, :, 0:128]))
                    v.tensor_tensor_scan(state[:, 0, :], rows[:, 2, :], rows[:, 0, :], LOW, ALU.add, ALU.max)
                    v.tensor_tensor_scan(state[:, 1, ::-1], rows[:, 3, ::-1], rows[:, 1, ::-1], LOW, ALU.add, ALU.max)
                    then(v.memset(carry[:, :, :], LOW))
                    v.tensor_copy(carry[:, 0, 1:128], state[:, 0, 0:127])
                    v.tensor_copy(carry[:, 1, 0:127], state[:, 1, 1:128]).then_inc(s["s_carry"], 1)
                    v.wait_ge(s["s_init"], 1)
                    then(v.tensor_copy(init[:, :, :], pR[:, 0:2, 128:128 + GH]))
                    scans(lambda n, hd: init[:, n, hd:hd + 1])
                    then(v.tensor_tensor(F[:, :, :], F[:, :, :], B[:, :, :], ALU.max))
                    v.tensor_tensor(A[:, :, :], A[:, :, :], F[:, :, :], ALU.subtract).then_inc(s["s_diff"], 1)
                    v.wait_ge(s["s_diff"], 1)
                    v.tensor_tensor(F[:, :, :], F[:, :, :], last[:, :].unsqueeze(1).broadcast_to([128, GH, RUN]), ALU.mult).then_inc(s["s_cl"], 1)
                    for n in range(2 * GH * CH):
                        k, q = n // (2 * GH), n % (2 * GH)
                        v.wait_ge(s["s_x"], n + 1)
                        v.tensor_copy(PCX[:, k * 128:(k + 1) * 128, q], pX[0:TE, n % 2, 0:128]).then_inc(s["s_pcx"], 1)

            with ExitStack() as c:
                def sb(name, shape, dt=F32):
                    return c.enter_context(nc.sbuf_tensor(name, shape, dt))

                ACC = sb("b_acc", [WN, NW, MW])

                with ExitStack() as d:
                    G = d.enter_context(nc.sbuf_tensor("b_g", [TE, GB, IG, D], F32))
                    M = d.enter_context(nc.sbuf_tensor("b_m", [TE, 2, IG, MW], F32))
                    OH = d.enter_context(nc.sbuf_tensor("b_oh", [TE, 2, IG, WN], F32))
                    IX = d.enter_context(nc.sbuf_tensor("b_ix", [TE, GB, IG], I32))
                    node = d.enter_context(nc.sbuf_tensor("b_node", [TE, WN], F32))
                    pM = d.enter_context(nc.psum_tensor("b_pM", [128, 2, IG, 512], F32))
                    block = d.enter_context(nc.Block())

                    @block.sync
                    def _(sp):
                        sp.wait_ge(s["b_const"], 3)
                        with sp.Fori(0, STEPS) as i:
                            for h in range(2):
                                q = 2 * i + h
                                sp.wait_ge(s["b_summed"], q + 1)
                                sp.dma_start(M[:, h, :, EA0:EA0 + ED],
                                             ea_d[bass.ds(q * IG, IG), :].rearrange("i (e c) -> e i c", c=ED)).then_inc(s[f"b_ea{h}"], 16)

                    @block.gpsimd
                    def _(p):
                        p.iota(node[:, :], pattern=[[1, WN]], base=0, channel_multiplier=0, allow_small_or_imprecise_dtypes=True).then_inc(s["b_const"], 1)
                        p.memset(M[:, :, :, :], 1.0).then_inc(s["b_const"], 1)
                        p.memset(ACC[:, :, :], 0.0).then_inc(s["b_const"], 1)
                        with p.Fori(0, STEPS // 2) as i:
                            for h in range(GB):
                                q = GB * i + h
                                p.wait_ge(s["b_weighted"], q + 1)
                                p.sem_inc(s["b_seen"], 1)
                                p.wait_ge(s["b_weighted_a"], q + 1)
                                p.sem_inc(s["b_seen"], 1)
                                p.tensor_copy(IX[:, h, :], SRCX[:, bass.ds(q * IG, IG)]).then_inc(s["b_ix"], 1)
                                p.wait_ge(s["b_ix"], q + 1)
                                p.sem_inc(s["b_seen"], 1)
                                for j in range(IG):
                                    p.indirect_dma_start(out=G[:, h, j, :], out_offset=None, in_=xl_d,
                                                         in_offset=bass.IndirectOffsetOnAxis(ap=IX[:, h, j:j + 1], axis=0)).then_inc(s[f"b_g{h}"], 16)

                    @block.tensor
                    def _(pe):
                        with pe.Fori(0, STEPS) as i:
                            for h in range(2):
                                q = 2 * i + h
                                pe.wait_ge(s["b_weighted"], q + GB + 1)
                                pe.wait_ge(s["b_weighted_a"], q + GB + 1)
                                pe.wait_ge(s["b_acc"], IG * q + 1)
                                pe.wait_ge(s[f"b_ea{h}"], 16 * i + 16)
                                for j in range(IG):
                                    ins = pe.matmul(pM[0:WN, h, j, 0:MW], OH[:, h, j, :], M[:, h, j, :], start=True, stop=True)
                                ins.then_inc(s["b_summed"], 1)

                    @block.scalar
                    def _(a):
                        with a.Fori(0, STEPS // 2) as i:
                            for b in range(GB):
                                q, h = GB * i + b, b % 2
                                a.wait_ge(s["b_copied"], q + 1)
                                a.wait_ge(s[f"b_g{b}"], 64 * i + 64)
                                for j in range(BYV, IG):
                                    for hd in range(GH):
                                        part = slice(hd * (D // GH), (hd + 1) * (D // GH))
                                        ins = a.activation(M[:, h, j, part], G[:, b, j, part], ACT.Copy, scale=M[:, h, j, D + hd:D + hd + 1])
                                ins.then_inc(s["b_weighted_a"], 1)

                    @block.vector
                    def _(v):
                        for name, k in (("b_weighted", GB), ("b_weighted_a", GB), ("b_summed", 2), ("b_acc", 2 * IG)):
                            v.sem_inc(s[name], k)
                        v.wait_ge(s["b_const"], 3)

                        def weigh(q, i, b):
                            h = b % 2
                            v.wait_ge(s["b_summed"], q + 1)
                            v.sem_inc(s["b_seen_v"], 1)
                            at = bass.ds(q * IG, IG) if not isinstance(q, int) else slice(q * IG, q * IG + IG)
                            v.tensor_tensor(OH[:, h, :, :], node[:, :].unsqueeze(1).broadcast_to([TE, IG, WN]),
                                            DLX[:, at].unsqueeze(2).broadcast_to([TE, IG, WN]), ALU.is_equal)
                            v.tensor_copy(M[:, h, :, D:D + 2 * GH], PCX[:, at, :]).then_inc(s["b_copied"], 1)
                            v.wait_ge(s[f"b_g{b}"], 64 * i + 64)
                            for j in range(BYV):
                                one = bass.ds(q * IG + j, 1) if not isinstance(q, int) else slice(q * IG + j, q * IG + j + 1)
                                ins = v.tensor_tensor(M[:, h, j, 0:D].rearrange("p (h d) -> p h d", h=GH), G[:, b, j, :].rearrange("p (h d) -> p h d", h=GH),
                                                      PCX[:, one, 0:GH].rearrange("p a h -> p (a h)").unsqueeze(2).broadcast_to([TE, GH, D // GH]), ALU.mult)
                            ins.then_inc(s["b_weighted"], 1)

                        flat = ACC[:, :, :].rearrange("p w m -> p (w m)")

                        def add(q, h):
                            four = v.value_load(WP[0:1, (slice(q, q + 1) if isinstance(q, int) else bass.ds(q, 1))], min_val=0, max_val=(1 << (5 * IG)) - 1)
                            at = [v.snap(((four >> (5 * j)) & 31) * MW) for j in range(IG)]
                            before = [IG * q + j + 2 * IG for j in range(IG)]
                            if not isinstance(q, int):
                                before = [v.snap(n) for n in before]
                            v.wait_ge(s["b_summed"], q + 3)
                            for j in range(IG):
                                a = flat[:, bass.ds(at[j].with_bounds(min_val=0, max_val=(NW - 1) * MW), MW)]
                                v.wait_ge(s["b_acc"], before[j])
                                v.tensor_tensor(a, a, pM[0:WN, h, j, 0:MW], ALU.add).then_inc(s["b_acc"], 1)

                        weigh(0, 0, 0)
                        with v.Fori(0, STEPS // 2 - 1) as i:
                            for b in range(GB):
                                weigh(GB * i + b + 1, i + (b + 1) // GB, (b + 1) % GB)
                                add(GB * i + b, b % 2)
                        last = 2 * STEPS - GB
                        for b in range(GB - 1):
                            weigh(last + b + 1, STEPS // 2 - 1, b + 1)
                            add(last + b, b % 2)
                        add(2 * STEPS - 1, 1)

                deg1 = sb("e_deg1", [WN, NW])
                la = sb("e_la", [WN, NW, ED])
                laT = sb("e_laT", [ED, 2, WN])
                weT = sb("e_weT", [ED, D])
                S = sb("e_s", [WN, NW, D])
                T = XRW[0:WN, :, :]
                own = sb("e_own", [WN, NW, GH])
                none = sb("e_none", [WN, NW])
                cmax = sb("e_cmax", [WN, NW, GH])
                m = sb("e_m", [WN, NW, GH])
                e12 = sb("e_e12", [WN, 2, NW, GH])
                den = sb("e_den", [WN, NW, GH])
                bias = sb("e_bias", [WN, D])
                pL = c.enter_context(nc.psum_tensor("e_pL", [128, 2, 512], F32))
                pE = c.enter_context(nc.psum_tensor("e_pE", [128, 2, 512], F32))
                block = c.enter_context(nc.Block())

                @block.sync
                def _(sp):
                    sp.dma_start(weT[:, :], g["W_eT"]).then_inc(s["e_w"], 16)
                    sp.dma_start(bias[:, :], g["bias"].unsqueeze(0).broadcast_to([WN, D])).then_inc(s["e_w"], 16)
                    sp.wait_ge(s["e_silu"], 1)
                    sp.dma_start(sums_d.rearrange("(w p) d -> p w d", p=WN), S[:, :, :]).then_inc(s["e_stored"], 16)
                    sp.wait_ge(s["e_stored"], 16)

                @block.tensor
                def _(pe):
                    pe.wait_ge(s["e_la"], 1)
                    pe.wait_ge(s["e_w"], 32)
                    for w in range(NW):
                        if w >= 2:
                            pe.wait_ge(s["e_laT"], w - 1)
                        pe.transpose(pL[0:ED, w % 2, 0:WN], la[:, w, :], ident[0:WN, 0:WN]).then_inc(s["e_lt"], 1)
                        pe.wait_ge(s["e_laT"], w + 1)
                        if w >= 2:
                            pe.wait_ge(s["e_sum"], w - 1)
                        pe.matmul(pE[0:WN, w % 2, 0:D], laT[:, w % 2, :], weT[:, :], start=True, stop=True).then_inc(s["e_feat"], 1)

                @block.scalar
                def _(a):
                    a.wait_ge(s["e_less"], 1)
                    a.activation(e12[:, :, :, :], e12[:, :, :, :], ACT.Exp).then_inc(s["e_exp"], 1)
                    a.wait_ge(s["e_out"], 1)
                    a.activation(S[:, :, :], S[:, :, :], ACT.Silu).then_inc(s["e_silu"], 1)

                @block.vector
                def _(v):
                    done = [0]

                    def then(ins):
                        done[0] += 1
                        ins.then_inc(s["e_chain"], 1)
                        v.wait_ge(s["e_chain"], done[0])

                    heads = lambda a: a.rearrange("p w (h d) -> p (w h) d", h=GH)
                    spread = lambda a, n: a.rearrange("p w h -> p (w h)").unsqueeze(2).broadcast_to([WN, NW * GH, n])
                    deg = ACC[:, :, EA0 + ED]
                    v.tensor_scalar(none[:, :], deg, 0.0, LOW, ALU.is_equal, ALU.mult)
                    then(v.tensor_scalar(deg1[:, :], deg, 1.0, None, ALU.max))
                    then(v.reciprocal(deg1[:, :], deg1[:, :]))
                    v.tensor_tensor(la[:, :, :], ACC[:, :, EA0:EA0 + ED], deg1[:, :].unsqueeze(2).broadcast_to([WN, NW, ED]), ALU.mult).then_inc(s["e_la"], 1)
                    v.tensor_tensor(cmax[:, :, :], ACC[:, :, D + GH:D + 2 * GH], none[:, :].unsqueeze(2).broadcast_to([WN, NW, GH]), ALU.add)
                    for w in range(NW):
                        v.wait_ge(s["e_lt"], w + 1)
                        v.tensor_copy(laT[:, w % 2, :], pL[0:ED, w % 2, 0:WN]).then_inc(s["e_laT"], 1)
                        v.wait_ge(s["e_feat"], w + 1)
                        v.tensor_tensor(S[:, w, :], pE[0:WN, w % 2, 0:D], XL[:, w, :], ALU.add).then_inc(s["e_sum"], 1)
                    v.wait_ge(s["e_sum"], NW)
                    then(v.tensor_tensor(S[:, :, :], S[:, :, :], XRW[0:WN, :, :], ALU.add))
                    then(v.scalar_tensor_tensor(out=S[:, :, :], in0=S[:, :, :], scalar=SLOPE, in1=S[:, :, :], op0=ALU.mult, op1=ALU.max))
                    then(v.tensor_tensor(S[:, :, :], S[:, :, :], attb[0:WN, :].unsqueeze(1).broadcast_to([WN, NW, D]), ALU.mult))
                    then(v.tensor_reduce(own[:, :, :].rearrange("p w h -> p (w h)"), heads(S[:, :, :]), AX.X, ALU.add))
                    then(v.tensor_tensor(m[:, :, :], cmax[:, :, :], own[:, :, :], ALU.max))
                    v.tensor_tensor(e12[:, 0, :, :], cmax[:, :, :], m[:, :, :], ALU.subtract)
                    v.tensor_tensor(e12[:, 1, :, :], own[:, :, :], m[:, :, :], ALU.subtract).then_inc(s["e_less"], 1)
                    v.wait_ge(s["e_exp"], 1)
                    then(v.tensor_tensor(den[:, :, :], ACC[:, :, D:D + GH], e12[:, 0, :, :], ALU.mult))
                    then(v.tensor_tensor(den[:, :, :], den[:, :, :], e12[:, 1, :, :], ALU.add))
                    then(v.tensor_scalar(den[:, :, :], den[:, :, :], 1e-16, None, ALU.add))
                    then(v.reciprocal(den[:, :, :], den[:, :, :]))
                    v.tensor_tensor(e12[:, 0, :, :], e12[:, 0, :, :], den[:, :, :], ALU.mult)
                    then(v.tensor_tensor(e12[:, 1, :, :], e12[:, 1, :, :], den[:, :, :], ALU.mult))
                    for w in range(NW):
                        hd = lambda a: a.rearrange("p (h d) -> p h d", h=GH)
                        by = lambda n: e12[:, n, w, :].unsqueeze(2).broadcast_to([WN, GH, D // GH])
                        v.tensor_tensor(hd(S[:, w, :]), hd(ACC[:, w, 0:D]), by(0), ALU.mult)
                        ins = v.tensor_tensor(hd(T[:, w, :]), hd(XL[:, w, :]), by(1), ALU.mult)
                    then(ins)
                    then(v.tensor_tensor(S[:, :, :], S[:, :, :], T[:, :, :], ALU.add))
                    v.wait_ge(s["e_w"], 32)
                    v.tensor_tensor(S[:, :, :], S[:, :, :], bias[:, :].unsqueeze(1).broadcast_to([WN, NW, D]), ALU.add).then_inc(s["e_out"], 1)


UN = 2 * P
UNITS = -(-NT // 2)
FIRST = 6
BS = 256
BLOCKS = (2 * N + EXPERTS * (BS - 1)) // BS
THRS = -(-N // BS)
TOTAL = UNITS + BLOCKS
SHARED = EXPERTS


def experts(nc, s, XS, ident, w, out, xg_d, y_d):
    with ExitStack() as c:
        def sb(name, shape, dt=F32):
            return c.enter_context(nc.sbuf_tensor(name, shape, dt))

        def ps(name, shape):
            return c.enter_context(nc.psum_tensor(name, shape, F32))

        HT = sb("f_ht", [128, KC, N])
        NR = sb("f_nr", [P, NT, D])
        w2 = sb("f_w2", [128, (EXPERTS + 1) * FC, D])
        w1 = sb("f_w1", [128, 2, KC, FF])
        b1 = sb("f_b1", [128, 2, FC])
        b2 = sb("f_b2", [128, 2, D])
        HID = sb("f_hid", [128, 2, FC, BS])
        XG = sb("f_xg", [128, 2, 2, D])
        XGT = sb("f_xgt", [128, 2, KC, BS])
        Y = sb("f_y", [128, 2, 2, D])
        zero = sb("f_zero", [128, D])
        wr = sb("f_wr", [128, KC, EXPERTS])
        lower = sb("f_lower", [P, P])
        ones = sb("f_ones", [P, P])
        st = sb("f_st", [P, GT, 6])
        mv = sb("f_mv", [P, GT, 2])
        ve = sb("f_ve", [P, GT])
        rstd = sb("f_rstd", [P, GT])
        mhalf = sb("f_mhalf", [P, GT])
        lane = sb("f_lane", [P, EXPERTS])
        thr = sb("f_thr", [P, THRS])
        bnum = sb("f_bnum", [P, BLOCKS])
        rw = sb("f_rw", [P, NT, EXPERTS])
        rmax = sb("f_rmax", [P, NT])
        rsum = sb("f_rsum", [P, NT])
        rrec = sb("f_rrec", [P, NT])
        top = sb("f_top", [P, NT, 8])
        topi = sb("f_topi", [P, NT, 8], U32)
        topf = sb("f_topf", [P, NT, 8])
        pick = sb("f_pick", [P, 2, NT, EXPERTS])
        mask = sb("f_mask", [P, NT, EXPERTS])
        tot = sb("f_tot", [P, NT, EXPERTS])
        upto = sb("f_upto", [P, NT, EXPERTS])
        rank = sb("f_rank", [P, NT, EXPERTS])
        over = sb("f_over", [P, EXPERTS, THRS])
        nb = sb("f_nb", [P, EXPERTS])
        nbi = sb("f_nbi", [P, EXPERTS])
        base = sb("f_base", [P, EXPERTS])
        before = sb("f_before", [P, BLOCKS, EXPERTS])
        eb = sb("f_eb", [P, 2, BLOCKS])
        table = sb("f_table", [P, 2, BLOCKS], I32)
        pos = sb("f_pos", [P, 2, NT])
        posi = sb("f_posi", [P, 2, NT], I32)
        gate = sb("f_gate", [P, 2, NT])
        pH = ps("f_pH", [128, 4, 512])
        pO = ps("f_pO", [128, 2, 512])
        pT = ps("f_pT", [128, 2, 512])
        Y1 = w2[0:P, 0:NT, :]

        block = c.enter_context(nc.Block())

        def unit_step(u):
            return u if u < FIRST else u + BLOCKS

        def tiles_of(u):
            return range(2 * u, min(2 * u + 2, NT))

        def steps(eng, unit, blk):
            for u in range(FIRST):
                unit(u)
            with eng.Fori(0, BLOCKS // 2) as i:
                for h in range(2):
                    blk(2 * i + h, h)
            for u in range(FIRST, UNITS):
                unit(u)

        @block.sync
        def _(sp):
            def load(slot, W1, B1, B2):
                sp.dma_start(w1[:, slot, :, :], chunked(W1)).then_inc(s[f"f_w{slot}"], 16)
                sp.dma_start(b1[:, slot, :], B1).then_inc(s[f"f_w{slot}"], 16)
                sp.dma_start(b2[:, slot, :], B2.unsqueeze(0).broadcast_to([128, D])).then_inc(s[f"f_w{slot}"], 16)

            def free(G):
                sp.wait_ge(s["f_gelu"], FC * G - FC + 4)
                sp.sem_inc(s["f_seen"], 1)
                sp.wait_ge(s["f_drained"], 2 * G)

            sp.dma_start(wr[:, :, :], chunked(w["Wr"])).then_inc(s["f_small"], 16)
            load(1, w["W1s"], w["b1s"], w["b2s"])
            sp.dma_start(w2[:, SHARED * FC:, :], chunked(w["W2s"])).then_inc(s["f_w2s"], 16)
            for e in range(EXPERTS):
                sp.dma_start(w2[:, e * FC:(e + 1) * FC, :], chunked(w["W2p"][e])).then_inc(s["f_w2p"], 16)
            sp.wait_ge(s["f_table"], 1)
            with sp.Fori(0, BLOCKS // 2) as i:
                for h in range(2):
                    b = 2 * i + h
                    e = sp.value_load(table[0:1, 0, bass.ds(b, 1)], min_val=0, max_val=EXPERTS - 1)
                    free(FIRST + b)
                    sp.sem_inc(s["f_seen"], 1)
                    load(h, picked(w["W1p"], e), picked(w["b1p"], e), picked(w["b2p"], e))
            free(FIRST + BLOCKS)
            load(0, w["W1s"], w["b1s"], w["b2s"])
            rows = out.rearrange("(t p) d -> p t d", p=P)
            for g in range(NG):
                sp.wait_ge(s["f_done"], GT * (g + 1))
                sp.dma_start(rows[:, g * GT:(g + 1) * GT, :], XS[:, g * GT:(g + 1) * GT, :]).then_inc(s["f_stored"], 16)
            sp.wait_ge(s["f_stored"], 16 * NG)

        @block.gpsimd
        def _(p):
            p.memset(mhalf[:, :], -0.5).then_inc(s["f_const"], 1)
            p.memset(ones[:, :], 1.0).then_inc(s["f_const"], 1)
            p.memset(zero[:, :], 0.0).then_inc(s["f_const"], 1)
            p.iota(lane[:, :], pattern=[[1, EXPERTS]], base=0, channel_multiplier=0,
                   allow_small_or_imprecise_dtypes=True).then_inc(s["f_const"], 1)
            p.iota(thr[:, :], pattern=[[BS, THRS]], base=0, channel_multiplier=0,
                   allow_small_or_imprecise_dtypes=True).then_inc(s["f_const"], 1)
            p.iota(bnum[:, :], pattern=[[1, BLOCKS]], base=0, channel_multiplier=0,
                   allow_small_or_imprecise_dtypes=True).then_inc(s["f_const"], 1)
            p.wait_ge(s["f_const"], 6)
            p.affine_select(out=lower[:, :], in_=ones[:, :], compare_op=ALU.is_ge, fill=0.0, base=-1,
                            pattern=[[1, P]], channel_multiplier=-1).then_inc(s["f_const"], 1)
            p.dma_start(xg_d.rearrange("(c p) d -> p c d", p=128),
                        zero[:, :].unsqueeze(1).broadcast_to([128, BLOCKS * BS // 128, D])).then_inc(s["f_zeroed"], 16)
            for n in range(NG):
                rstd_side(p, s, "f_ln", n, ve, rstd, mhalf)
            p.wait_ge(s["f_zeroed"], 16)
            p.wait_ge(s["f_posi"], 1)
            for t in range(NT):
                for k in range(2):
                    p.indirect_dma_start(out=xg_d, out_offset=bass.IndirectOffsetOnAxis(ap=posi[:, k, t:t + 1], axis=0),
                                         in_=NR[:, t, :], in_offset=None).then_inc(s["f_scattered"], 16)
            p.wait_ge(s["f_scattered"], 32 * NT)
            blocks = xg_d.rearrange("(b c p) d -> b p c d", p=128, c=2)
            outs = y_d.rearrange("(b c p) d -> b p c d", p=128, c=2)
            at = lambda a, b: a[b] if isinstance(b, int) else a[bass.ds(b, 1)].rearrange("a p c d -> (a p) c d")

            def fetch(b, h):
                p.wait_ge(s["f_xgt"], b + 1)
                p.dma_start(XG[:, h, :, :], at(blocks, b)).then_inc(s[f"f_xg{h}"], 16)

            def store(b, h):
                p.wait_ge(s["f_drained"], 2 * (FIRST + b) + 4)
                p.dma_start(at(outs, b), Y[:, h, :, :]).then_inc(s[f"f_y{h}"], 16)

            fetch(0, 0)
            fetch(1, 1)
            with p.Fori(0, BLOCKS // 2 - 1) as i:
                for h in range(2):
                    fetch(2 * i + 2 + h, h)
                    store(2 * i + h, h)
            store(BLOCKS - 2, 0)
            store(BLOCKS - 1, 1)
            for h in range(2):
                p.wait_ge(s[f"f_y{h}"], 16 * (BLOCKS // 2))
            for t in range(NT):
                for k, rows in enumerate((NR, Y1)):
                    p.indirect_dma_start(out=rows[:, t, :], out_offset=None, in_=y_d,
                                         in_offset=bass.IndirectOffsetOnAxis(ap=posi[:, k, t:t + 1], axis=0)).then_inc(s[f"f_mine{t // GT}"], 16)

        @block.tensor
        def _(pe):
            pL = pH[:, 0:3, :].rearrange("p b (j q) -> p (b j) q", q=128)
            for g in range(NG):
                pe.wait_ge(s["f_ln_out"], GT * (g + 1))
                if g:
                    pe.wait_ge(s["f_t_out"], g)
                for k in range(KC):
                    for j in range(GT):
                        ins = pe.transpose(pL[:, GT * k + j, 0:P], NR[:, GT * g + j, k * 128:(k + 1) * 128], ident[0:P, 0:P])
                ins.then_inc(s["f_t_full"], 1)
            pe.wait_ge(s["f_t_out"], NG)
            pe.wait_ge(s["f_small"], 16)
            for t in range(NT):
                for k in range(KC):
                    ins = pe.matmul(pT[0:P, 0, t * EXPERTS:(t + 1) * EXPERTS], HT[:, k, t * P:(t + 1) * P], wr[:, k, :],
                                    start=(k == 0), stop=(k == KC - 1))
            ins.then_inc(s["f_logits"], 1)

            def hidden(G, slot, n, x):
                for f in range(FC):
                    pe.wait_ge(s["f_gelu"], FC * G + f + 1)
                    for k in range(KC):
                        ins = pe.matmul(pH[:, f % 4, 0:n], w1[:, slot, k, f * 128:(f + 1) * 128], x(k),
                                        start=(k == 0), stop=(k == KC - 1))
                    ins.then_inc(s["f_hid"], 1)

            def hidden_unit(u, slot):
                at, n = u * UN, P * len(tiles_of(u))
                hidden(unit_step(u), slot, n, lambda k: HT[:, k, at:at + n])

            def hidden_block(b, h):
                pe.wait_ge(s["f_xgt"], b + 3)
                if h:
                    pe.wait_ge(s["f_w1"], 24 * b + 72)
                else:
                    pe.wait_ge(s["f_w0"], 24 * b + 48)
                hidden(FIRST + b, h, BS, lambda k: XGT[:, h, k, :])

            def rows(G, hid, tiles, m, second):
                pe.wait_ge(s["f_gelu"], FC * G + FC + 4)
                for j in range(tiles):
                    pe.wait_ge(s["f_drained"], 2 * G + j + 1)
                    for f in range(FC):
                        ins = pe.matmul(pO[0:m, j, 0:D], HID[:, hid, f, j * m:(j + 1) * m], second(f), start=(f == 0), stop=(f == FC - 1))
                    ins.then_inc(s["f_rows"], 1)

            def rows_unit(u):
                rows(unit_step(u), unit_step(u) % 2, len(tiles_of(u)), P, lambda f: w2[:, SHARED * FC + f, :])

            def rows_block(b, h):
                e8 = pe.value_load(table[0:1, 1, (slice(b, b + 1) if isinstance(b, int) else bass.ds(b, 1))],
                                   min_val=0, max_val=(EXPERTS - 1) * FC)
                rows(FIRST + b, h, 2, 128, lambda f: w2[:, bass.ds(e8 + f, 1), :].rearrange("p a d -> p (a d)"))

            def turn(b, h):
                pe.wait_ge(s["f_xgt"], b + 1)
                pe.wait_ge(s[f"f_xg{h}"], (8 * b + 16) if h == 0 else (8 * b + 8))
                for k in range(KC):
                    for r in range(2):
                        ins = pe.transpose(pT[:, h, (2 * k + r) * 128:(2 * k + r + 1) * 128],
                                           XG[:, h, r, k * 128:(k + 1) * 128], ident[:, :])
                ins.then_inc(s["f_turned"], 1)

            pe.wait_ge(s["f_w1"], 48)
            hidden_unit(0, 1)
            hidden_unit(1, 1)
            pe.wait_ge(s["f_mask"], 1)
            pe.wait_ge(s["f_const"], 7)
            picked_of = mask[:, :, :].rearrange("p t e -> p (t e)")
            for n, m in enumerate((lower, ones)):
                ins = pe.matmul(pT[0:P, 1, n * NT * EXPERTS:(n + 1) * NT * EXPERTS], m[:, :], picked_of, start=True, stop=True)
            ins.then_inc(s["f_counts"], 1)
            pe.wait_ge(s["f_w2s"], 16)
            rows_unit(0)
            for u in range(2, FIRST):
                hidden_unit(u, 1)
                rows_unit(u - 1)
            pe.wait_ge(s["f_table"], 1)
            turn(0, 0)
            rows_unit(FIRST - 1)
            pe.wait_ge(s["f_w2p"], 16 * EXPERTS)
            hidden_block(0, 0)
            turn(1, 1)
            with pe.Fori(0, BLOCKS // 2 - 1) as i:
                for h in range(2):
                    b = 2 * i + h
                    hidden_block(b + 1, 1 - h)
                    turn(b + 2, h)
                    rows_block(b, h)
            hidden_block(BLOCKS - 1, 1)
            rows_block(BLOCKS - 2, 0)
            pe.wait_ge(s["f_w0"], 24 * BLOCKS + 48)
            hidden_unit(FIRST, 0)
            rows_block(BLOCKS - 1, 1)
            for u in range(FIRST + 1, UNITS):
                hidden_unit(u, 0)
                rows_unit(u - 1)
            rows_unit(UNITS - 1)

        @block.scalar
        def _(a):
            a.wait_ge(s["f_lsub"], 1)
            a.activation(rw[:, :, :], rw[:, :, :], ACT.Exp).then_inc(s["f_rexp"], 1)

            def gelus(G, slot, hid, n):
                if not (isinstance(G, int) and G < 2):
                    a.wait_ge(s["f_rows"], 2 * G - 2)
                for f in range(FC):
                    a.wait_ge(s["f_hid"], FC * G + f + 1)
                    a.activation(HID[:, hid, f, 0:n], pH[:, f % 4, 0:n], ACT.Gelu, bias=b1[:, slot, f:f + 1]).then_inc(s["f_gelu"], 1)

            def unit(u):
                G = unit_step(u)
                gelus(G, 1 if u < FIRST else 0, G % 2, P * len(tiles_of(u)))

            steps(a, unit, lambda b, h: gelus(FIRST + b, h, h, BS))

        @block.vector
        def _(v):
            done = [0]

            def then(ins):
                done[0] += 1
                ins.then_inc(s["f_chain"], 1)
                v.wait_ge(s["f_chain"], done[0])

            v.sem_inc(s["f_gelu"], 4)
            v.sem_inc(s["f_drained"], 2)
            v.sem_inc(s["f_xgt"], 2)
            for g in range(NG):
                layer_norm(v, s, "f_ln", g, lambda j: XS[:, g * GT + j, :], lambda j: NR[:, g * GT + j, :], st, mv, ve, rstd)
                v.wait_ge(s["f_t_full"], g + 1)
                for k in range(KC):
                    pL = pH[:, 0:3, :].rearrange("p b (j q) -> p (b j) q", q=128)
                    ins = v.tensor_copy(HT[:, k, g * GN:(g + 1) * GN].rearrange("p (j q) -> p j q", j=GT),
                                        pL[:, GT * k:GT * k + GT, 0:P])
                ins.then_inc(s["f_t_out"], 1)

            def spread(x):
                return x.unsqueeze(2).broadcast_to([P, NT, EXPERTS])

            v.wait_ge(s["f_logits"], 1)
            logits = pT[0:P, 0, 0:NT * EXPERTS].rearrange("p (t e) -> p t e", t=NT)
            then(v.tensor_reduce(rmax[:, :], logits, AX.X, ALU.max))
            v.tensor_tensor(rw[:, :, :], logits, spread(rmax[:, :]), ALU.subtract).then_inc(s["f_lsub"], 1)
            v.wait_ge(s["f_rexp"], 1)
            then(v.tensor_reduce(rsum[:, :], rw[:, :, :], AX.X, ALU.add))
            then(v.reciprocal(rrec[:, :], rsum[:, :]))
            then(v.tensor_tensor(rw[:, :, :], rw[:, :, :], spread(rrec[:, :]), ALU.mult))
            for t in range(NT):
                ins = v.max(top[:, t, :], rw[:, t, :])
            then(ins)
            for t in range(NT):
                ins = v.max_index(topi[:, t, :], top[:, t, :], rw[:, t, :])
            then(ins)
            v.tensor_tensor(rsum[:, :], top[:, :, 0], top[:, :, 1], ALU.add)
            then(v.tensor_copy(topf[:, :, :], topi[:, :, :]))
            v.wait_ge(s["f_const"], 7)
            lanes = lane[:, :].unsqueeze(1).broadcast_to([P, NT, EXPERTS])
            for n in range(2):
                ins = v.tensor_tensor(pick[:, n, :, :], lanes, spread(topf[:, :, n]), ALU.is_equal)
            then(ins)
            v.tensor_tensor(mask[:, :, :], pick[:, 0, :, :], pick[:, 1, :, :], ALU.add).then_inc(s["f_mask"], 1)
            then(v.reciprocal(rrec[:, :], rsum[:, :]))
            for n in range(2):
                v.tensor_tensor(gate[:, n, :], top[:, :, n], rrec[:, :], ALU.mult)

            v.wait_ge(s["f_counts"], 1)
            size = NT * EXPERTS
            counted = lambda n: pT[0:P, 1, n * size:(n + 1) * size].rearrange("p (t e) -> p t e", t=NT)
            then(v.tensor_copy(tot[:, :, :], counted(1)))
            for e in range(EXPERTS):
                ins = v.tensor_tensor_scan(upto[:, :, e], zero[0:P, 0:NT], tot[:, :, e], 0.0, ALU.add, ALU.add)
            then(ins)
            then(v.tensor_tensor(over[:, :, :], upto[:, NT - 1, :].unsqueeze(2).broadcast_to([P, EXPERTS, THRS]),
                                 thr[:, :].unsqueeze(1).broadcast_to([P, EXPERTS, THRS]), ALU.is_gt))
            then(v.tensor_reduce(nb[:, :], over[:, :, :], AX.X, ALU.add))
            then(v.tensor_tensor_scan(nbi[:, :], zero[0:P, 0:EXPERTS], nb[:, :], 0.0, ALU.add, ALU.add))
            then(v.tensor_tensor(base[:, :], nbi[:, :], nb[:, :], ALU.subtract))
            v.tensor_scalar(base[:, :], base[:, :], float(BS), None, ALU.mult)
            then(v.tensor_tensor(rank[:, :, :], upto[:, :, :], tot[:, :, :], ALU.subtract))
            then(v.tensor_tensor(rank[:, :, :], rank[:, :, :], counted(0), ALU.add))
            then(v.tensor_tensor(rank[:, :, :], rank[:, :, :], base[:, :].unsqueeze(1).broadcast_to([P, NT, EXPERTS]), ALU.add))
            for n in range(2):
                ins = v.tensor_tensor(pick[:, n, :, :], pick[:, n, :, :], rank[:, :, :], ALU.mult)
            then(ins)
            then(v.tensor_reduce(pos[:, :, :], pick[:, :, :, :], AX.X, ALU.add))
            v.tensor_copy(posi[:, :, :], pos[:, :, :]).then_inc(s["f_posi"], 1)
            then(v.tensor_tensor(before[:, :, :], nbi[:, :].unsqueeze(1).broadcast_to([P, BLOCKS, EXPERTS]),
                                 bnum[:, :].unsqueeze(2).broadcast_to([P, BLOCKS, EXPERTS]), ALU.is_le))
            then(v.tensor_reduce(eb[:, 0, :], before[:, :, :], AX.X, ALU.add))
            then(v.tensor_scalar(eb[:, 0, :], eb[:, 0, :], float(EXPERTS - 1), None, ALU.min))
            then(v.tensor_scalar(eb[:, 1, :], eb[:, 0, :], float(FC), None, ALU.mult))
            v.tensor_copy(table[:, :, :], eb[:, :, :]).then_inc(s["f_table"], 1)

            v.wait_ge(s["f_w1"], 48)
            then(v.tensor_tensor(XS[:, :, :], XS[:, :, :], b2[0:P, 1, :].unsqueeze(1).broadcast_to([P, NT, D]), ALU.add))

            def xgt(b, h):
                v.wait_ge(s["f_turned"], b + 1)
                v.wait_ge(s["f_hid"], FC * (FIRST + b - 1))
                v.tensor_copy(XGT[:, h, :, :].rearrange("p k n -> p (k n)"), pT[:, h, :]).then_inc(s["f_xgt"], 1)

            def unit_rows(u):
                G = unit_step(u)
                for j, t in enumerate(tiles_of(u)):
                    v.wait_ge(s["f_rows"], 2 * G + j + 1)
                    v.tensor_tensor(XS[:, t, :], XS[:, t, :], pO[0:P, j, 0:D], ALU.add).then_inc(s["f_drained"], 1)

            def block_rows(b, h):
                if not isinstance(b, int) or b >= 2:
                    v.wait_ge(s[f"f_y{h}"], (8 * b) if h == 0 else (8 * b - 8))
                for j in range(2):
                    v.wait_ge(s["f_rows"], 2 * (FIRST + b) + j + 1)
                    v.tensor_tensor(Y[:, h, j, :], pO[:, j, 0:D], b2[:, h, :], ALU.add).then_inc(s["f_drained"], 1)

            for u in range(FIRST - 1):
                unit_rows(u)
            xgt(0, 0)
            unit_rows(FIRST - 1)
            xgt(1, 1)
            xgt(2, 0)
            block_rows(0, 0)
            xgt(3, 1)
            block_rows(1, 1)
            with v.Fori(1, BLOCKS // 2 - 1) as i:
                for h in range(2):
                    xgt(2 * i + h + 2, h)
                    block_rows(2 * i + h, h)
            block_rows(BLOCKS - 2, 0)
            block_rows(BLOCKS - 1, 1)
            for u in range(FIRST, UNITS):
                unit_rows(u)
            v.wait_ge(s["f_drained"], 2 * TOTAL + 1)
            for t in range(NT):
                v.wait_ge(s[f"f_mine{t // GT}"], 32 * GT)
                for k, rows in enumerate((NR, Y1)):
                    ins = v.scalar_tensor_tensor(out=XS[:, t, :], in0=rows[:, t, :], scalar=gate[:, k, t:t + 1], in1=XS[:, t, :],
                                                 op0=ALU.mult, op1=ALU.add)
                    if k == 0:
                        ins.then_inc(s["f_half"], 1)
                        v.wait_ge(s["f_half"], t + 1)
                ins.then_inc(s["f_done"], 1)


def add_branches(nc, s, XS, x, xn_d, sums_d):
    with ExitStack() as c:
        parts = [c.enter_context(nc.sbuf_tensor(f"c_{n}", [P, NT, D], F32)) for n in ("x", "xn", "g")]
        block = c.enter_context(nc.Block())

        @block.sync
        def _(sp):
            for n, a in enumerate((x, xn_d, sums_d[0:N, :])):
                sp.dma_start(parts[n][:, :, :], a.rearrange("(t p) d -> p t d", p=P)).then_inc(s[f"c_part{n}"], 16)

        @block.vector
        def _(v):
            for n in range(3):
                v.wait_ge(s[f"c_part{n}"], 16)
                if n:
                    v.wait_ge(s["c_added"], n)
                v.tensor_tensor(XS[:, :, :], XS[:, :, :], parts[n][:, :, :], ALU.add).then_inc(s["c_added"], 1)


def gps_layer(nc, a, out):
    with ExitStack() as c:
        XS = c.enter_context(nc.sbuf_tensor("XS", [P, NT, D], F32))
        ident = c.enter_context(nc.sbuf_tensor("ident", [128, 128], F32))
        dram = lambda n, shape, dt=F32: nc.dram_tensor(n, shape, dt).ap()
        xn_d = dram("xn_d", (N, D))
        sums_d = dram("sums_d", (NW * WN, D))
        scratch = {"key": dram("key_d", (ITEMS * TE + 2,)), "dl": dram("dl_d", (ITEMS, TE)),
                   "eat": dram("eat_d", (ITEMS, ED * TE)), "ea": dram("ea_d", (ITEMS, ED * TE)),
                   "xl": dram("xl_d", (NW * WN, D)), "al": dram("al_d", (ITEMS, GH, TE)),
                   "pc": dram("pc_d", (ITEMS, 2 * GH, TE)), "wl": dram("wl_d", (ITEMS,), I32)}
        xg_d, y_d = dram("xg_d", (BLOCKS * BS, D)), dram("y_d", (BLOCKS * BS, D))
        s = Names(nc)
        with nc.Block() as block:
            @block.gpsimd
            def _(p):
                p.memset(ident[:, :], 0.0).then_inc(s["const"], 1)
                p.wait_ge(s["const"], 1)
                p.affine_select(out=ident[:, :], in_=ident[:, :], compare_op=ALU.not_equal, fill=1.0, base=0,
                                pattern=[[-1, 128]], channel_multiplier=1).then_inc(s["const"], 1)
                p.wait_ge(s["const"], 2)
        part = lambda prefix: {n[len(prefix):]: v for n, v in a.items() if n.startswith(prefix)}
        s.give_back()
        for stage in (lambda s: graph_attention(nc, s, XS, ident, a["x"], xn_d, part("gnn_"), sums_d, scratch),
                      lambda s: mixer(nc, s, XS, ident, part("mix_")),
                      lambda s: add_branches(nc, s, XS, a["x"], xn_d, sums_d),
                      lambda s: experts(nc, s, XS, ident, part("ffn_"), out, xg_d, y_d)):
            s = Names(nc)
            stage(s)
            s.give_back()


def laid_out(inputs):
    a = {n: np.asarray(v) for n, v in inputs.items()}
    ea = a["edge_attr_16"].reshape(NTE, TE, ED)
    src, dst = (a[n].reshape(NTE, TE) for n in ("src", "dst"))
    d = {"x": a["x"], "gnn_src": src, "gnn_dst": dst, "gnn_dstT": dst.T, "gnn_ea": ea.reshape(NTE, -1),
         "gnn_eaT": ea.transpose(0, 2, 1).reshape(NTE, -1)}
    for n in ("W_l", "W_r", "W_e"):
        d[f"gnn_{n}T"] = a[f"L0_gnn_{n}"].T
    for n in ("b_l", "b_r", "att", "bias"):
        d[f"gnn_{n}"] = a[f"L0_gnn_{n}"]
    for n in ("Wq", "Wk", "Wv", "Wo", "bo", "W1", "W2", "b2"):
        d[f"mix_{n}"] = a[f"L0_mix_{n}"]
    for n in ("ln1_g", "ln1_b", "b1", "ln2_g", "ln2_b"):
        d[f"mix_{n}"] = columns(a[f"L0_mix_{n}"])
    for n in ("Wr", "W1s", "W2s", "b2s", "W1p", "W2p", "b2p"):
        d[f"ffn_{n}"] = a[f"L0_ffn_{n}"]
    for n in ("b1s", "b1p"):
        d[f"ffn_{n}"] = columns(a[f"L0_ffn_{n}"])
    return {n: np.ascontiguousarray(v) for n, v in d.items()}


def kernel(**inputs):
    import concourse.bacc as bacc
    from concourse.bass_utils import run_bass_kernel_spmd

    nc = bacc.Bacc("TRN2", target_bir_lowering=False, num_devices=1)
    arrays, args = {}, {}
    for name, v in laid_out(inputs).items():
        arrays[f"in_{name}"] = v
        args[name] = nc.dram_tensor(f"in_{name}", v.shape, mybir.dt.from_np(v.dtype), kind="ExternalInput").ap()
    out = nc.dram_tensor("out", (N, D), F32, kind="ExternalOutput").ap()
    gps_layer(nc, args, out)
    return run_bass_kernel_spmd(nc, [arrays], core_ids=[0]).results[0]["out"]
```

```python
from contextlib import ExitStack

import numpy as np

import concourse.bass as bass
from concourse import mybir

F32 = mybir.dt.float32
I32 = mybir.dt.int32
U32 = mybir.dt.uint32
ALU = mybir.AluOpType
ACT = mybir.ActivationFunctionType
AX = mybir.AxisListType

N, D = 3125, 256
P = 125
NT = N // P
GT = 5
NG = NT // GT
GN = GT * P
KC = D // 128
HALVES = ((0, 313), (313, 312))
DEPTH = 4
EXPERTS = 8

E, ED = 100000, 16
TE = 125
NTE = E // TE
WN = 112
NW = -(-N // WN)
GH = 4
IG = 4
STEPS = 2 * -(-(NTE + NW - 1) // (4 * IG))
GB = 4
BYV = 3
CH = -(-(2 * IG * STEPS) // 128)
ITEMS = 128 * CH
RUN = CH * TE
EA0 = D + 2 * GH
MW = EA0 + ED + 1
SLOPE = 0.2
LOW = -1.0e30
MH, MD = 8, 32
FF = 1024
FC = FF // 128
QK_SCALE = float(MD) ** -0.25
EPS = 1e-5
LOWEST = -3.0e38


class Names:

    def __init__(self, nc):
        self._nc, self._all = nc, {}

    def __getitem__(self, name):
        if name not in self._all:
            self._all[name] = self._nc.alloc_semaphore(name=name)
        return self._all[name]

    def give_back(self):
        self._nc.clear_and_free_semaphores(list(self._all.values()))
        self._nc.all_engine_barrier()


def chunked(w):
    return w.rearrange("(k p) n -> p k n", p=128)


def columns(v):
    v = np.asarray(v)
    return np.ascontiguousarray(np.swapaxes(v.reshape(v.shape[:-1] + (-1, 128)), -1, -2))


def layer_norm(v, s, tag, n, src, dst, st, mv, ve, rstd):
    v.sem_inc(s[tag + "_seen"], 1)
    for j in range(GT):
        v.bn_stats(st[:, j, :], src(j)).then_inc(s[tag + "_stats"], 1)
    v.wait_ge(s[tag + "_stats"], GT * n + GT)
    v.sem_inc(s[tag + "_seen"], 1)
    for j in range(GT):
        v.bn_aggr(mv[:, j, :], st[:, j, :]).then_inc(s[tag + "_aggr"], 1)
    v.wait_ge(s[tag + "_aggr"], GT * n + GT)
    v.tensor_scalar(ve[:, :], mv[:, :, 1], EPS, None, ALU.add).then_inc(s[tag + "_vareps"], 1)
    v.wait_ge(s[tag + "_rstd"], n + 1)
    for j in range(GT):
        v.tensor_scalar(dst(j), src(j), mv[:, j, 0:1], rstd[:, j:j + 1],
                        ALU.subtract, ALU.mult).then_inc(s[tag + "_out"], 1)


def rstd_side(p, s, tag, n, ve, rstd, mhalf):
    p.wait_ge(s[tag + "_vareps"], n + 1)
    p.tensor_tensor(rstd[:, :], ve[:, :], mhalf[:, :], ALU.pow).then_inc(s[tag + "_rstd"], 1)


def all_stats(v, s, tag, src, st, mv, ve, ready=None):
    for t in range(NT):
        if ready and t % GT == 0:
            ready(t // GT)
        v.bn_stats(st[:, t, :], src(t)).then_inc(s[tag + "_stats"], 1)
    v.wait_ge(s[tag + "_stats"], NT)
    for t in range(NT):
        v.bn_aggr(mv[:, t, :], st[:, t, :]).then_inc(s[tag + "_aggr"], 1)
    v.wait_ge(s[tag + "_aggr"], NT)
    v.tensor_scalar(ve[:, :], mv[:, :, 1], EPS, None, ALU.add).then_inc(s[tag + "_vareps"], 1)
    v.wait_ge(s[tag + "_rstd"], 1)


def normalised(v, s, tag, g, src, dst, mv, rstd):
    for t in range(g * GT, (g + 1) * GT):
        v.tensor_scalar(dst(t), src(t), mv[:, t, 0:1], rstd[:, t:t + 1], ALU.subtract, ALU.mult).then_inc(s[tag + "_out"], 1)


def row(x, g, j):
    return x[:, g * GT + j, :] if isinstance(g, int) else x[:, bass.ds(g * GT + j, 1), :].rearrange("p a d -> p (a d)")


def picked(a, l):
    if isinstance(l, int):
        return a[l]
    return a[bass.ds(l, 1)].rearrange("a b c -> (a b) c" if len(a.shape) == 3 else "a b -> (a b)")


def mixer(nc, s, XS, ident, w, xg_d, x, xn_d, sums_d, xx_d):
    with ExitStack() as c:
        def sb(name, shape, dt=F32):
            return c.enter_context(nc.sbuf_tensor(name, shape, dt))

        def ps(name, shape):
            return c.enter_context(nc.psum_tensor(name, shape, F32))

        KK = sb("m_kk", [P, NT, D])
        VV = sb("m_vv", [P, NT, D])
        HT = sb("m_ht", [128, KC, N])
        H2 = sb("m_h2", [128, KC, GN])
        N2 = sb("m_n2", [P, GT, D])
        HID = sb("m_hid", [128, FC, GN])
        QE = sb("m_qe", [P, 2, GT, D])
        QN = sb("m_qn", [P, GT, D])
        wqkv = sb("m_wqkv", [128, KC, 3 * D])
        wo = sb("m_wo", [128, KC, D])
        w1 = sb("m_w1", [128, KC, FF])
        w2 = sb("m_w2", [128, FC, D])
        ln1 = sb("m_ln1", [128, 2, KC])
        ln2 = sb("m_ln2", [128, 2, KC])
        b1 = sb("m_b1", [128, FC])
        bias = sb("m_bias", [P, 2, D])
        ones = sb("m_ones", [128, 128])
        st = sb("m_st", [P, GT, 6])
        mv = sb("m_mv", [P, GT, 2])
        ve = sb("m_ve", [P, GT])
        rstd = sb("m_rstd", [P, GT])
        mhalf = sb("m_mhalf", [P, NT])
        st0 = sb("m_st0", [P, NT, 6])
        mv0 = sb("m_mv0", [P, NT, 2])
        ve0 = sb("m_ve0", [P, NT])
        rstd0 = sb("m_rstd0", [P, NT])
        zero = sb("m_zero", [128, D])
        parts = sb("m_parts", [P, 3, GT, D])
        qmax = sb("m_qmax", [P, GT, MH])
        qsum = sb("m_qsum", [P, GT * MH])
        qrec = sb("m_qrec", [P, GT * MH])
        KM = sb("m_kmax", [P, D])
        KG = sb("m_kgroup", [P, D])
        KS = sb("m_ksum", [P, GT, D])
        kcol = sb("m_kcol", [128, KC])
        kdiag = sb("m_kdiag", [128, KC, 128])
        CT = sb("m_ct", [128, KC, 128])
        rk = sb("m_rk", [128, KC])
        MO = sb("m_mo", [128, KC, D])
        pH = ps("m_pH", [128, 4, 512])
        pO0 = ps("m_pO0", [128, 512])
        pT = ps("m_pT", [128, 12, 128])
        pO = (pO0[:, 0:D], pT[:, 10:12, :].rearrange("p a b -> p (a b)"))

        block = c.enter_context(nc.Block())

        PER_T, PER_O = 15, 52
        FILL_Q = (4, 6, 7, 8, 9)
        FILL_LN1 = (0, 1, 2, 3, 5)
        T2 = lambda l, g: PER_T * l + 10 + g
        OUT_FIRST, OUT_LAST = 2, 47
        OUT_ATTN = lambda g: 7 + 10 * g
        OUT_MLP = lambda g: 12 + 10 * g
        KM_STEPS = NG + 1
        ATTN_DMAS, FF_DMAS = 7, 6

        @block.sync
        def _(sp):
            def load_attn(l):
                for i, name in enumerate(("Wq", "Wk", "Wv")):
                    sp.dma_start(wqkv[:, :, i * D:(i + 1) * D], chunked(picked(w[name], l))).then_inc(s["m_attn_w"], 16)
                sp.dma_start(wo[:, :, :], chunked(picked(w["Wo"], l))).then_inc(s["m_attn_w"], 16)
                sp.dma_start(ln1[:, 0, :], picked(w["ln1_g"], l)).then_inc(s["m_attn_w"], 16)
                sp.dma_start(ln1[:, 1, :], picked(w["ln1_b"], l)).then_inc(s["m_attn_w"], 16)
                sp.dma_start(bias[:, 0, :], picked(w["bo"], l).unsqueeze(0).broadcast_to([P, D])).then_inc(s["m_attn_w"], 16)

            def load_ff(l):
                sp.dma_start(w1[:, :, :], chunked(picked(w["W1"], l))).then_inc(s["m_ff_w"], 16)
                sp.dma_start(w2[:, :, :], chunked(picked(w["W2"], l))).then_inc(s["m_ff_w"], 16)
                sp.dma_start(ln2[:, 0, :], picked(w["ln2_g"], l)).then_inc(s["m_ff_w"], 16)
                sp.dma_start(ln2[:, 1, :], picked(w["ln2_b"], l)).then_inc(s["m_ff_w"], 16)
                sp.dma_start(b1[:, :], picked(w["b1"], l)).then_inc(s["m_ff_w"], 16)
                sp.dma_start(bias[:, 1, :], picked(w["b2"], l).unsqueeze(0).broadcast_to([P, D])).then_inc(s["m_ff_w"], 16)

            load_attn(0)
            load_ff(0)
            with sp.Fori(0, DEPTH - 1) as l:
                sp.wait_ge(s["m_o_out"], PER_O * l + OUT_ATTN(NG - 2) + GT + 2)
                load_attn(l + 1)
                sp.wait_ge(s["m_o_out"], PER_O * l + PER_O + 2)
                load_ff(l + 1)

        @block.gpsimd
        def _(p):
            p.memset(mhalf[:, :], -0.5).then_inc(s["m_const"], 1)
            p.memset(ones[:, :], 1.0).then_inc(s["m_const"], 1)
            p.memset(CT[:, :, :], 0.0).then_inc(s["m_const"], 1)
            p.memset(zero[:, :], 0.0).then_inc(s["m_zero"], 1)
            p.wait_ge(s["m_const"], 3)
            rstd_side(p, s, "m_ln0", 0, ve0, rstd0, mhalf)
            p.wait_ge(s["m_zero"], 1)
            p.dma_start(xg_d.rearrange("(c p) d -> p c d", p=128),
                        zero[:, :].unsqueeze(1).broadcast_to([128, xg_d.shape[0] // 128, D])).then_inc(s["m_zeroed"], 16)
            for g in range(NG):
                group = lambda a: a[g * GN:(g + 1) * GN, :].rearrange("(t p) d -> p t d", p=P)
                if g:
                    p.wait_ge(s["m_xx"], 16 * g)
                for n, a in enumerate((x, xn_d, sums_d)):
                    p.dma_start(parts[:, n, :, :], group(a)).then_inc(s["m_parts"], 16)
                p.wait_ge(s["m_parts"], 48 * (g + 1))
                p.tensor_tensor(parts[:, 0, :, :], parts[:, 0, :, :], parts[:, 1, :, :], ALU.add).then_inc(s["m_sum"], 1)
                p.wait_ge(s["m_sum"], 2 * g + 1)
                p.tensor_tensor(parts[:, 0, :, :], parts[:, 0, :, :], parts[:, 2, :, :], ALU.add).then_inc(s["m_sum"], 1)
                p.wait_ge(s["m_sum"], 2 * g + 2)
                p.dma_start(group(xx_d), parts[:, 0, :, :]).then_inc(s["m_xx"], 16)
            p.wait_ge(s["m_xx"], 16 * NG)
            with p.Fori(0, DEPTH) as l:
                for g in range(1, NG):
                    p.wait_ge(s["m_kexp"], NG * l + g + 1)
                    if g > 1:
                        p.wait_ge(s["m_ks"], (NG - 1) * l + g - 1)
                    p.tensor_tensor(KS[:, :, :], KK[:, 0:GT, :] if g == 1 else KS[:, :, :], KK[:, g * GT:(g + 1) * GT, :], ALU.add).then_inc(s["m_ks"], 1)
                with p.Fori(0, 2 * NG) as n:
                    rstd_side(p, s, "m_ln", 2 * NG * l + n, ve, rstd, mhalf[:, 0:GT])
            p.wait_ge(s["m_zeroed"], 16)

        @block.tensor
        def _(pe):
            def cols(g, j):
                return slice((g * GT + j) * P, (g * GT + j + 1) * P) if isinstance(g, int) else bass.ds((g * GT + j) * P, P)

            def transposes(n, src, ready, count, outs):
                pe.wait_ge(s[ready], count)
                pe.wait_ge(s["m_t_out"], n + 1)
                pe.wait_ge(s["m_o_out"], outs + 2)
                for k in range(KC):
                    for j in range(GT):
                        ins = pe.transpose(pT[:, GT * k + j, 0:P], src(j)[:, k * 128:(k + 1) * 128], ident[0:P, 0:P])
                ins.then_inc(s["m_t_full"], 1)

            def qkv(l, g, tiles):
                for j in tiles:
                    t = NT * l + g * GT + j
                    b = 2 * ((g * GT + j) % 2)
                    pe.wait_ge(s["m_qkv_act"], t + (g == 0 and j == 0))
                    pe.wait_ge(s["m_qkv_dve"], t + (g == 0 and j == 0))
                    for k in range(KC):
                        pe.matmul(pH[0:P, b, 0:256], HT[:, k, cols(g, j)], wqkv[:, k, 0:256], start=(k == 0), stop=(k == KC - 1))
                    for k in range(KC):
                        ins = pe.matmul(pH[0:P, b + 1, 0:512], HT[:, k, cols(g, j)], wqkv[:, k, 256:768],
                                        start=(k == 0), stop=(k == KC - 1))
                    ins.then_inc(s["m_qkv_full"], 1)

            def context(l, g, first, last):
                pe.wait_ge(s["m_kexp"], NG * l + g + 1)
                for j in range(GT):
                    f, e = first and j == 0, last and j == GT - 1
                    k_, v_ = row(KK, g, j), row(VV, g, j)
                    for m in range(KC):
                        half = slice(m * 128, (m + 1) * 128)
                        pe.matmul(pH[:, m, 0:128], v_[:, half], k_[:, half], start=f, stop=e)
                if last:
                    pe.wait_ge(s["m_ks"], (NG - 1) * l + NG - 1)
                    for m in range(KC):
                        for j in range(GT):
                            ins = pe.matmul(pH[:, 2 + m, 0:1], KS[:, j, m * 128:(m + 1) * 128], ones[0:P, 0:1], start=(j == 0), stop=(j == GT - 1))
                    ins.then_inc(s["m_ctx"], 1)

            def out_rows(l, base, parity, lhs, rhs, chunks, t_out):
                for j in range(GT):
                    o = pO[(j + parity) % 2][0:P, :]
                    if (j + parity) % 2:
                        pe.wait_ge(s["m_t_out"], t_out + 1)
                    pe.wait_ge(s["m_o_out"], PER_O * l + base + j + 1)
                    for k in range(chunks):
                        ins = pe.matmul(o, lhs(k, j), rhs[:, k, :], start=(k == 0), stop=(k == chunks - 1))
                    ins.then_inc(s["m_o_full"], 1)

            def attn_out(l, g, base, parity):
                t_out = PER_T * l + FILL_Q[4] + 1 if g < 2 else T2(l, g - 1) + 1
                out_rows(l, base, parity, lambda k, j: HT[:, k, cols(g, j)], MO, KC, t_out)

            def mlp_out(l, g, base, parity):
                pe.wait_ge(s["m_gelu"], FC * (NG * l + g) + FC + 2)
                out_rows(l, base, parity, lambda k, j: HID[:, k, j * P:(j + 1) * P], w2, FC,
                         T2(l, min(g + 1, NG - 1)) + 1)

            def hidden(l, g):
                pe.wait_ge(s["m_t_out"], T2(l, g) + 2)
                for f in range(FC):
                    b = 2 * (f % 2)
                    pe.wait_ge(s["m_gelu"], FC * (NG * l + g) + f + 1)
                    for h, (at, n) in enumerate(HALVES):
                        for k in range(KC):
                            ins = pe.matmul(pH[:, b + h, 0:n], w1[:, k, f * 128:(f + 1) * 128], H2[:, k, at:at + n],
                                            start=(k == 0), stop=(k == KC - 1))
                    ins.then_inc(s["m_hid"], 1)

            pe.wait_ge(s["m_const"], 3)
            with pe.Fori(0, DEPTH) as l:
                pe.wait_ge(s["m_attn_w"], 16 * ATTN_DMAS * l + 16 * ATTN_DMAS)
                def ln1_turned(g):
                    transposes(PER_T * l + FILL_LN1[g], lambda j: row(KK, g, j), "m_ln_out", 50 * l + 25, PER_O * l)

                def q_turned(g):
                    transposes(PER_T * l + FILL_Q[g], lambda j: QN[:, j, :], "m_qn", NG * l + g + 1, PER_O * l)

                ln1_turned(0)
                ln1_turned(1)
                for g in range(NG):
                    qkv(l, g, (0, 1))
                    if g + 2 < NG:
                        ln1_turned(g + 2)
                    qkv(l, g, (2, 3))
                    if g:
                        q_turned(g - 1)
                    qkv(l, g, (4,))

                pe.wait_ge(s["m_kmax"], KM_STEPS * l + NG + 1)
                for k in range(KC):
                    ins = pe.transpose(pO0[:, k * 128:k * 128 + P], KM[:, k * 128:(k + 1) * 128], ident[0:P, 0:P])
                ins.then_inc(s["m_kturned"], 1)
                pe.wait_ge(s["m_kdiag"], KC * l + KC)
                for k in range(KC):
                    ins = pe.matmul(pO0[0:P, 256 + k * 128:256 + (k + 1) * 128], ones[:, 0:P], kdiag[:, k, :], start=True, stop=True)
                ins.then_inc(s["m_kmax_rows"], 1)

                pe.wait_ge(s["m_qkv_act"], NT * l + NT + 1)
                pe.wait_ge(s["m_qkv_dve"], NT * l + NT + 1)
                for g in range(NG):
                    if g == NG - 1:
                        q_turned(4)
                    context(l, g, g == 0, g == NG - 1)
                pe.wait_ge(s["m_ct"], 8 * l + 8)
                pe.wait_ge(s["m_t_out"], PER_T * l + FILL_Q[4] + 2)
                pe.wait_ge(s["m_ksub"], NG * l + NG)
                for m in range(KC):
                    pe.wait_ge(s["m_o_out"], PER_O * l + m + 1)
                    pe.matmul(pO[m], CT[:, m, :], wo[:, m, :], start=True, stop=True).then_inc(s["m_o_full"], 1)
                pe.wait_ge(s["m_o_out"], PER_O * l + 4)

                attn_out(l, 0, OUT_FIRST, 0)
                attn_out(l, 1, OUT_ATTN(0), 1)
                transposes(T2(l, 0), lambda j: N2[:, j, :], "m_ln_out", 50 * l + 30, PER_O * l + OUT_ATTN(0) + GT)
                pe.wait_ge(s["m_ff_w"], 16 * FF_DMAS * l + 16 * FF_DMAS)
                for g in range(NG - 1):
                    if g:
                        attn_out(l, g + 1, OUT_ATTN(g), 1)
                    hidden(l, g)
                    transposes(T2(l, g + 1), lambda j: N2[:, j, :], "m_ln_out", 50 * l + 10 * g + 35, PER_O * l + OUT_ATTN(g) + GT)
                    mlp_out(l, g, OUT_MLP(g), 0)
                hidden(l, NG - 1)
                mlp_out(l, NG - 1, OUT_LAST, 1)

        @block.scalar
        def _(a):
            with a.Fori(0, DEPTH) as l:
                for g in range(NG):
                    for j in range(GT):
                        b = 2 * ((g * GT + j) % 2)
                        a.wait_ge(s["m_qkv_full"], NT * l + g * GT + j + 1)
                        a.activation(row(KK, g, j), pH[0:P, b + 1, 0:256], ACT.Copy)
                        a.activation(row(VV, g, j), pH[0:P, b + 1, 256:512], ACT.Copy).then_inc(s["m_qkv_act"], 1)
                    a.wait_ge(s["m_qkv_dve"], NT * l + g * GT + GT + 1)
                    a.activation(QE[:, g % 2, :, :], QE[:, g % 2, :, :], ACT.Exp, scale=QK_SCALE).then_inc(s["m_qexp"], 1)
                with a.Fori(0, NG) as g:
                    a.wait_ge(s["m_ksub"], NG * l + g + 1)
                    kg = KK[:, bass.ds(g * GT, GT), :]
                    a.activation(kg, kg, ACT.Exp, scale=QK_SCALE).then_inc(s["m_kexp"], 1)
                a.wait_ge(s["m_ff_w"], 16 * FF_DMAS * l + 16 * FF_DMAS)
                with a.Fori(0, NG) as g:
                    a.wait_ge(s["m_o_full"], PER_O * l + 10 * g + 7)
                    for f in range(FC):
                        b = 2 * (f % 2)
                        a.wait_ge(s["m_hid"], FC * (NG * l + g) + f + 1)
                        for h, (at, n) in enumerate(HALVES):
                            ins = a.activation(HID[:, f, at:at + n], pH[:, b + h, 0:n], ACT.Gelu, bias=b1[:, f:f + 1])
                        ins.then_inc(s["m_gelu"], 1)

        @block.vector
        def _(v):
            def norm(n, src, dst):
                layer_norm(v, s, "m_ln", n, src, dst, st, mv, ve, rstd)

            def out_transposed(n, dst, ln=None):
                v.wait_ge(s["m_t_full"], n + 1)
                for k in range(KC):
                    o = dst(k).rearrange("p (j q) -> p j q", j=GT)
                    i = pT[:, GT * k:GT * k + GT, 0:P]
                    if ln is None:
                        ins = v.tensor_copy(o, i)
                    else:
                        ins = v.tensor_scalar(o, i, ln[:, 0, k:k + 1], ln[:, 1, k:k + 1], ALU.mult, ALU.add)
                ins.then_inc(s["m_t_out"], 1)

            def group_cols(g):
                return lambda k: HT[:, k, g * GN:(g + 1) * GN] if isinstance(g, int) else HT[:, k, bass.ds(g * GN, GN)]

            def q_tile(l, g, j):
                t = NT * l + g * GT + j
                b = 2 * ((g * GT + j) % 2)
                v.wait_ge(s["m_qkv_full"], t + 1)
                q = pH[0:P, b, 0:256].rearrange("p (h d) -> p h d", h=MH)
                v.tensor_reduce(qmax[:, j, :], q, AX.X, ALU.max).then_inc(s["m_qmax"], 1)
                v.wait_ge(s["m_qmax"], t + 1)
                v.tensor_tensor(QE[:, g % 2, j, :].rearrange("p (h d) -> p h d", h=MH), q,
                                qmax[:, j, :].unsqueeze(2).broadcast_to([P, MH, MD]), ALU.subtract).then_inc(s["m_qkv_dve"], 1)

            def k_max(l, g):
                v.wait_ge(s["m_qkv_act"], NT * l + g * GT + GT + 1)
                kg = KK[:, g * GT:(g + 1) * GT, :] if isinstance(g, int) else KK[:, bass.ds(g * GT, GT), :]
                v.tensor_reduce(KG[:, :], kg.rearrange("p j d -> p d j"), AX.X, ALU.max).then_inc(s["m_kgroup"], 1)
                v.wait_ge(s["m_kgroup"], NG * l + g + 1)
                v.wait_ge(s["m_kmax"], KM_STEPS * l + g + 1)
                v.tensor_tensor(KM[:, :], KM[:, :], KG[:, :], ALU.max).then_inc(s["m_kmax"], 1)

            def q_exp(g):
                return QE[:, g % 2, :, :].rearrange("p j (h d) -> p (j h) d", h=MH)

            def q_sum(l, g):
                v.wait_ge(s["m_qexp"], NG * l + g + 1)
                v.tensor_reduce(qsum[:, :], q_exp(g), AX.X, ALU.add).then_inc(s["m_qsum"], 1)
                v.wait_ge(s["m_qsum"], NG * l + g + 1)
                v.reciprocal(qrec[:, :], qsum[:, :]).then_inc(s["m_qrec"], 1)

            def q_norm(l, g):
                v.wait_ge(s["m_qrec"], NG * l + g + 1)
                v.tensor_tensor(QN[:, :, :].rearrange("p j (h d) -> p (j h) d", h=MH), q_exp(g),
                                qrec[:, :].unsqueeze(2).broadcast_to([P, GT * MH, MD]), ALU.mult).then_inc(s["m_qn"], 1)

            def add_rows(l, g, base, parity, which, n):
                x = XS[:, g * GT:(g + 1) * GT, :] if isinstance(g, int) else XS[:, bass.ds(g * GT, GT), :]
                v.tensor_tensor(x, x, bias[:, which, :].unsqueeze(1).broadcast_to([P, GT, D]), ALU.add).then_inc(s["m_biased"], 1)
                v.wait_ge(s["m_biased"], 2 * NG * l + n + 1)
                v.sem_inc(s["m_bias_seen"], 1)
                for j in range(GT):
                    v.wait_ge(s["m_o_full"], PER_O * l + base + j + 1)
                    x = row(XS, g, j)
                    v.tensor_tensor(x, x, pO[(j + parity) % 2][0:P, :], ALU.add).then_inc(s["m_o_out"], 1)

            def norm_after(l, g, n, base, dst):
                v.wait_ge(s["m_o_out"], PER_O * l + base + GT + 2)
                norm(n, lambda j: row(XS, g, j), dst)

            for name, k in (("m_t_out", 1), ("m_o_out", 2), ("m_gelu", 2), ("m_qkv_act", 1), ("m_qkv_dve", 1)):
                v.sem_inc(s[name], k)
            all_stats(v, s, "m_ln0", lambda t: XS[:, t, :], st0, mv0, ve0)
            for g in range(NG):
                normalised(v, s, "m_ln0", g, lambda t: XS[:, t, :], lambda t: KK[:, t, :], mv0, rstd0)
            v.wait_ge(s["m_ln0_out"], NT)
            v.sem_inc(s["m_ln_out"], NT)
            with v.Fori(0, DEPTH) as l:
                v.wait_ge(s["m_attn_w"], 16 * ATTN_DMAS * l + 16 * ATTN_DMAS)
                v.memset(KM[:, :], LOWEST).then_inc(s["m_kmax"], 1)
                out_transposed(PER_T * l + FILL_LN1[0], group_cols(0), ln1)
                out_transposed(PER_T * l + FILL_LN1[1], group_cols(1), ln1)
                for g in range(NG):
                    q_tile(l, g, 0)
                    if g:
                        k_max(l, g - 1)
                    q_tile(l, g, 1)
                    if g:
                        q_sum(l, g - 1)
                    if g + 2 < NG:
                        out_transposed(PER_T * l + FILL_LN1[g + 2], group_cols(g + 2), ln1)
                    q_tile(l, g, 2)
                    if g:
                        q_norm(l, g - 1)
                    q_tile(l, g, 3)
                    if g:
                        out_transposed(PER_T * l + FILL_Q[g - 1], group_cols(g - 1))
                    q_tile(l, g, 4)
                k_max(l, 4)
                v.wait_ge(s["m_kturned"], l + 1)
                v.tensor_reduce(kcol[:, :], pO0[:, 0:D].rearrange("p (k n) -> p k n", k=KC)[:, :, 0:P], AX.X, ALU.max).then_inc(s["m_kcol"], 1)
                v.wait_ge(s["m_kcol"], l + 1)
                for k in range(KC):
                    v.tensor_scalar(kdiag[:, k, :], ident[:, :], kcol[:, k:k + 1], None, ALU.mult).then_inc(s["m_kdiag"], 1)
                v.wait_ge(s["m_kmax_rows"], l + 1)
                v.wait_ge(s["m_qkv_act"], NT * l + NT + 1)
                v.sem_inc(s["m_k_seen"], 1)
                kmax_rows = pO0[0:P, 256:512].unsqueeze(1).broadcast_to([P, GT, D])
                with v.Fori(0, NG) as g:
                    kg = KK[:, bass.ds(g * GT, GT), :]
                    v.tensor_tensor(kg, kg, kmax_rows, ALU.subtract).then_inc(s["m_ksub"], 1)
                q_sum(l, 4)
                q_norm(l, 4)
                out_transposed(PER_T * l + FILL_Q[4], group_cols(4))

                v.wait_ge(s["m_ctx"], l + 1)
                v.reciprocal(rk[:, :], pH[:, 2:4, 0]).then_inc(s["m_rk"], 1)
                for m in range(KC):
                    for b in range(4):
                        r = slice(32 * b, 32 * b + 32)
                        v.tensor_copy(CT[r, m, 32 * b:32 * b + 32], pH[r, m, 32 * b:32 * b + 32]).then_inc(s["m_ct"], 1)
                v.wait_ge(s["m_rk"], l + 1)
                for m in range(KC):
                    v.wait_ge(s["m_o_full"], PER_O * l + m + 1)
                    v.tensor_scalar(MO[:, m, :], pO[m], rk[:, m:m + 1], None, ALU.mult).then_inc(s["m_o_out"], 1)

                v.wait_ge(s["m_ff_w"], 16 * FF_DMAS * l + 16 * FF_DMAS)
                to_n2, to_h2 = (lambda j: N2[:, j, :]), (lambda k: H2[:, k, :])
                add_rows(l, 0, OUT_FIRST, 0, 0, 0)
                norm_after(l, 0, 10 * l, OUT_FIRST, to_n2)
                add_rows(l, 1, OUT_ATTN(0), 1, 0, 1)
                out_transposed(T2(l, 0), to_h2, ln2)

                def ln1_after(g):
                    norm_after(l, g, 10 * l + 2 * g + 2, OUT_MLP(g), lambda j: row(KK, g, j))

                def ff_group(g, first):
                    if not first:
                        add_rows(l, g + 1, OUT_ATTN(g), 1, 0, 2 * g + 1)
                        ln1_after(g - 1)
                    norm_after(l, g + 1, 10 * l + 2 * g + 1, OUT_ATTN(g), to_n2)
                    out_transposed(T2(l, g + 1), to_h2, ln2)
                    add_rows(l, g, OUT_MLP(g), 0, 1, 2 * g + 2)

                ff_group(0, True)
                with v.Fori(1, NG - 1) as g:
                    ff_group(g, False)
                ln1_after(NG - 2)
                add_rows(l, NG - 1, OUT_LAST, 1, 1, 2 * NG - 1)
                norm_after(l, NG - 1, 10 * l + 9, OUT_LAST, lambda j: row(KK, NG - 1, j))


def graph_attention(nc, s, XS, ident, x, xn_d, g, sums_d, scratch):
    key_d, dl_d, eat_d, ea_d, xl_d, al_d, pc_d, wl_d = (scratch[n] for n in ("key", "dl", "eat", "ea", "xl", "al", "pc", "wl"))
    with ExitStack() as keep:
        def kept(name, shape, dt=F32):
            return keep.enter_context(nc.sbuf_tensor(name, shape, dt))

        XL = kept("g_xl", [WN, NW, D])
        XRW = kept("g_xr", [128, NW, D])
        SRCX = kept("g_srcx", [TE, ITEMS], I32)
        DLX = kept("g_dlx", [TE, ITEMS])
        WI = kept("g_wi", [1, ITEMS], I32)
        WP = kept("g_wp", [1, ITEMS // IG], I32)
        attb = kept("g_attb", [128, D])

        with ExitStack() as c:
            XT = c.enter_context(nc.sbuf_tensor("p_xt", [128, KC, NW * WN], F32))
            wlr = c.enter_context(nc.sbuf_tensor("p_wlr", [128, KC, 2 * D], F32))
            blr = c.enter_context(nc.sbuf_tensor("p_blr", [WN, 2 * D], F32))
            st = c.enter_context(nc.sbuf_tensor("p_st", [P, NT, 6], F32))
            mv = c.enter_context(nc.sbuf_tensor("p_mv", [P, NT, 2], F32))
            ve = c.enter_context(nc.sbuf_tensor("p_ve", [P, NT], F32))
            rstd = c.enter_context(nc.sbuf_tensor("p_rstd", [P, NT], F32))
            mhalf = c.enter_context(nc.sbuf_tensor("p_mhalf", [P, NT], F32))
            pT = c.enter_context(nc.psum_tensor("p_pT", [128, 12, 128], F32))
            pP = c.enter_context(nc.psum_tensor("p_pP", [128, 2, 512], F32))

            def sb(name, shape, dt=F32):
                return c.enter_context(nc.sbuf_tensor(name, shape, dt))

            ends_i = sb("i_ends_i", [NW, 2, NTE], I32)
            ends = sb("i_ends", [NW, 2, NTE])
            below = sb("i_below", [NW, 2, NTE])
            wbase = sb("i_wbase", [NW, 2])
            counts = sb("i_counts", [NW, 2])
            nitems = sb("i_nitems", [NW, 1])
            wide = sb("i_wide", [NW, 2, 128])
            one28 = sb("i_one28", [NW, 128])
            upto = sb("i_upto", [NW, NW])
            inum = sb("i_inum", [128, CH])
            lane = sb("i_lane", [128, NW])
            tab = sb("i_tab", [128, 3, NW])
            shift = sb("i_shift", [128, NW])
            cmp = sb("i_cmp", [128, CH, NW])
            wv = sb("i_wv", [128, CH])
            tile_f = sb("i_tile_f", [128, CH])
            tile_i = sb("i_tile_i", [128, CH], I32)
            base = sb("i_base", [128, CH])
            wc_i = sb("i_wc_i", [128, CH], I32)
            src_i = sb("i_src_i", [128, CH, TE], I32)
            dst_i = sb("i_dst_i", [128, CH, TE], I32)
            src_f = sb("i_src_f", [128, CH, TE])
            dst_f = sb("i_dst_f", [128, CH, TE])
            dl = sb("i_dl", [128, CH, TE])
            ok = sb("i_ok", [128, 2, CH, TE])
            eaT = sb("i_eaT", [128, 2, ED * TE])
            ea = sb("i_ea", [128, 2, ED * TE])
            edge = sb("i_edge", [1, 2])
            pN = c.enter_context(nc.psum_tensor("i_pN", [128, 512], F32))
            pX = c.enter_context(nc.psum_tensor("i_pX", [128, 2, 512], F32))
            block = c.enter_context(nc.Block())

            @block.sync
            def _(sp):
                sp.dma_start(ends_i[:, 0, :], g["dstT"][0:1, :].broadcast_to([NW, NTE])).then_inc(s["i_ends"], 16)
                sp.dma_start(ends_i[:, 1, :], g["dstT"][TE - 1:TE, :].broadcast_to([NW, NTE])).then_inc(s["i_ends"], 16)
                for q in range(NG):
                    sp.dma_start(XS[:, q * GT:(q + 1) * GT, :], x[q * GN:(q + 1) * GN, :].rearrange("(t p) d -> p t d", p=P)).then_inc(s[f"p_x{q}"], 16)
                sp.dma_start(wlr[:, :, 0:D], chunked(g["W_lT"])).then_inc(s["p_w"], 16)
                sp.dma_start(wlr[:, :, D:], chunked(g["W_rT"])).then_inc(s["p_w"], 16)
                sp.dma_start(blr[:, 0:D], g["b_l"].unsqueeze(0).broadcast_to([WN, D])).then_inc(s["p_w"], 16)
                sp.dma_start(blr[:, D:], g["b_r"].unsqueeze(0).broadcast_to([WN, D])).then_inc(s["p_w"], 16)
                sp.dma_start(attb[:, :], g["att"].rearrange("h d -> (h d)").unsqueeze(0).broadcast_to([128, D])).then_inc(s["p_att"], 16)
                sp.dma_start(XRW[WN:128, :, :], g["W_eT"].unsqueeze(1).broadcast_to([ED, NW, D])).then_inc(s["p_we"], 16)
                sp.wait_ge(s["i_wc"], 1)
                with nc.allow_non_contiguous_dma(reason="896 words"):
                    sp.dma_start(wl_d.rearrange("(c p) -> p c", p=128), wc_i[:, :]).then_inc(s["i_wl"], 16)
                sp.wait_ge(s["i_wl"], 16)
                sp.dma_start(WI[0:1, :], wl_d.unsqueeze(0)).then_inc(s["i_stored"], 16)
                sp.wait_ge(s["p_ln_out"], NT)
                sp.dma_start(xn_d.rearrange("(t p) d -> p t d", p=P), XS[:, :, :]).then_inc(s["p_stored"], 16)
                sp.wait_ge(s["p_xl"], NW)
                sp.dma_start(xl_d.rearrange("(w p) d -> p w d", p=WN), XL[:, :, :]).then_inc(s["p_stored"], 16)
                sp.wait_ge(s["p_we"], 16)
                sp.wait_ge(s["p_att"], 16)
                sp.wait_ge(s["i_dl"], 1)
                sp.dma_start(dl_d.rearrange("(c p) e -> p c e", p=128), dl[:, :, :]).then_inc(s["i_stored"], 16)
                sp.wait_ge(s["i_key"], 1)
                sp.dma_start(key_d[1:1 + ITEMS * TE].rearrange("(c p e) -> p c e", p=128, e=TE), ok[:, 0, :, :]).then_inc(s["i_stored"], 16)
                sp.wait_ge(s["i_const"], 5)
                sp.dma_start(key_d[0:1].unsqueeze(0), edge[0:1, 0:1]).then_inc(s["i_stored"], 16)
                sp.dma_start(key_d[ITEMS * TE + 1:ITEMS * TE + 2].unsqueeze(0), edge[0:1, 1:2]).then_inc(s["i_stored"], 16)
                sp.wait_ge(s["i_stored"], 16 * 5)
                sp.wait_ge(s["p_stored"], 32)

            @block.scalar
            def _(a):
                for k in range(CH):
                    a.wait_ge(s[f"i_ea{k % 2}"], 32 * (k // 2 + 1))
                    a.dma_start(eat_d[k * 128:(k + 1) * 128, :], eaT[:, k % 2, :]).then_inc(s[f"i_ea_out{k % 2}"], 16)
                    a.dma_start(ea_d[k * 128:(k + 1) * 128, :], ea[:, k % 2, :]).then_inc(s[f"i_ea_out{k % 2}"], 16)
                a.wait_ge(s["i_ea_out0"], 32 * 4)
                a.wait_ge(s["i_ea_out1"], 32 * 3)

            @block.gpsimd
            def _(p):
                p.memset(mhalf[:, :], -0.5).then_inc(s["p_const"], 1)
                p.memset(XT[:, :, N:], 0.0).then_inc(s["p_const"], 1)
                p.wait_ge(s["p_const"], 2)
                p.iota(wbase[:, :], pattern=[[WN, 2]], base=0, channel_multiplier=WN, allow_small_or_imprecise_dtypes=True).then_inc(s["i_const"], 1)
                p.iota(inum[:, :], pattern=[[128, CH]], base=0, channel_multiplier=1, allow_small_or_imprecise_dtypes=True).then_inc(s["i_const"], 1)
                p.iota(lane[:, :], pattern=[[1, NW]], base=0, channel_multiplier=0, allow_small_or_imprecise_dtypes=True).then_inc(s["i_const"], 1)
                p.memset(edge[:, :], -1.0).then_inc(s["i_const"], 1)
                p.memset(one28[:, :], 1.0).then_inc(s["i_const"], 1)
                p.wait_ge(s["i_const"], 5)
                p.affine_select(out=upto[:, :], in_=one28[:, 0:NW], compare_op=ALU.is_ge, fill=0.0, base=0,
                                pattern=[[1, NW]], channel_multiplier=-1).then_inc(s["i_upto"], 1)
                p.wait_ge(s["i_tile"], 1)
                for k in range(CH):
                    at = bass.IndirectOffsetOnAxis(ap=tile_i[:, k:k + 1], axis=0)
                    p.indirect_dma_start(out=dst_i[:, k, :], out_offset=None, in_=g["dst"], in_offset=at).then_inc(s["i_dst"], 16)
                    p.indirect_dma_start(out=src_i[:, k, :], out_offset=None, in_=g["src"], in_offset=at).then_inc(s["i_src"], 16)
                rstd_side(p, s, "p_ln", 0, ve, rstd, mhalf)
                for k in range(CH):
                    at = bass.IndirectOffsetOnAxis(ap=tile_i[:, k:k + 1], axis=0)
                    if k >= 2:
                        p.wait_ge(s[f"i_ea_out{k % 2}"], 32 * (k // 2))
                    p.indirect_dma_start(out=eaT[:, k % 2, :], out_offset=None, in_=g["eaT"], in_offset=at).then_inc(s[f"i_ea{k % 2}"], 16)
                    p.indirect_dma_start(out=ea[:, k % 2, :], out_offset=None, in_=g["ea"], in_offset=at).then_inc(s[f"i_ea{k % 2}"], 16)

            @block.tensor
            def _(pe):
                pe.wait_ge(s["i_wide"], 2)
                pe.wait_ge(s["i_upto"], 1)
                pe.matmul(pN[:, 0:NW], wide[:, 0, :], upto[:, :], start=True, stop=True)
                pe.matmul(pN[:, NW:2 * NW], wide[:, 0, :], ident[0:NW, 0:NW], start=True, stop=True)
                pe.matmul(pN[:, 2 * NW:3 * NW], wide[:, 1, :], ident[0:NW, 0:NW], start=True, stop=True).then_inc(s["i_tab"], 1)
                for q in range(NG):
                    pe.wait_ge(s["p_ln_out"], GT * (q + 1))
                    if q:
                        pe.wait_ge(s["p_t_out"], q)
                    for k in range(KC):
                        for j in range(GT):
                            ins = pe.transpose(pT[:, GT * k + j, 0:P], XS[:, GT * q + j, k * 128:(k + 1) * 128], ident[0:P, 0:P])
                    ins.then_inc(s["p_t_full"], 1)
                pe.wait_ge(s["p_t_out"], NG)
                pe.wait_ge(s["p_w"], 64)
                pe.wait_ge(s["p_const"], 2)
                for w in range(NW):
                    if w >= 2:
                        pe.wait_ge(s["p_xl"], w - 1)
                        pe.wait_ge(s["p_xr"], w - 1)
                    for k in range(KC):
                        ins = pe.matmul(pP[0:WN, w % 2, :], XT[:, k, w * WN:(w + 1) * WN], wlr[:, k, :], start=(k == 0), stop=(k == KC - 1))
                    ins.then_inc(s["p_lr"], 1)
                for n, (ready, t) in enumerate([("i_src_f", src_f)] * CH + [("i_dl", dl)] * CH):
                    pe.wait_ge(s[ready], 1)
                    if n >= 2:
                        pe.wait_ge(s["i_x_out"], n - 1)
                    pe.transpose(pX[0:TE, n % 2, 0:128], t[:, n % CH, :], ident[:, :]).then_inc(s["i_x"], 1)

            @block.vector
            def _(v):
                chain = s["i_chain"]
                done = [0]

                def then(ins):
                    done[0] += 1
                    ins.then_inc(chain, 1)
                    v.wait_ge(chain, done[0])

                v.wait_ge(s["i_ends"], 32)
                v.wait_ge(s["i_const"], 5)
                then(v.tensor_copy(ends[:, :, :], ends_i[:, :, :]))
                v.tensor_scalar(below[:, 0, :], ends[:, 1, :], wbase[:, 0:1], None, ALU.is_lt)
                then(v.tensor_scalar(below[:, 1, :], ends[:, 0, :], wbase[:, 1:2], None, ALU.is_lt))
                then(v.tensor_reduce(counts[:, :], below[:, :, :], AX.X, ALU.add))
                then(v.tensor_tensor(nitems[:, :], counts[:, 1:2], counts[:, 0:1], ALU.subtract))
                v.tensor_scalar(wide[:, 0, :], one28[:, :], nitems[:, 0:1], None, ALU.mult).then_inc(s["i_wide"], 1)
                v.tensor_scalar(wide[:, 1, :], one28[:, :], counts[:, 0:1], None, ALU.mult).then_inc(s["i_wide"], 1)
                v.wait_ge(s["i_tab"], 1)
                then(v.tensor_copy(tab[:, :, :], pN[:, 0:3 * NW].rearrange("p (a w) -> p a w", a=3)))
                then(v.tensor_tensor(shift[:, :], tab[:, 2, :], tab[:, 0, :], ALU.subtract))
                then(v.tensor_tensor(shift[:, :], shift[:, :], tab[:, 1, :], ALU.add))
                over_w = lambda a: a.unsqueeze(1).broadcast_to([128, CH, NW])
                over_c = lambda a: a.unsqueeze(2).broadcast_to([128, CH, NW])
                then(v.tensor_tensor(cmp[:, :, :], over_w(tab[:, 0, :]), over_c(inum[:, :]), ALU.is_le))
                then(v.tensor_reduce(wv[:, :], cmp[:, :, :], AX.X, ALU.add))
                then(v.tensor_tensor(cmp[:, :, :], over_w(lane[:, :]), over_c(wv[:, :]), ALU.is_equal))
                then(v.tensor_tensor(cmp[:, :, :], cmp[:, :, :], over_w(shift[:, :]), ALU.mult))
                then(v.tensor_reduce(tile_f[:, :], cmp[:, :, :], AX.X, ALU.add))
                then(v.tensor_tensor(tile_f[:, :], tile_f[:, :], inum[:, :], ALU.add))
                then(v.tensor_scalar(tile_f[:, :], tile_f[:, :], float(NTE - 1), None, ALU.min))
                v.tensor_copy(tile_i[:, :], tile_f[:, :]).then_inc(s["i_tile"], 1)
                v.tensor_scalar(base[:, :], wv[:, :], float(WN), None, ALU.mult)
                v.tensor_scalar(wc_i[:, :], wv[:, :], float(NW - 1), None, ALU.min).then_inc(s["i_wc"], 1)
                all_stats(v, s, "p_ln", lambda t: XS[:, t, :], st, mv, ve, lambda q: v.wait_ge(s[f"p_x{q}"], 16))
                for q in range(NG + 1):
                    if q < NG:
                        normalised(v, s, "p_ln", q, lambda t: XS[:, t, :], lambda t: XS[:, t, :], mv, rstd)
                    q -= 1
                    if q < 0:
                        continue
                    v.wait_ge(s["p_t_full"], q + 1)
                    for k in range(KC):
                        ins = v.tensor_copy(XT[:, k, q * GN:(q + 1) * GN].rearrange("p (j n) -> p j n", j=GT), pT[:, GT * k:GT * k + GT, 0:P])
                    ins.then_inc(s["p_t_out"], 1)
                v.wait_ge(s["p_w"], 64)
                for w in range(NW):
                    v.wait_ge(s["p_lr"], w + 1)
                    v.tensor_tensor(XL[:, w, :], pP[0:WN, w % 2, 0:D], blr[:, 0:D], ALU.add).then_inc(s["p_xl"], 1)
                    v.tensor_tensor(XRW[0:WN, w, :], pP[0:WN, w % 2, D:], blr[:, D:], ALU.add).then_inc(s["p_xr"], 1)
                v.wait_ge(s["i_src"], 16 * CH)
                v.wait_ge(s["i_dst"], 16 * CH)
                v.tensor_copy(src_f[:, :, :], src_i[:, :, :]).then_inc(s["i_src_f"], 1)
                then(v.tensor_copy(dst_f[:, :, :], dst_i[:, :, :]))
                then(v.tensor_tensor(dl[:, :, :], dst_f[:, :, :], base[:, :].unsqueeze(2).broadcast_to([128, CH, TE]), ALU.subtract))
                v.sem_inc(s["i_dl"], 1)
                v.tensor_scalar(ok[:, 0, :, :], dl[:, :, :], 0.0, None, ALU.is_ge)
                then(v.tensor_scalar(ok[:, 1, :, :], dl[:, :, :], float(WN), None, ALU.is_lt))
                then(v.tensor_tensor(ok[:, 0, :, :], ok[:, 0, :, :], ok[:, 1, :, :], ALU.mult))
                then(v.tensor_scalar(dst_f[:, :, :], dst_f[:, :, :], 1.0, None, ALU.add))
                v.tensor_tensor(ok[:, 0, :, :], ok[:, 0, :, :], dst_f[:, :, :], ALU.mult).then_inc(s["i_key"], 1)
                for n in range(2 * CH):
                    v.wait_ge(s["i_x"], n + 1)
                    to = SRCX if n < CH else DLX
                    k = n % CH
                    v.tensor_copy(to[:, k * 128:(k + 1) * 128], pX[0:TE, n % 2, 0:128]).then_inc(s["i_x_out"], 1)

        with ExitStack() as mid:
            PCX = mid.enter_context(nc.sbuf_tensor("g_pcx", [TE, ITEMS, 2 * GH], F32))

            with ExitStack() as c:
                def sb(name, shape, dt=F32):
                    return c.enter_context(nc.sbuf_tensor(name, shape, dt))

                LT = sb("a_lt", [128, GB, IG, TE])
                DB = sb("a_db", [WN, GB, IG, TE])
                G = sb("a_g", [TE, GB, IG, D])
                R = sb("a_r", [TE, 2, IG, D])
                IX = sb("a_ix", [TE, GB, IG], I32)
                AX_ = sb("a_alpha", [TE, ITEMS, GH])
                AT = sb("a_alphaT", [128, CH, GH, TE])
                node = sb("a_node", [128, 1])
                pS = c.enter_context(nc.psum_tensor("a_pS", [128, GB, IG * D], F32))
                block = c.enter_context(nc.Block())

                @block.sync
                def _(sp):
                    with sp.Fori(0, STEPS // 2) as i:
                        for h in range(GB):
                            q = GB * i + h
                            sp.wait_ge(s["a_scored"], q + 1)
                            at = bass.ds(q * IG, IG)
                            sp.dma_start(IX[:, h, :], SRCX[:, at]).then_inc(s[f"a_ix{h}"], 16)
                            sp.dma_start(DB[:, h, :, :], dl_d[at, :].rearrange("i e -> (i e)").unsqueeze(0).broadcast_to([WN, IG * TE])
                                         .rearrange("p (i e) -> p i e", i=IG)).then_inc(s[f"a_db{h}"], 16)
                            sp.dma_start(LT[WN:128, h, :, :], eat_d[at, :].rearrange("i (c e) -> c i e", c=ED)).then_inc(s[f"a_eat{h}"], 16)
                    sp.wait_ge(s["a_at"], CH)
                    sp.dma_start(al_d.rearrange("(c p) h e -> p c h e", p=128), AT[:, :, :, :]).then_inc(s["a_stored"], 16)
                    sp.wait_ge(s["a_stored"], 16)

                @block.gpsimd
                def _(p):
                    p.iota(node[:, :], pattern=[[0, 1]], base=0, channel_multiplier=1, allow_small_or_imprecise_dtypes=True).then_inc(s["a_const"], 1)
                    p.memset(AX_[:, STEPS * 2 * IG:, :], 0.0).then_inc(s["a_const"], 1)
                    with p.Fori(0, STEPS // 2) as i:
                        for h in range(GB):
                            p.wait_ge(s[f"a_ix{h}"], 16 * i + 16)
                            p.sem_inc(s["a_seen"], 1)
                            for j in range(IG):
                                p.indirect_dma_start(out=G[:, h, j, :], out_offset=None, in_=xl_d,
                                                     in_offset=bass.IndirectOffsetOnAxis(ap=IX[:, h, j:j + 1], axis=0)).then_inc(s[f"a_g{h}"], 16)

                @block.tensor
                def _(pe):
                    with pe.Fori(0, STEPS // 2) as i:
                        for h in range(GB):
                            q = GB * i + h
                            ws = [pe.value_load(WI[0:1, bass.ds(q * IG + j, 1)], min_val=0, max_val=NW - 1) for j in range(IG)]
                            pe.wait_ge(s["a_summed"], q + 1)
                            pe.wait_ge(s["a_onehot"], q + 1)
                            pe.wait_ge(s[f"a_eat{h}"], 16 * i + 16)
                            pe.wait_ge(s[f"a_g{h}"], 64 * i + 64)
                            for j in range(IG):
                                o = pS[0:TE, h, j * D:(j + 1) * D]
                                pe.matmul(o, LT[:, h, j, :], XRW[:, bass.ds(ws[j], 1), :].rearrange("p a d -> p (a d)"), start=True, stop=False)
                                ins = pe.matmul(o, ident[0:TE, 0:TE], G[:, h, j, :], start=False, stop=True)
                            ins.then_inc(s["a_scored"], 1)
                    pe.wait_ge(s["a_alpha"], 2 * STEPS + 2)
                    pe.wait_ge(s["a_const"], 2)
                    for k in range(CH):
                        if k >= 2:
                            pe.wait_ge(s["a_at"], k - 1)
                        for hd in range(GH):
                            ins = pe.transpose(pS[:, k % 2, hd * TE:(hd + 1) * TE], AX_[:, k * 128:(k + 1) * 128, hd], ident[0:TE, 0:TE])
                        ins.then_inc(s["a_ta"], 1)

                @block.scalar
                def _(a):
                    with a.Fori(0, STEPS // 2) as i:
                        for h in range(GB):
                            q = GB * i + h
                            a.wait_ge(s["a_scored"], q + GB + 1)
                            a.wait_ge(s["a_alpha"], q + 1)
                            a.activation(R[:, h % 2, :, :].rearrange("p i d -> p (i d)"), pS[0:TE, h, :], ACT.Copy, scale=SLOPE).then_inc(s["a_fifth"], 1)

                @block.vector
                def _(v):
                    for name, k in (("a_scored", GB), ("a_summed", GB), ("a_alpha", 2)):
                        v.sem_inc(s[name], k)
                    v.wait_ge(s["a_const"], 2)

                    def onehot(q, i, h):
                        v.wait_ge(s[f"a_db{h}"], 16 * i + 16)
                        v.tensor_scalar(LT[0:WN, h, :, :], DB[:, h, :, :], node[0:WN, 0:1], None, ALU.is_equal).then_inc(s["a_onehot"], 1)

                    def score(q, h):
                        r = R[:, h % 2, :, :]
                        flat = r.rearrange("p i d -> p (i d)")
                        v.wait_ge(s["a_fifth"], q + 1)
                        v.tensor_tensor(flat, flat, pS[0:TE, h, :], ALU.max).then_inc(s["a_summed"], 1)
                        v.wait_ge(s["a_summed"], q + GB + 1)
                        v.tensor_tensor(r, r, attb[0:TE, :].unsqueeze(1).broadcast_to([TE, IG, D]), ALU.mult).then_inc(s["a_times"], 1)
                        v.wait_ge(s["a_times"], q + 1)
                        v.sem_inc(s["a_seen_v"], 1)
                        v.tensor_reduce(AX_[:, bass.ds(q * IG, IG), :].rearrange("p i h -> p (i h)"),
                                        r.rearrange("p i (h d) -> p (i h) d", h=GH), AX.X, ALU.add).then_inc(s["a_alpha"], 1)

                    onehot(0, 0, 0)
                    onehot(1, 0, 1)
                    with v.Fori(0, STEPS // 2 - 1) as i:
                        for h in range(GB):
                            onehot(GB * i + h + 2, i + (h + 2) // GB, (h + 2) % GB)
                            score(GB * i + h, h)
                    for h in range(GB):
                        if h < 2:
                            onehot(2 * STEPS - GB + h + 2, STEPS // 2 - 1, h + 2)
                        score(2 * STEPS - GB + h, h)
                    for k in range(CH):
                        v.wait_ge(s["a_ta"], k + 1)
                        v.tensor_copy(AT[:, k, :, :].rearrange("p h e -> p (h e)"), pS[:, k % 2, 0:GH * TE]).then_inc(s["a_at"], 1)

            with ExitStack() as c:
                def sb(name, shape, dt=F32):
                    return c.enter_context(nc.sbuf_tensor(name, shape, dt))

                A = sb("s_a", [128, GH, RUN])
                F = sb("s_f", [128, GH, RUN])
                B = sb("s_b", [128, GH, RUN])
                key = sb("s_key", [128, 3, RUN])
                edge = sb("s_edge", [128, 2, RUN])
                last = sb("s_last", [128, RUN])
                outside = sb("s_outside", [128, RUN])
                sums = sb("s_sums", [128, 4, GH])
                rows = sb("s_rows", [GH, 4, 128])
                state = sb("s_state", [GH, 2, 128])
                carry = sb("s_carry", [GH, 2, 128])
                init = sb("s_init", [128, 2, GH])
                PT = sb("s_pt", [128, 2, 2 * GH, TE])
                wf = sb("s_wf", [1, ITEMS // IG, IG])
                digit = sb("s_digit", [1, IG])
                wsum = sb("s_wsum", [1, ITEMS // IG])
                pR = c.enter_context(nc.psum_tensor("s_pR", [128, 4, 512], F32))
                pX = c.enter_context(nc.psum_tensor("s_pX", [128, 2, 512], F32))
                block = c.enter_context(nc.Block())

                @block.sync
                def _(sp):
                    for hd in range(GH):
                        sp.dma_start(A[:, hd, :].rearrange("p (k e) -> p k e", e=TE),
                                     al_d.rearrange("(p k) h e -> h p k e", p=128)[hd]).then_inc(s["s_in"], 16)
                    for n in range(3):
                        sp.dma_start(key[:, n, :], key_d[n:n + ITEMS * TE].rearrange("(p r) -> p r", p=128)).then_inc(s["s_in"], 16)
                    sp.wait_ge(s["s_p"], 1)
                    sp.wait_ge(s["s_cl"], 1)
                    view = pc_d.rearrange("(p k) c e -> c p k e", p=128)
                    for hd in range(GH):
                        sp.dma_start(view[hd], A[:, hd, :].rearrange("p (k e) -> p k e", e=TE)).then_inc(s["s_pc"], 16)
                        sp.dma_start(view[GH + hd], F[:, hd, :].rearrange("p (k e) -> p k e", e=TE)).then_inc(s["s_pc"], 16)
                    sp.wait_ge(s["s_pc"], 16 * 2 * GH)
                    for k in range(CH):
                        if k >= 2:
                            sp.wait_ge(s["s_x"], 2 * (k - 1))
                        sp.dma_start(PT[:, k % 2, :, :], pc_d[k * 128:(k + 1) * 128, :, :]).then_inc(s[f"s_pt{k % 2}"], 16)

                @block.scalar
                def _(a):
                    a.wait_ge(s["s_diff"], 1)
                    a.activation(A[:, :, :], A[:, :, :], ACT.Exp).then_inc(s["s_p"], 1)

                @block.tensor
                def _(pe):
                    pe.wait_ge(s["s_sums"], 1)
                    for n in range(4):
                        ins = pe.transpose(pR[0:GH, n, 0:128], sums[:, n, :], ident[:, :])
                    ins.then_inc(s["s_rows"], 1)
                    pe.wait_ge(s["s_carry"], 1)
                    for n in range(2):
                        ins = pe.transpose(pR[:, n, 128:128 + GH], carry[:, n, :], ident[0:GH, 0:GH])
                    ins.then_inc(s["s_init"], 1)
                    for k in range(CH):
                        pe.wait_ge(s[f"s_pt{k % 2}"], 16 * (k // 2 + 1))
                        for n in range(2):
                            if k:
                                pe.wait_ge(s["s_pcx"], 2 * k + n - 1)
                            for hd in range(GH):
                                ins = pe.transpose(pX[0:TE, n, hd * 128:(hd + 1) * 128], PT[:, k % 2, n * GH + hd, :], ident[:, :])
                            ins.then_inc(s["s_x"], 1)

                @block.vector
                def _(v):
                    done = [0]

                    def then(ins):
                        done[0] += 1
                        ins.then_inc(s["s_chain"], 1)
                        v.wait_ge(s["s_chain"], done[0])

                    for j in range(IG):
                        v.memset(digit[:, j:j + 1], float(1 << (5 * j)))
                    then(v.tensor_copy(wf[:, :, :], WI[:, :].rearrange("p (n i) -> p n i", i=IG)))
                    then(v.tensor_tensor(wf[:, :, :], wf[:, :, :], digit[:, :].unsqueeze(1).broadcast_to([1, ITEMS // IG, IG]), ALU.mult))
                    then(v.tensor_reduce(wsum[:, :], wf[:, :, :], AX.X, ALU.add))
                    then(v.tensor_copy(WP[:, :], wsum[:, :]))
                    v.wait_ge(s["s_in"], 16 * (GH + 3))
                    v.tensor_tensor(edge[:, 0, :], key[:, 1, :], key[:, 0, :], ALU.not_equal)
                    v.tensor_tensor(last[:, :], key[:, 1, :], key[:, 2, :], ALU.not_equal)
                    then(v.tensor_scalar(outside[:, :], key[:, 1, :], 0.0, LOW, ALU.is_equal, ALU.mult))
                    v.tensor_scalar(edge[:, 0, :], edge[:, 0, :], LOW, None, ALU.mult)
                    v.tensor_scalar(edge[:, 1, :], last[:, :], LOW, None, ALU.mult)
                    then(v.tensor_tensor(A[:, :, :], A[:, :, :], outside[:, :].unsqueeze(1).broadcast_to([128, GH, RUN]), ALU.add))

                    def scans(initial):
                        for hd in range(GH):
                            v.tensor_tensor_scan(F[:, hd, :], edge[:, 0, :], A[:, hd, :], initial(0, hd), ALU.add, ALU.max)
                            ins = v.tensor_tensor_scan(B[:, hd, ::-1], edge[:, 1, ::-1], A[:, hd, ::-1], initial(1, hd), ALU.add, ALU.max)
                        then(ins)

                    scans(lambda n, hd: LOW)
                    v.tensor_copy(sums[:, 0, :], F[:, :, RUN - 1])
                    v.tensor_copy(sums[:, 1, :], B[:, :, 0])
                    v.tensor_reduce(sums[:, 2, 0:1], edge[:, 0, :], AX.X, ALU.min)
                    then(v.tensor_reduce(sums[:, 3, 0:1], edge[:, 1, :], AX.X, ALU.min))
                    for n in (2, 3):
                        ins = v.tensor_copy(sums[:, n, 1:GH], sums[:, n, 0:1].broadcast_to([128, GH - 1]))
                    ins.then_inc(s["s_sums"], 1)
                    v.wait_ge(s["s_rows"], 1)
                    then(v.tensor_copy(rows[:, :, :], pR[0:GH, :, 0:128]))
                    v.tensor_tensor_scan(state[:, 0, :], rows[:, 2, :], rows[:, 0, :], LOW, ALU.add, ALU.max)
                    v.tensor_tensor_scan(state[:, 1, ::-1], rows[:, 3, ::-1], rows[:, 1, ::-1], LOW, ALU.add, ALU.max)
                    then(v.memset(carry[:, :, :], LOW))
                    v.tensor_copy(carry[:, 0, 1:128], state[:, 0, 0:127])
                    v.tensor_copy(carry[:, 1, 0:127], state[:, 1, 1:128]).then_inc(s["s_carry"], 1)
                    v.wait_ge(s["s_init"], 1)
                    then(v.tensor_copy(init[:, :, :], pR[:, 0:2, 128:128 + GH]))
                    scans(lambda n, hd: init[:, n, hd:hd + 1])
                    then(v.tensor_tensor(F[:, :, :], F[:, :, :], B[:, :, :], ALU.max))
                    v.tensor_tensor(A[:, :, :], A[:, :, :], F[:, :, :], ALU.subtract).then_inc(s["s_diff"], 1)
                    v.wait_ge(s["s_diff"], 1)
                    v.tensor_tensor(F[:, :, :], F[:, :, :], last[:, :].unsqueeze(1).broadcast_to([128, GH, RUN]), ALU.mult).then_inc(s["s_cl"], 1)
                    for k in range(CH):
                        for n in range(2):
                            v.wait_ge(s["s_x"], 2 * k + n + 1)
                            v.tensor_copy(PCX[:, k * 128:(k + 1) * 128, n * GH:(n + 1) * GH].rearrange("p i h -> p h i"),
                                          pX[0:TE, n, :].rearrange("p (h i) -> p h i", h=GH)).then_inc(s["s_pcx"], 1)

            with ExitStack() as c:
                def sb(name, shape, dt=F32):
                    return c.enter_context(nc.sbuf_tensor(name, shape, dt))

                ACC = sb("b_acc", [WN, NW, MW])

                with ExitStack() as d:
                    G = d.enter_context(nc.sbuf_tensor("b_g", [TE, GB, IG, D], F32))
                    M = d.enter_context(nc.sbuf_tensor("b_m", [TE, 2, IG, MW], F32))
                    OH = d.enter_context(nc.sbuf_tensor("b_oh", [TE, 2, IG, WN], F32))
                    IX = d.enter_context(nc.sbuf_tensor("b_ix", [TE, GB, IG], I32))
                    node = d.enter_context(nc.sbuf_tensor("b_node", [TE, WN], F32))
                    pM = d.enter_context(nc.psum_tensor("b_pM", [128, 2, IG, 512], F32))
                    block = d.enter_context(nc.Block())

                    @block.sync
                    def _(sp):
                        sp.wait_ge(s["b_const"], 3)

                        def sources(q, b):
                            sp.wait_ge(s["b_weighted"], q + 1)
                            sp.sem_inc(s["b_seen_sp"], 1)
                            sp.wait_ge(s["b_weighted_a"], q + 1)
                            at = slice(q * IG, q * IG + IG) if isinstance(q, int) else bass.ds(q * IG, IG)
                            sp.dma_start(IX[:, b, :], SRCX[:, at]).then_inc(s[f"b_ix{b}"], 16)

                        def attributes(q, h):
                            sp.wait_ge(s["b_summed"], q + 1)
                            at = slice(q * IG, q * IG + IG) if isinstance(q, int) else bass.ds(q * IG, IG)
                            sp.dma_start(M[:, h, :, EA0:EA0 + ED],
                                         ea_d[at, :].rearrange("i (e c) -> e i c", c=ED)).then_inc(s[f"b_ea{h}"], 16)

                        sources(0, 0)
                        sources(1, 1)
                        with sp.Fori(0, STEPS // 2 - 1) as i:
                            for b in range(GB):
                                sources(GB * i + b + 2, (b + 2) % GB)
                                attributes(GB * i + b, b % 2)
                        for b in range(GB):
                            q = 2 * STEPS - GB + b
                            if q + 2 < 2 * STEPS:
                                sources(q + 2, (b + 2) % GB)
                            attributes(q, b % 2)

                    @block.gpsimd
                    def _(p):
                        p.iota(node[:, :], pattern=[[1, WN]], base=0, channel_multiplier=0, allow_small_or_imprecise_dtypes=True).then_inc(s["b_const"], 1)
                        p.memset(M[:, :, :, :], 1.0).then_inc(s["b_const"], 1)
                        p.memset(ACC[:, :, :], 0.0).then_inc(s["b_const"], 1)
                        with p.Fori(0, STEPS // 2) as i:
                            for h in range(GB):
                                p.wait_ge(s[f"b_ix{h}"], 16 * i + 16)
                                p.sem_inc(s["b_seen"], 1)
                                for j in range(IG):
                                    p.indirect_dma_start(out=G[:, h, j, :], out_offset=None, in_=xl_d,
                                                         in_offset=bass.IndirectOffsetOnAxis(ap=IX[:, h, j:j + 1], axis=0)).then_inc(s[f"b_g{h}"], 16)

                    @block.tensor
                    def _(pe):
                        with pe.Fori(0, STEPS) as i:
                            for h in range(2):
                                q = 2 * i + h
                                pe.wait_ge(s["b_weighted"], q + GB + 1)
                                pe.wait_ge(s["b_weighted_a"], q + GB + 1)
                                pe.wait_ge(s["b_acc"], IG * q + 1)
                                pe.wait_ge(s[f"b_ea{h}"], 16 * i + 16)
                                for j in range(IG):
                                    ins = pe.matmul(pM[0:WN, h, j, 0:MW], OH[:, h, j, :], M[:, h, j, :], start=True, stop=True)
                                ins.then_inc(s["b_summed"], 1)

                    @block.scalar
                    def _(a):
                        with a.Fori(0, STEPS // 2) as i:
                            for b in range(GB):
                                q, h = GB * i + b, b % 2
                                a.wait_ge(s["b_copied"], q + 1)
                                a.wait_ge(s[f"b_g{b}"], 64 * i + 64)
                                for j in range(BYV, IG):
                                    for hd in range(GH):
                                        part = slice(hd * (D // GH), (hd + 1) * (D // GH))
                                        ins = a.activation(M[:, h, j, part], G[:, b, j, part], ACT.Copy, scale=M[:, h, j, D + hd:D + hd + 1])
                                ins.then_inc(s["b_weighted_a"], 1)

                    @block.vector
                    def _(v):
                        for name, k in (("b_weighted", GB), ("b_weighted_a", GB), ("b_summed", 2), ("b_acc", 2 * IG)):
                            v.sem_inc(s[name], k)
                        v.wait_ge(s["b_const"], 3)

                        def weigh(q, i, b):
                            h = b % 2
                            v.wait_ge(s["b_summed"], q + 1)
                            v.sem_inc(s["b_seen_v"], 1)
                            at = bass.ds(q * IG, IG) if not isinstance(q, int) else slice(q * IG, q * IG + IG)
                            v.tensor_tensor(OH[:, h, :, :], node[:, :].unsqueeze(1).broadcast_to([TE, IG, WN]),
                                            DLX[:, at].unsqueeze(2).broadcast_to([TE, IG, WN]), ALU.is_equal)
                            v.tensor_copy(M[:, h, :, D:D + 2 * GH], PCX[:, at, :]).then_inc(s["b_copied"], 1)
                            v.wait_ge(s[f"b_g{b}"], 64 * i + 64)
                            some = bass.ds(q * IG, BYV) if not isinstance(q, int) else slice(q * IG, q * IG + BYV)
                            heads = lambda a: a.rearrange("p i (h d) -> p i h d", h=GH)
                            ins = v.tensor_tensor(heads(M[:, h, 0:BYV, 0:D]), heads(G[:, b, 0:BYV, :]),
                                                  PCX[:, some, 0:GH].unsqueeze(3).broadcast_to([TE, BYV, GH, D // GH]), ALU.mult)
                            ins.then_inc(s["b_weighted"], 1)

                        flat = ACC[:, :, :].rearrange("p w m -> p (w m)")

                        def add(q, h):
                            four = v.value_load(WP[0:1, (slice(q, q + 1) if isinstance(q, int) else bass.ds(q, 1))], min_val=0, max_val=(1 << (5 * IG)) - 1)
                            at = [v.snap(((four >> (5 * j)) & 31) * MW) for j in range(IG)]
                            before = [IG * q + j + 2 * IG for j in range(IG)]
                            if not isinstance(q, int):
                                before = [v.snap(n) for n in before]
                            v.wait_ge(s["b_summed"], q + 3)
                            for j in range(IG):
                                a = flat[:, bass.ds(at[j].with_bounds(min_val=0, max_val=(NW - 1) * MW), MW)]
                                v.wait_ge(s["b_acc"], before[j])
                                v.tensor_tensor(a, a, pM[0:WN, h, j, 0:MW], ALU.add).then_inc(s["b_acc"], 1)

                        weigh(0, 0, 0)
                        with v.Fori(0, STEPS // 2 - 1) as i:
                            for b in range(GB):
                                weigh(GB * i + b + 1, i + (b + 1) // GB, (b + 1) % GB)
                                add(GB * i + b, b % 2)
                        last = 2 * STEPS - GB
                        for b in range(GB - 1):
                            weigh(last + b + 1, STEPS // 2 - 1, b + 1)
                            add(last + b, b % 2)
                        add(2 * STEPS - 1, 1)

                deg1 = sb("e_deg1", [WN, NW])
                la = sb("e_la", [WN, NW, ED])
                laT = sb("e_laT", [ED, NW * WN])
                weT = sb("e_weT", [ED, D])
                S = sb("e_s", [WN, NW, D])
                T = XRW[0:WN, :, :]
                own = sb("e_own", [WN, NW, GH])
                none = sb("e_none", [WN, NW])
                cmax = sb("e_cmax", [WN, NW, GH])
                m = sb("e_m", [WN, NW, GH])
                e12 = sb("e_e12", [WN, 2, NW, GH])
                den = sb("e_den", [WN, NW, GH])
                bias = sb("e_bias", [WN, D])
                pL = c.enter_context(nc.psum_tensor("e_pL", [128, 2, 512], F32))
                pE = c.enter_context(nc.psum_tensor("e_pE", [128, 4, 512], F32))
                LW, EW = 4, 2
                HALF = NW // 2
                block = c.enter_context(nc.Block())

                @block.sync
                def _(sp):
                    sp.dma_start(weT[:, :], g["W_eT"]).then_inc(s["e_w"], 16)
                    sp.dma_start(bias[:, :], g["bias"].unsqueeze(0).broadcast_to([WN, D])).then_inc(s["e_w"], 16)
                    for n in range(2):
                        at = slice(n * HALF, (n + 1) * HALF)
                        sp.wait_ge(s["e_silu"], n + 1)
                        sp.dma_start(sums_d.rearrange("(w p) d -> p w d", p=WN)[:, at, :], S[:, at, :]).then_inc(s["e_stored"], 16)
                    sp.wait_ge(s["e_stored"], 32)

                @block.gpsimd
                def _(p):
                    for n in range(4):
                        at = slice(n * NW // 4, (n + 1) * NW // 4)
                        p.tensor_tensor(T[:, at, :], XRW[0:WN, at, :], XL[:, at, :], ALU.add).then_inc(s["e_lr"], 1)
                    p.wait_ge(s["e_gates"], 1)
                    for n in range(2):
                        at = slice(n * HALF, (n + 1) * HALF)
                        p.tensor_tensor(T[:, at, :].rearrange("p w (h d) -> p (w h) d", h=GH), XL[:, at, :].rearrange("p w (h d) -> p (w h) d", h=GH),
                                        e12[:, 1, at, :].rearrange("p w h -> p (w h)").unsqueeze(2).broadcast_to([WN, HALF * GH, D // GH]),
                                        ALU.mult).then_inc(s["e_own"], 1)

                @block.tensor
                def _(pe):
                    pe.wait_ge(s["e_la"], 1)
                    for n in range(NW // LW):
                        if n >= 2:
                            pe.wait_ge(s["e_laT"], n - 1)
                        for i in range(LW):
                            ins = pe.transpose(pL[0:ED, n % 2, i * WN:(i + 1) * WN], la[:, LW * n + i, :], ident[0:WN, 0:WN])
                        ins.then_inc(s["e_lt"], 1)
                    pe.wait_ge(s["e_w"], 32)
                    for n in range(NW // EW):
                        pe.wait_ge(s["e_laT"], EW * n // LW + 1)
                        if n >= 4:
                            pe.wait_ge(s["e_sum"], n - 3)
                        for i in range(EW):
                            w = EW * n + i
                            o = pE[0:WN, n % 4, i * D:(i + 1) * D]
                            ins = pe.matmul(o, laT[:, w * WN:(w + 1) * WN], weT[:, :], start=True, stop=True)
                        ins.then_inc(s["e_feat"], 1)

                @block.scalar
                def _(a):
                    a.wait_ge(s["e_less"], 1)
                    a.activation(e12[:, :, :, :], e12[:, :, :, :], ACT.Exp).then_inc(s["e_exp"], 1)
                    for n in range(2):
                        at = slice(n * HALF, (n + 1) * HALF)
                        a.wait_ge(s["e_out"], n + 1)
                        a.activation(S[:, at, :], S[:, at, :], ACT.Silu).then_inc(s["e_silu"], 1)

                @block.vector
                def _(v):
                    done = [0]

                    def then(ins):
                        done[0] += 1
                        ins.then_inc(s["e_chain"], 1)
                        v.wait_ge(s["e_chain"], done[0])

                    heads = lambda a: a.rearrange("p w (h d) -> p (w h) d", h=GH)
                    spread = lambda a, n: a.rearrange("p w h -> p (w h)").unsqueeze(2).broadcast_to([WN, NW * GH, n])
                    deg = ACC[:, :, EA0 + ED]
                    v.tensor_scalar(none[:, :], deg, 0.0, LOW, ALU.is_equal, ALU.mult)
                    then(v.tensor_scalar(deg1[:, :], deg, 1.0, None, ALU.max))
                    then(v.reciprocal(deg1[:, :], deg1[:, :]))
                    v.tensor_tensor(la[:, :, :], ACC[:, :, EA0:EA0 + ED], deg1[:, :].unsqueeze(2).broadcast_to([WN, NW, ED]), ALU.mult).then_inc(s["e_la"], 1)
                    v.tensor_tensor(cmax[:, :, :], ACC[:, :, D + GH:D + 2 * GH], none[:, :].unsqueeze(2).broadcast_to([WN, NW, GH]), ALU.add)
                    for n in range(NW // LW):
                        v.wait_ge(s["e_lt"], n + 1)
                        v.tensor_copy(laT[:, n * LW * WN:(n + 1) * LW * WN], pL[0:ED, n % 2, 0:LW * WN]).then_inc(s["e_laT"], 1)
                    two = lambda a, n: a[:, EW * n:EW * n + EW, :].rearrange("p w d -> p (w d)")
                    for n in range(NW // EW + 1):
                        if n < NW // EW:
                            v.wait_ge(s["e_feat"], n + 1)
                            v.wait_ge(s["e_lr"], (EW * n + EW - 1) * 4 // NW + 1)
                            v.tensor_tensor(two(S, n), two(T, n), pE[0:WN, n % 4, :], ALU.add).then_inc(s["e_sum"], 1)
                        if n:
                            v.wait_ge(s["e_sum"], n)
                            v.scalar_tensor_tensor(out=two(S, n - 1), in0=two(S, n - 1), scalar=SLOPE, in1=two(S, n - 1),
                                                   op0=ALU.mult, op1=ALU.max).then_inc(s["e_leaky"], 1)
                    v.wait_ge(s["e_leaky"], NW // EW)
                    then(v.tensor_tensor(S[:, :, :], S[:, :, :], attb[0:WN, :].unsqueeze(1).broadcast_to([WN, NW, D]), ALU.mult))
                    then(v.tensor_reduce(own[:, :, :].rearrange("p w h -> p (w h)"), heads(S[:, :, :]), AX.X, ALU.add))
                    then(v.tensor_tensor(m[:, :, :], cmax[:, :, :], own[:, :, :], ALU.max))
                    v.tensor_tensor(e12[:, 0, :, :], cmax[:, :, :], m[:, :, :], ALU.subtract)
                    v.tensor_tensor(e12[:, 1, :, :], own[:, :, :], m[:, :, :], ALU.subtract).then_inc(s["e_less"], 1)
                    v.wait_ge(s["e_exp"], 1)
                    then(v.tensor_tensor(den[:, :, :], ACC[:, :, D:D + GH], e12[:, 0, :, :], ALU.mult))
                    then(v.tensor_tensor(den[:, :, :], den[:, :, :], e12[:, 1, :, :], ALU.add))
                    then(v.tensor_scalar(den[:, :, :], den[:, :, :], 1e-16, None, ALU.add))
                    then(v.reciprocal(den[:, :, :], den[:, :, :]))
                    v.tensor_tensor(e12[:, 0, :, :], e12[:, 0, :, :], den[:, :, :], ALU.mult)
                    v.tensor_tensor(e12[:, 1, :, :], e12[:, 1, :, :], den[:, :, :], ALU.mult).then_inc(s["e_gates"], 1)
                    v.wait_ge(s["e_gates"], 1)
                    v.wait_ge(s["e_w"], 32)
                    for n in range(2):
                        at = slice(n * HALF, (n + 1) * HALF)
                        hd = lambda a: a.rearrange("p w (h d) -> p w h d", h=GH)
                        half = S[:, at, :]
                        then(v.tensor_tensor(hd(half), hd(ACC[:, at, 0:D]), e12[:, 0, at, :].unsqueeze(3).broadcast_to([WN, HALF, GH, D // GH]), ALU.mult))
                        then(v.tensor_tensor(half, half, bias[:, :].unsqueeze(1).broadcast_to([WN, HALF, D]), ALU.add))
                        v.wait_ge(s["e_own"], n + 1)
                        v.tensor_tensor(half, half, T[:, at, :], ALU.add).then_inc(s["e_out"], 1)


UN = 2 * P
UNITS = -(-NT // 2)
FIRST = 6
BS = 256
BLOCKS = (2 * N + EXPERTS * (BS - 1)) // BS
THRS = -(-N // BS)
TOTAL = UNITS + BLOCKS
SHARED = EXPERTS


def experts(nc, s, XS, ident, w, out, xg_d, y_d, xx_d):
    with ExitStack() as c:
        def sb(name, shape, dt=F32):
            return c.enter_context(nc.sbuf_tensor(name, shape, dt))

        def ps(name, shape):
            return c.enter_context(nc.psum_tensor(name, shape, F32))

        HT = sb("f_ht", [128, KC, N])
        NR = sb("f_nr", [P, NT, D])
        w2 = sb("f_w2", [128, (EXPERTS + 1) * FC, D])
        w1 = sb("f_w1", [128, 2, KC, FF])
        b1 = sb("f_b1", [128, 2, FC])
        b2 = sb("f_b2", [128, 2, D])
        b2s = sb("f_b2s", [P, D])
        HID = sb("f_hid", [128, 2, FC, BS])
        XG = sb("f_xg", [128, 2, 2, D])
        XGT = sb("f_xgt", [128, 2, KC, BS])
        Y = sb("f_y", [128, 2, 2, D])
        zero = sb("f_zero", [P, NT])
        wr = sb("f_wr", [128, KC, EXPERTS])
        lower = sb("f_lower", [P, P])
        ones = sb("f_ones", [P, P])
        st = sb("f_st", [P, NT, 6])
        mv = sb("f_mv", [P, NT, 2])
        ve = sb("f_ve", [P, NT])
        rstd = sb("f_rstd", [P, NT])
        mhalf = sb("f_mhalf", [P, NT])
        lane = sb("f_lane", [P, EXPERTS])
        thr = sb("f_thr", [P, THRS])
        bnum = sb("f_bnum", [P, BLOCKS])
        rw = sb("f_rw", [P, NT, EXPERTS])
        rmax = sb("f_rmax", [P, NT])
        rsum = sb("f_rsum", [P, NT])
        rrec = sb("f_rrec", [P, NT])
        top = sb("f_top", [P, NT, 8])
        topi = sb("f_topi", [P, NT, 8], U32)
        topf = sb("f_topf", [P, NT, 8])
        pick = sb("f_pick", [P, 2, NT, EXPERTS])
        mask = sb("f_mask", [P, NT, EXPERTS])
        tot = sb("f_tot", [P, NT, EXPERTS])
        upto = sb("f_upto", [P, NT, EXPERTS])
        rank = sb("f_rank", [P, NT, EXPERTS])
        over = sb("f_over", [P, EXPERTS, THRS])
        nb = sb("f_nb", [P, EXPERTS])
        nbi = sb("f_nbi", [P, EXPERTS])
        base = sb("f_base", [P, EXPERTS])
        before = sb("f_before", [P, BLOCKS, EXPERTS])
        eb = sb("f_eb", [P, 2, BLOCKS])
        table = sb("f_table", [P, 2, BLOCKS], I32)
        pos = sb("f_pos", [P, 2, NT])
        posi = sb("f_posi", [P, 2, NT], I32)
        gate = sb("f_gate", [P, 2, NT])
        pH = ps("f_pH", [128, 4, 512])
        pO = ps("f_pO", [128, 2, 512])
        pT = ps("f_pT", [128, 2, 512])
        Y1 = w2[0:P, 0:NT, :]

        block = c.enter_context(nc.Block())

        def unit_step(u):
            return u if u < FIRST else u + BLOCKS

        def tiles_of(u):
            return range(2 * u, min(2 * u + 2, NT))

        def steps(eng, unit, blk):
            for u in range(FIRST):
                unit(u)
            with eng.Fori(0, BLOCKS // 2) as i:
                for h in range(2):
                    blk(2 * i + h, h)
            for u in range(FIRST, UNITS):
                unit(u)

        @block.sync
        def _(sp):
            def load(slot, W1, B1):
                sp.dma_start(w1[:, slot, :, :], chunked(W1)).then_inc(s[f"f_w{slot}"], 16)
                sp.dma_start(b1[:, slot, :], B1).then_inc(s[f"f_w{slot}"], 16)

            def free(G):
                sp.wait_ge(s["f_gelu"], FC * G - FC + 4)
                sp.sem_inc(s["f_seen"], 1)

            def load_b2(b, h):
                e = sp.value_load(table[0:1, 0, (slice(b, b + 1) if isinstance(b, int) else bass.ds(b, 1))], min_val=0, max_val=EXPERTS - 1)
                sp.wait_ge(s["f_drained"], 2 * (FIRST + b))
                sp.sem_inc(s["f_seen"], 1)
                sp.dma_start(b2[:, h, :], picked(w["b2p"], e).unsqueeze(0).broadcast_to([128, D])).then_inc(s[f"f_b2{h}"], 16)

            sp.dma_start(wr[:, :, :], chunked(w["Wr"])).then_inc(s["f_small"], 16)
            load(1, w["W1s"], w["b1s"])
            for g in range(NG):
                tiles, nodes = slice(g * GT, (g + 1) * GT), slice(g * GN, (g + 1) * GN)
                sp.dma_start(NR[:, tiles, :], xx_d[nodes, :].rearrange("(t p) d -> p t d", p=P)).then_inc(s[f"f_part{g}"], 16)
            sp.dma_start(b2s[:, :], w["b2s"].unsqueeze(0).broadcast_to([P, D])).then_inc(s["f_b2s"], 16)
            sp.dma_start(w2[:, SHARED * FC:, :], chunked(w["W2s"])).then_inc(s["f_w2s"], 16)
            for e in range(EXPERTS):
                sp.dma_start(w2[:, e * FC:(e + 1) * FC, :], chunked(w["W2p"][e])).then_inc(s["f_w2p"], 16)
            sp.wait_ge(s["f_table"], 1)

            def load_w1(b, h):
                e = sp.value_load(table[0:1, 0, (slice(b, b + 1) if isinstance(b, int) else bass.ds(b, 1))], min_val=0, max_val=EXPERTS - 1)
                free(FIRST + b)
                load(h, picked(w["W1p"], e), picked(w["b1p"], e))

            load_w1(0, 0)
            with sp.Fori(0, BLOCKS // 2 - 1) as i:
                for h in range(2):
                    load_w1(2 * i + h + 1, 1 - h)
                    load_b2(2 * i + h, h)
            load_w1(BLOCKS - 1, 1)
            load_b2(BLOCKS - 2, 0)
            free(FIRST + BLOCKS)
            load(0, w["W1s"], w["b1s"])
            load_b2(BLOCKS - 1, 1)
            rows = out.rearrange("(t p) d -> p t d", p=P)
            for g in range(NG):
                sp.wait_ge(s["f_done"], 2 * GT * (g + 1))
                sp.dma_start(rows[:, g * GT:(g + 1) * GT, :], XS[:, g * GT:(g + 1) * GT, :]).then_inc(s["f_stored"], 16)
            sp.wait_ge(s["f_stored"], 16 * NG)

        @block.gpsimd
        def _(p):
            p.memset(mhalf[:, :], -0.5).then_inc(s["f_const"], 1)
            p.memset(ones[:, :], 1.0).then_inc(s["f_const"], 1)
            p.memset(zero[:, :], 0.0).then_inc(s["f_const"], 1)
            p.iota(lane[:, :], pattern=[[1, EXPERTS]], base=0, channel_multiplier=0,
                   allow_small_or_imprecise_dtypes=True).then_inc(s["f_const"], 1)
            p.iota(thr[:, :], pattern=[[BS, THRS]], base=0, channel_multiplier=0,
                   allow_small_or_imprecise_dtypes=True).then_inc(s["f_const"], 1)
            p.iota(bnum[:, :], pattern=[[1, BLOCKS]], base=0, channel_multiplier=0,
                   allow_small_or_imprecise_dtypes=True).then_inc(s["f_const"], 1)
            p.wait_ge(s["f_const"], 6)
            p.affine_select(out=lower[:, :], in_=ones[:, :], compare_op=ALU.is_ge, fill=0.0, base=-1,
                            pattern=[[1, P]], channel_multiplier=-1).then_inc(s["f_const"], 1)
            rstd_side(p, s, "f_ln", 0, ve, rstd, mhalf)
            p.wait_ge(s["f_posi"], 1)
            for t in range(NT):
                for k in range(2):
                    p.indirect_dma_start(out=xg_d, out_offset=bass.IndirectOffsetOnAxis(ap=posi[:, k, t:t + 1], axis=0),
                                         in_=NR[:, t, :], in_offset=None).then_inc(s["f_scattered"], 16)
            p.wait_ge(s["f_scattered"], 32 * NT)
            blocks = xg_d.rearrange("(b c p) d -> b p c d", p=128, c=2)
            outs = y_d.rearrange("(b c p) d -> b p c d", p=128, c=2)
            at = lambda a, b: a[b] if isinstance(b, int) else a[bass.ds(b, 1)].rearrange("a p c d -> (a p) c d")

            def fetch(b, h):
                p.wait_ge(s["f_xgt"], b + 1)
                p.dma_start(XG[:, h, :, :], at(blocks, b)).then_inc(s[f"f_xg{h}"], 16)

            def store(b, h):
                p.wait_ge(s["f_drained"], 2 * (FIRST + b) + 4)
                p.dma_start(at(outs, b), Y[:, h, :, :]).then_inc(s[f"f_y{h}"], 16)

            fetch(0, 0)
            fetch(1, 1)
            with p.Fori(0, BLOCKS // 2 - 1) as i:
                for h in range(2):
                    fetch(2 * i + 2 + h, h)
                    store(2 * i + h, h)
            store(BLOCKS - 2, 0)
            store(BLOCKS - 1, 1)
            for h in range(2):
                p.wait_ge(s[f"f_y{h}"], 16 * (BLOCKS // 2))
            for t in range(NT):
                for k, rows in enumerate((NR, Y1)):
                    p.indirect_dma_start(out=rows[:, t, :], out_offset=None, in_=y_d,
                                         in_offset=bass.IndirectOffsetOnAxis(ap=posi[:, k, t:t + 1], axis=0)).then_inc(s[f"f_mine{t // GT}"], 16)

        @block.tensor
        def _(pe):
            def logits(g):
                for t in range(g * GT, (g + 1) * GT):
                    for k in range(KC):
                        ins = pe.matmul(pT[0:P, 0, t * EXPERTS:(t + 1) * EXPERTS], HT[:, k, t * P:(t + 1) * P], wr[:, k, :],
                                        start=(k == 0), stop=(k == KC - 1))
                return ins

            pL = pH[:, 0:3, :].rearrange("p b (j q) -> p (b j) q", q=128)
            pe.wait_ge(s["f_small"], 16)
            for g in range(NG):
                pe.wait_ge(s["f_ln_out"], GT * (g + 1))
                if g:
                    pe.wait_ge(s["f_t_out"], g)
                for k in range(KC):
                    for j in range(GT):
                        ins = pe.transpose(pL[:, GT * k + j, 0:P], NR[:, GT * g + j, k * 128:(k + 1) * 128], ident[0:P, 0:P])
                ins.then_inc(s["f_t_full"], 1)
                if g:
                    logits(g - 1)
            pe.wait_ge(s["f_t_out"], NG)
            logits(NG - 1).then_inc(s["f_logits"], 1)

            def hidden(G, slot, n, x):
                for f in range(FC):
                    pe.wait_ge(s["f_gelu"], FC * G + f + 1)
                    for k in range(KC):
                        ins = pe.matmul(pH[:, f % 4, 0:n], w1[:, slot, k, f * 128:(f + 1) * 128], x(k),
                                        start=(k == 0), stop=(k == KC - 1))
                    ins.then_inc(s["f_hid"], 1)

            def hidden_unit(u, slot):
                at, n = u * UN, P * len(tiles_of(u))
                hidden(unit_step(u), slot, n, lambda k: HT[:, k, at:at + n])

            def hidden_block(b, h):
                pe.wait_ge(s["f_xgt"], b + 3)
                if h:
                    pe.wait_ge(s["f_w1"], 16 * b + 48)
                else:
                    pe.wait_ge(s["f_w0"], 16 * b + 32)
                hidden(FIRST + b, h, BS, lambda k: XGT[:, h, k, :])

            def rows(G, hid, tiles, m, second):
                pe.wait_ge(s["f_gelu"], FC * G + FC + 4)
                for j in range(tiles):
                    pe.wait_ge(s["f_drained"], 2 * G + j + 1)
                    for f in range(FC):
                        ins = pe.matmul(pO[0:m, j, 0:D], HID[:, hid, f, j * m:(j + 1) * m], second(f), start=(f == 0), stop=(f == FC - 1))
                    ins.then_inc(s["f_rows"], 1)

            def rows_unit(u):
                rows(unit_step(u), unit_step(u) % 2, len(tiles_of(u)), P, lambda f: w2[:, SHARED * FC + f, :])

            def rows_block(b, h):
                e8 = pe.value_load(table[0:1, 1, (slice(b, b + 1) if isinstance(b, int) else bass.ds(b, 1))],
                                   min_val=0, max_val=(EXPERTS - 1) * FC)
                rows(FIRST + b, h, 2, 128, lambda f: w2[:, bass.ds(e8 + f, 1), :].rearrange("p a d -> p (a d)"))

            def turn(b, h):
                pe.wait_ge(s["f_xgt"], b + 1)
                pe.wait_ge(s[f"f_xg{h}"], (8 * b + 16) if h == 0 else (8 * b + 8))
                for k in range(KC):
                    for r in range(2):
                        ins = pe.transpose(pT[:, h, (2 * k + r) * 128:(2 * k + r + 1) * 128],
                                           XG[:, h, r, k * 128:(k + 1) * 128], ident[:, :])
                ins.then_inc(s["f_turned"], 1)

            pe.wait_ge(s["f_w1"], 32)
            hidden_unit(0, 1)
            hidden_unit(1, 1)
            pe.wait_ge(s["f_mask"], 1)
            pe.wait_ge(s["f_const"], 7)
            picked_of = mask[:, :, :].rearrange("p t e -> p (t e)")
            for n, m in enumerate((lower, ones)):
                ins = pe.matmul(pT[0:P, 1, n * NT * EXPERTS:(n + 1) * NT * EXPERTS], m[:, :], picked_of, start=True, stop=True)
            ins.then_inc(s["f_counts"], 1)
            pe.wait_ge(s["f_w2s"], 16)
            rows_unit(0)
            for u in range(2, FIRST):
                hidden_unit(u, 1)
                rows_unit(u - 1)
            pe.wait_ge(s["f_table"], 1)
            turn(0, 0)
            rows_unit(FIRST - 1)
            pe.wait_ge(s["f_w2p"], 16 * EXPERTS)
            hidden_block(0, 0)
            turn(1, 1)
            with pe.Fori(0, BLOCKS // 2 - 1) as i:
                for h in range(2):
                    b = 2 * i + h
                    hidden_block(b + 1, 1 - h)
                    turn(b + 2, h)
                    rows_block(b, h)
            hidden_block(BLOCKS - 1, 1)
            rows_block(BLOCKS - 2, 0)
            pe.wait_ge(s["f_w0"], 16 * BLOCKS + 32)
            hidden_unit(FIRST, 0)
            rows_block(BLOCKS - 1, 1)
            for u in range(FIRST + 1, UNITS):
                hidden_unit(u, 0)
                rows_unit(u - 1)
            rows_unit(UNITS - 1)

        @block.scalar
        def _(a):
            a.wait_ge(s["f_lsub"], 1)
            a.activation(rw[:, :, :], rw[:, :, :], ACT.Exp).then_inc(s["f_rexp"], 1)

            def gelus(G, slot, hid, n):
                if not (isinstance(G, int) and G < 2):
                    a.wait_ge(s["f_rows"], 2 * G - 2)
                for f in range(FC):
                    a.wait_ge(s["f_hid"], FC * G + f + 1)
                    a.activation(HID[:, hid, f, 0:n], pH[:, f % 4, 0:n], ACT.Gelu, bias=b1[:, slot, f:f + 1]).then_inc(s["f_gelu"], 1)

            def unit(u):
                G = unit_step(u)
                gelus(G, 1 if u < FIRST else 0, G % 2, P * len(tiles_of(u)))

            steps(a, unit, lambda b, h: gelus(FIRST + b, h, h, BS))

        @block.vector
        def _(v):
            done = [0]

            def then(ins):
                done[0] += 1
                ins.then_inc(s["f_chain"], 1)
                v.wait_ge(s["f_chain"], done[0])

            v.sem_inc(s["f_gelu"], 4)
            v.sem_inc(s["f_drained"], 2)
            v.sem_inc(s["f_xgt"], 2)


            def whole(g):
                tiles = XS[:, g * GT:(g + 1) * GT, :]
                v.wait_ge(s[f"f_part{g}"], 16)
                v.tensor_tensor(tiles, tiles, NR[:, g * GT:(g + 1) * GT, :], ALU.add).then_inc(s["f_added"], 1)
                v.wait_ge(s["f_added"], g + 1)

            all_stats(v, s, "f_ln", lambda t: XS[:, t, :], st, mv, ve, whole)
            for g in range(NG + 1):
                if g < NG:
                    normalised(v, s, "f_ln", g, lambda t: XS[:, t, :], lambda t: NR[:, t, :], mv, rstd)
                g -= 1
                if g < 0:
                    continue
                v.wait_ge(s["f_t_full"], g + 1)
                for k in range(KC):
                    pL = pH[:, 0:3, :].rearrange("p b (j q) -> p (b j) q", q=128)
                    ins = v.tensor_copy(HT[:, k, g * GN:(g + 1) * GN].rearrange("p (j q) -> p j q", j=GT),
                                        pL[:, GT * k:GT * k + GT, 0:P])
                ins.then_inc(s["f_t_out"], 1)

            def spread(x):
                return x.unsqueeze(2).broadcast_to([P, NT, EXPERTS])

            v.wait_ge(s["f_logits"], 1)
            logits = pT[0:P, 0, 0:NT * EXPERTS].rearrange("p (t e) -> p t e", t=NT)
            then(v.tensor_reduce(rmax[:, :], logits, AX.X, ALU.max))
            v.tensor_tensor(rw[:, :, :], logits, spread(rmax[:, :]), ALU.subtract).then_inc(s["f_lsub"], 1)
            v.wait_ge(s["f_rexp"], 1)
            then(v.tensor_reduce(rsum[:, :], rw[:, :, :], AX.X, ALU.add))
            then(v.reciprocal(rrec[:, :], rsum[:, :]))
            then(v.tensor_tensor(rw[:, :, :], rw[:, :, :], spread(rrec[:, :]), ALU.mult))
            for t in range(NT):
                ins = v.max(top[:, t, :], rw[:, t, :])
            then(ins)
            for t in range(NT):
                ins = v.max_index(topi[:, t, :], top[:, t, :], rw[:, t, :])
            then(ins)
            v.tensor_tensor(rsum[:, :], top[:, :, 0], top[:, :, 1], ALU.add)
            then(v.tensor_copy(topf[:, :, :], topi[:, :, :]))
            v.wait_ge(s["f_const"], 7)
            lanes = lane[:, :].unsqueeze(1).broadcast_to([P, NT, EXPERTS])
            for n in range(2):
                ins = v.tensor_tensor(pick[:, n, :, :], lanes, spread(topf[:, :, n]), ALU.is_equal)
            then(ins)
            v.tensor_tensor(mask[:, :, :], pick[:, 0, :, :], pick[:, 1, :, :], ALU.add).then_inc(s["f_mask"], 1)
            then(v.reciprocal(rrec[:, :], rsum[:, :]))
            for n in range(2):
                v.tensor_tensor(gate[:, n, :], top[:, :, n], rrec[:, :], ALU.mult)

            v.wait_ge(s["f_counts"], 1)
            size = NT * EXPERTS
            counted = lambda n: pT[0:P, 1, n * size:(n + 1) * size].rearrange("p (t e) -> p t e", t=NT)
            then(v.tensor_copy(tot[:, :, :], counted(1)))
            for e in range(EXPERTS):
                ins = v.tensor_tensor_scan(upto[:, :, e], zero[0:P, 0:NT], tot[:, :, e], 0.0, ALU.add, ALU.add)
            then(ins)
            then(v.tensor_tensor(over[:, :, :], upto[:, NT - 1, :].unsqueeze(2).broadcast_to([P, EXPERTS, THRS]),
                                 thr[:, :].unsqueeze(1).broadcast_to([P, EXPERTS, THRS]), ALU.is_gt))
            then(v.tensor_reduce(nb[:, :], over[:, :, :], AX.X, ALU.add))
            then(v.tensor_tensor_scan(nbi[:, :], zero[0:P, 0:EXPERTS], nb[:, :], 0.0, ALU.add, ALU.add))
            then(v.tensor_tensor(base[:, :], nbi[:, :], nb[:, :], ALU.subtract))
            v.tensor_scalar(base[:, :], base[:, :], float(BS), None, ALU.mult)
            then(v.tensor_tensor(rank[:, :, :], upto[:, :, :], tot[:, :, :], ALU.subtract))
            then(v.tensor_tensor(rank[:, :, :], rank[:, :, :], counted(0), ALU.add))
            then(v.tensor_tensor(rank[:, :, :], rank[:, :, :], base[:, :].unsqueeze(1).broadcast_to([P, NT, EXPERTS]), ALU.add))
            for n in range(2):
                ins = v.tensor_tensor(pick[:, n, :, :], pick[:, n, :, :], rank[:, :, :], ALU.mult)
            then(ins)
            then(v.tensor_reduce(pos[:, :, :], pick[:, :, :, :], AX.X, ALU.add))
            v.tensor_copy(posi[:, :, :], pos[:, :, :]).then_inc(s["f_posi"], 1)
            then(v.tensor_tensor(before[:, :, :], nbi[:, :].unsqueeze(1).broadcast_to([P, BLOCKS, EXPERTS]),
                                 bnum[:, :].unsqueeze(2).broadcast_to([P, BLOCKS, EXPERTS]), ALU.is_le))
            then(v.tensor_reduce(eb[:, 0, :], before[:, :, :], AX.X, ALU.add))
            then(v.tensor_scalar(eb[:, 0, :], eb[:, 0, :], float(EXPERTS - 1), None, ALU.min))
            then(v.tensor_scalar(eb[:, 1, :], eb[:, 0, :], float(FC), None, ALU.mult))
            v.tensor_copy(table[:, :, :], eb[:, :, :]).then_inc(s["f_table"], 1)

            v.wait_ge(s["f_b2s"], 16)
            then(v.tensor_tensor(XS[:, :, :], XS[:, :, :], b2s[:, :].unsqueeze(1).broadcast_to([P, NT, D]), ALU.add))

            def xgt(b, h):
                v.wait_ge(s["f_turned"], b + 1)
                v.wait_ge(s["f_hid"], FC * (FIRST + b - 1))
                v.tensor_copy(XGT[:, h, :, :].rearrange("p k n -> p (k n)"), pT[:, h, :]).then_inc(s["f_xgt"], 1)

            def unit_rows(u):
                G = unit_step(u)
                for j, t in enumerate(tiles_of(u)):
                    v.wait_ge(s["f_rows"], 2 * G + j + 1)
                    v.tensor_tensor(XS[:, t, :], XS[:, t, :], pO[0:P, j, 0:D], ALU.add).then_inc(s["f_drained"], 1)

            def block_rows(b, h):
                if not isinstance(b, int) or b >= 2:
                    v.wait_ge(s[f"f_y{h}"], (8 * b) if h == 0 else (8 * b - 8))
                v.wait_ge(s[f"f_b2{h}"], (8 * b + 16) if h == 0 else (8 * b + 8))
                for j in range(2):
                    v.wait_ge(s["f_rows"], 2 * (FIRST + b) + j + 1)
                    v.tensor_tensor(Y[:, h, j, :], pO[:, j, 0:D], b2[:, h, :], ALU.add).then_inc(s["f_drained"], 1)

            for u in range(FIRST - 1):
                unit_rows(u)
            xgt(0, 0)
            unit_rows(FIRST - 1)
            xgt(1, 1)
            xgt(2, 0)
            block_rows(0, 0)
            xgt(3, 1)
            block_rows(1, 1)
            with v.Fori(1, BLOCKS // 2 - 1) as i:
                for h in range(2):
                    xgt(2 * i + h + 2, h)
                    block_rows(2 * i + h, h)
            block_rows(BLOCKS - 2, 0)
            block_rows(BLOCKS - 1, 1)

            def combine(g):
                v.wait_ge(s[f"f_mine{g}"], 32 * GT)
                for k, rows in enumerate((NR, Y1)):
                    for t in range(g * GT, (g + 1) * GT):
                        v.scalar_tensor_tensor(out=XS[:, t, :], in0=rows[:, t, :], scalar=gate[:, k, t:t + 1], in1=XS[:, t, :],
                                               op0=ALU.mult, op1=ALU.add).then_inc(s["f_done"], 1)
                    v.wait_ge(s["f_done"], GT * (2 * g + k + 1))

            after = {9: (0, 1), 10: (2,), 11: (3,), 12: (4,)}
            for u in range(FIRST, UNITS):
                unit_rows(u)
                if u in after:
                    v.wait_ge(s["f_drained"], 2 * unit_step(u) + len(tiles_of(u)) + 2)
                    for g in after[u]:
                        combine(g)


def gps_layer(nc, a, out):
    with ExitStack() as c:
        XS = c.enter_context(nc.sbuf_tensor("XS", [P, NT, D], F32))
        ident = c.enter_context(nc.sbuf_tensor("ident", [128, 128], F32))
        dram = lambda n, shape, dt=F32: nc.dram_tensor(n, shape, dt).ap()
        xn_d, xx_d = dram("xn_d", (N, D)), dram("xx_d", (N, D))
        sums_d = dram("sums_d", (NW * WN, D))
        scratch = {"key": dram("key_d", (ITEMS * TE + 2,)), "dl": dram("dl_d", (ITEMS, TE)),
                   "eat": dram("eat_d", (ITEMS, ED * TE)), "ea": dram("ea_d", (ITEMS, ED * TE)),
                   "xl": dram("xl_d", (NW * WN, D)), "al": dram("al_d", (ITEMS, GH, TE)),
                   "pc": dram("pc_d", (ITEMS, 2 * GH, TE)), "wl": dram("wl_d", (ITEMS,), I32)}
        xg_d, y_d = dram("xg_d", (BLOCKS * BS, D)), dram("y_d", (BLOCKS * BS, D))
        s = Names(nc)
        with nc.Block() as block:
            @block.gpsimd
            def _(p):
                p.memset(ident[:, :], 0.0).then_inc(s["const"], 1)
                p.wait_ge(s["const"], 1)
                p.affine_select(out=ident[:, :], in_=ident[:, :], compare_op=ALU.not_equal, fill=1.0, base=0,
                                pattern=[[-1, 128]], channel_multiplier=1).then_inc(s["const"], 1)
                p.wait_ge(s["const"], 2)
        part = lambda prefix: {n[len(prefix):]: v for n, v in a.items() if n.startswith(prefix)}
        s.give_back()
        for stage in (lambda s: graph_attention(nc, s, XS, ident, a["x"], xn_d, part("gnn_"), sums_d, scratch),
                      lambda s: mixer(nc, s, XS, ident, part("mix_"), xg_d, a["x"], xn_d, sums_d, xx_d),
                      lambda s: experts(nc, s, XS, ident, part("ffn_"), out, xg_d, y_d, xx_d)):
            s = Names(nc)
            stage(s)
            s.give_back()


def laid_out(inputs):
    a = {n: np.asarray(v) for n, v in inputs.items()}
    ea = a["edge_attr_16"].reshape(NTE, TE, ED)
    src, dst = (a[n].reshape(NTE, TE) for n in ("src", "dst"))
    d = {"x": a["x"], "gnn_src": src, "gnn_dst": dst, "gnn_dstT": dst.T, "gnn_ea": ea.reshape(NTE, -1),
         "gnn_eaT": ea.transpose(0, 2, 1).reshape(NTE, -1)}
    for n in ("W_l", "W_r", "W_e"):
        d[f"gnn_{n}T"] = a[f"L0_gnn_{n}"].T
    for n in ("b_l", "b_r", "att", "bias"):
        d[f"gnn_{n}"] = a[f"L0_gnn_{n}"]
    for n in ("Wq", "Wk", "Wv", "Wo", "bo", "W1", "W2", "b2"):
        d[f"mix_{n}"] = a[f"L0_mix_{n}"]
    for n in ("ln1_g", "ln1_b", "b1", "ln2_g", "ln2_b"):
        d[f"mix_{n}"] = columns(a[f"L0_mix_{n}"])
    for n in ("Wr", "W1s", "W2s", "b2s", "W1p", "W2p", "b2p"):
        d[f"ffn_{n}"] = a[f"L0_ffn_{n}"]
    for n in ("b1s", "b1p"):
        d[f"ffn_{n}"] = columns(a[f"L0_ffn_{n}"])
    return {n: np.ascontiguousarray(v) for n, v in d.items()}


def kernel(**inputs):
    import concourse.bacc as bacc
    from concourse.bass_utils import run_bass_kernel_spmd

    nc = bacc.Bacc("TRN2", target_bir_lowering=False, num_devices=1)
    arrays, args = {}, {}
    for name, v in laid_out(inputs).items():
        arrays[f"in_{name}"] = v
        args[name] = nc.dram_tensor(f"in_{name}", v.shape, mybir.dt.from_np(v.dtype), kind="ExternalInput").ap()
    out = nc.dram_tensor("out", (N, D), F32, kind="ExternalOutput").ap()
    gps_layer(nc, args, out)
    return run_bass_kernel_spmd(nc, [arrays], core_ids=[0]).results[0]["out"]
```
